# Optimizing a Trainium2 kernel written in Bass

```python
import numpy as np
import jax
import jax.numpy as jnp

def _softmax(x, axis=-1):
    return jax.nn.softmax(x, axis=axis)

def _gelu(x):
    return jax.nn.gelu(x, approximate=True)

def _silu(x):
    return jax.nn.silu(x)

def _sigmoid(x):
    return jax.nn.sigmoid(x)

def _layernorm(x, axis=-1, eps=1e-05):
    m = jnp.mean(x, axis=axis, keepdims=True)
    v = jnp.var(x, axis=axis, keepdims=True)
    return (x - m) / jnp.sqrt(v + eps)

def _scatter_add(tgt, idx, src, axis=0):
    return tgt.at[idx].add(src)

def _segment_sum(src, seg, n):
    return jax.ops.segment_sum(src, seg, n)
kernel_name = 'mk_flamingo_gated_d2_seqx_r4_8d144c'

def setup_inputs(seed: int=0):
    np.random.seed(seed)
    _w = jnp.asarray

    def _rec_inputs():
        import jax
        import jax.numpy as jnp
        _rk = jax.random.key(seed)
        x = 7.22e-05 + 1 * jax.random.normal(jax.random.fold_in(_rk, 1), (4, 512, 256), jnp.float32)
        _lenS = 512 - jax.random.randint(jax.random.fold_in(_rk, 7), (4,), 0, max(1, 512 // 4) + 1, jnp.int32)
        _lenS2 = 512 - jax.random.randint(jax.random.fold_in(_rk, 8), (4,), 0, max(1, 512 // 4) + 1, jnp.int32)
        _ctx_1024P = jax.random.normal(jax.random.fold_in(_rk, 11), (4, 16, 256), jnp.float32)
        _ctx_1024c = jax.random.dirichlet(jax.random.fold_in(_rk, 511), 0.3 * jnp.ones((16,), jnp.float32), (4, 512))
        _ctx_1024t = jnp.einsum('bsk,bkd->bsd', _ctx_1024c, _ctx_1024P)
        _ctx_1024t = _ctx_1024t * jax.lax.rsqrt(jnp.mean(jnp.square(_ctx_1024t)) + 1e-12) * 0.953939
        ctx_1024 = 4.13588e-05 + 0.999923 * (_ctx_1024t + 0.3 * jax.random.normal(jax.random.fold_in(_rk, 611), (4, 512, 256), jnp.float32))
        _g = jax.random.normal(jax.random.fold_in(_rk, 9001), (2, 2), jnp.float32)
        _g = jnp.sign(_g) * jnp.maximum(jnp.abs(_g), 1.0) + (_g == 0) * 1.0
        g_xattn = _g[0]
        g_ffn = _g[1]
        return (x, ctx_1024, g_xattn, g_ffn)
    x, ctx_1024, g_xattn, g_ffn = _rec_inputs()

    def _L0_xattn_setup():
        import jax, jax.numpy as jnp
        import numpy as np
        THETA = 10000.0
        SCALE_BASE = 512.0
        GAMMA = 0.96875

        def _dup_interleave(x):
            return jnp.repeat(x, 2, axis=-1)

        def _xpos(x, offset, inverse_scale):
            L, d = (x.shape[-2], x.shape[-1])
            half = d // 2
            base = (jnp.arange(0, d, 2, dtype=x.dtype) + 0.4 * d) / (1.4 * d)
            pos = jnp.arange(offset, offset + L, dtype=x.dtype)
            scale = base[None, :] ** (pos[:, None] / SCALE_BASE)
            freqs = 1.0 / THETA ** (jnp.arange(half, dtype=x.dtype) / half)
            sin_in = pos[:, None] * freqs[None, :]
            if inverse_scale:
                scale = 1.0 / scale
            sin = _dup_interleave(jnp.sin(sin_in) * scale)
            cos = _dup_interleave(jnp.cos(sin_in) * scale)
            rot = jnp.stack((-x[..., 1::2], x[..., ::2]), axis=-1).reshape(x.shape)
            return x * cos + rot * sin

        def _decay_mask(L, gamma, dtype):
            u = jnp.arange(L, dtype=dtype)[:, None]
            v = jnp.arange(L, dtype=dtype)[None, :]
            return jnp.where(u >= v, gamma ** (u - v), jnp.zeros((), dtype))
        key = jax.random.key(seed)
        ks = jax.random.split(key, 6)
        B, L, E = (2, 1024, 256)
        query = jax.random.normal(ks[0], (B, L, E), jnp.float32)
        k_in = jax.random.normal(ks[1], (B, L, E), jnp.float32)
        value = jax.random.normal(ks[2], (B, L, E), jnp.float32)
        s = 1.0 / np.sqrt(E)
        Wq = jax.random.normal(ks[3], (E, E), jnp.float32) * s
        Wk = jax.random.normal(ks[4], (E, E), jnp.float32) * s
        Wv = jax.random.normal(ks[5], (E, E), jnp.float32) * s
        return {'query': query, 'key': k_in, 'value': value, 'Wq': Wq, 'Wk': Wk, 'Wv': Wv}
    _L0_xattn_all = _L0_xattn_setup()
    _L0_xattn_in = {k: v for k, v in _L0_xattn_all.items() if k in ('Wq', 'Wk', 'Wv')}
    del _L0_xattn_all

    def _L0_ffn_setup():
        import jax, jax.numpy as jnp
        import numpy as np
        B, S, DIM, FFN, E = (4, 512, 256, 1024, 8)
        key = jax.random.key(seed)
        k0, k1, k2, k3 = jax.random.split(key, 4)
        scale = 0.02
        return {'hidden_states': jax.random.normal(k0, (B, S, DIM), jnp.float32), 'router_w': jax.random.normal(k1, (DIM, E), jnp.float32) * scale, 'router_b': jnp.zeros((E,), jnp.float32), 'w1': jax.random.normal(k2, (E, DIM, 2 * FFN), jnp.float32) * scale, 'w2': jax.random.normal(k3, (E, FFN, DIM), jnp.float32) * scale}
    _L0_ffn_all = _L0_ffn_setup()
    _L0_ffn_in = {k: v for k, v in _L0_ffn_all.items() if k in ('router_w', 'router_b', 'w1', 'w2')}
    del _L0_ffn_all

    def _L1_xattn_setup():
        import jax, jax.numpy as jnp
        import numpy as np
        EPS = 1e-05

        def layer_norm(x, w, b):
            mu = jnp.mean(x, axis=-1, keepdims=True)
            var = jnp.mean((x - mu) ** 2, axis=-1, keepdims=True)
            return (x - mu) * jax.lax.rsqrt(var + EPS) * w + b
        key = jax.random.key(seed)
        ks = jax.random.split(key, 8)
        b, Nx, Nz, D = (16, 1024, 64, 256)
        H, Dh = (8, 64)
        inner = H * Dh
        s = 1.0 / np.sqrt(D)
        return {'x': jax.random.normal(ks[0], (b, Nx, D), jnp.float32), 'latents': jax.random.normal(ks[1], (b, Nz, D), jnp.float32), 'ln_media_w': jnp.ones((D,), jnp.float32), 'ln_media_b': jnp.zeros((D,), jnp.float32), 'ln_lat_w': jnp.ones((D,), jnp.float32), 'ln_lat_b': jnp.zeros((D,), jnp.float32), 'Wq': jax.random.normal(ks[2], (D, inner), jnp.float32) * s, 'Wk': jax.random.normal(ks[3], (D, inner), jnp.float32) * s, 'Wv': jax.random.normal(ks[4], (D, inner), jnp.float32) * s, 'Wout': jax.random.normal(ks[5], (inner, D), jnp.float32) * (1.0 / np.sqrt(inner))}
    _L1_xattn_all = _L1_xattn_setup()
    _L1_xattn_in = {k: v for k, v in _L1_xattn_all.items() if k in ('ln_media_w', 'ln_media_b', 'ln_lat_w', 'ln_lat_b', 'Wq', 'Wk', 'Wv', 'Wout')}
    del _L1_xattn_all

    def _L1_ffn_setup():
        import jax, jax.numpy as jnp
        import numpy as np
        EMB_DIM = 256
        HIDDEN = int(2 / 3 * 4 * EMB_DIM)
        NUM_EXPERTS = 8
        TOP_K = 2
        B, S = (4, 256)
        key = jax.random.key(seed)
        ks = jax.random.split(key, 5)
        sc = 1.0 / np.sqrt(EMB_DIM)
        sh = 1.0 / np.sqrt(HIDDEN)
        return {'x': jax.random.normal(ks[0], (B, S, EMB_DIM), dtype=jnp.float32), 'Wg': jax.random.normal(ks[1], (NUM_EXPERTS, EMB_DIM), dtype=jnp.float32) * sc, 'W1': jax.random.normal(ks[2], (NUM_EXPERTS, HIDDEN, EMB_DIM), dtype=jnp.float32) * sc, 'W2': jax.random.normal(ks[3], (NUM_EXPERTS, HIDDEN, EMB_DIM), dtype=jnp.float32) * sc, 'W3': jax.random.normal(ks[4], (NUM_EXPERTS, EMB_DIM, HIDDEN), dtype=jnp.float32) * sh}
    _L1_ffn_all = _L1_ffn_setup()
    _L1_ffn_in = {k: v for k, v in _L1_ffn_all.items() if k in ('Wg', 'W1', 'W2', 'W3')}
    del _L1_ffn_all
    return {'x': x, 'ctx_1024': ctx_1024, 'g_xattn': g_xattn, 'g_ffn': g_ffn, 'L0_xattn_Wq': _L0_xattn_in['Wq'], 'L0_xattn_Wk': _L0_xattn_in['Wk'], 'L0_xattn_Wv': _L0_xattn_in['Wv'], 'L0_ffn_router_w': _L0_ffn_in['router_w'], 'L0_ffn_router_b': _L0_ffn_in['router_b'], 'L0_ffn_w1': _L0_ffn_in['w1'], 'L0_ffn_w2': _L0_ffn_in['w2'], 'L1_xattn_ln_media_w': _L1_xattn_in['ln_media_w'], 'L1_xattn_ln_media_b': _L1_xattn_in['ln_media_b'], 'L1_xattn_ln_lat_w': _L1_xattn_in['ln_lat_w'], 'L1_xattn_ln_lat_b': _L1_xattn_in['ln_lat_b'], 'L1_xattn_Wq': _L1_xattn_in['Wq'], 'L1_xattn_Wk': _L1_xattn_in['Wk'], 'L1_xattn_Wv': _L1_xattn_in['Wv'], 'L1_xattn_Wout': _L1_xattn_in['Wout'], 'L1_ffn_Wg': _L1_ffn_in['Wg'], 'L1_ffn_W1': _L1_ffn_in['W1'], 'L1_ffn_W2': _L1_ffn_in['W2'], 'L1_ffn_W3': _L1_ffn_in['W3']}

def reference(x, ctx_1024, g_xattn, g_ffn, L0_xattn_Wq, L0_xattn_Wk, L0_xattn_Wv, L0_ffn_router_w, L0_ffn_router_b, L0_ffn_w1, L0_ffn_w2, L1_xattn_ln_media_w, L1_xattn_ln_media_b, L1_xattn_ln_lat_w, L1_xattn_ln_lat_b, L1_xattn_Wq, L1_xattn_Wk, L1_xattn_Wv, L1_xattn_Wout, L1_ffn_Wg, L1_ffn_W1, L1_ffn_W2, L1_ffn_W3):
    import jax
    import jax.numpy as jnp

    def _L0_xattn_ref(query, key, value, Wq, Wk, Wv):
        import jax, jax.numpy as jnp
        import numpy as np
        THETA = 10000.0
        SCALE_BASE = 512.0
        GAMMA = 0.96875

        def _dup_interleave(x):
            return jnp.repeat(x, 2, axis=-1)

        def _xpos(x, offset, inverse_scale):
            L, d = (x.shape[-2], x.shape[-1])
            half = d // 2
            base = (jnp.arange(0, d, 2, dtype=x.dtype) + 0.4 * d) / (1.4 * d)
            pos = jnp.arange(offset, offset + L, dtype=x.dtype)
            scale = base[None, :] ** (pos[:, None] / SCALE_BASE)
            freqs = 1.0 / THETA ** (jnp.arange(half, dtype=x.dtype) / half)
            sin_in = pos[:, None] * freqs[None, :]
            if inverse_scale:
                scale = 1.0 / scale
            sin = _dup_interleave(jnp.sin(sin_in) * scale)
            cos = _dup_interleave(jnp.cos(sin_in) * scale)
            rot = jnp.stack((-x[..., 1::2], x[..., ::2]), axis=-1).reshape(x.shape)
            return x * cos + rot * sin

        def _decay_mask(L, gamma, dtype):
            u = jnp.arange(L, dtype=dtype)[:, None]
            v = jnp.arange(L, dtype=dtype)[None, :]
            return jnp.where(u >= v, gamma ** (u - v), jnp.zeros((), dtype))
        q = jnp.einsum('ble,de->bld', query, Wq)
        k = jnp.einsum('ble,de->bld', key, Wk)
        v = jnp.einsum('ble,de->bld', value, Wv)
        q = _xpos(q, 0, False)
        k = _xpos(k, 0, True)
        L = q.shape[-2]
        mask = _decay_mask(L, jnp.asarray(GAMMA, q.dtype), q.dtype)
        retention = jnp.einsum('bqd,bkd->bqk', q, k) * mask[None, :, :]
        out = jnp.einsum('bqk,bkv->bqv', retention, v)
        return out

    def _L0_ffn_ref(hidden_states, router_w, router_b, w1, w2):
        import jax, jax.numpy as jnp
        import numpy as np
        B, S, DIM, FFN, E = (4, 512, 256, 1024, 8)
        b, s, d = hidden_states.shape
        x = hidden_states.reshape(-1, d)
        logits = x @ router_w + router_b
        route = jax.nn.softmax(logits, axis=1)
        max_prob = jnp.max(route, axis=1, keepdims=True)
        max_ind = jnp.argmax(route, axis=1)
        out = jnp.zeros_like(x)
        num_experts = w1.shape[0]
        for e in range(num_experts):
            h = x @ w1[e]
            a, g = jnp.split(h, 2, axis=1)
            y = jax.nn.silu(a) * g @ w2[e]
            out = jnp.where((max_ind == e)[:, None], y, out)
        out = out * max_prob
        return out.reshape(b, s, d)

    def _L1_xattn_ref(x, latents, ln_media_w, ln_media_b, ln_lat_w, ln_lat_b, Wq, Wk, Wv, Wout):
        import jax, jax.numpy as jnp
        import numpy as np
        EPS = 1e-05

        def layer_norm(x, w, b):
            mu = jnp.mean(x, axis=-1, keepdims=True)
            var = jnp.mean((x - mu) ** 2, axis=-1, keepdims=True)
            return (x - mu) * jax.lax.rsqrt(var + EPS) * w + b
        H, Dh = (8, 64)
        scale = Dh ** (-0.5)
        b, Nz, D = latents.shape
        xn = layer_norm(x, ln_media_w, ln_media_b)
        zn = layer_norm(latents, ln_lat_w, ln_lat_b)
        q = (zn @ Wq).reshape(b, Nz, H, Dh).transpose(0, 2, 1, 3)
        kv_in = jnp.concatenate([xn, zn], axis=1)
        F = kv_in.shape[1]
        k = (kv_in @ Wk).reshape(b, F, H, Dh).transpose(0, 2, 1, 3)
        v = (kv_in @ Wv).reshape(b, F, H, Dh).transpose(0, 2, 1, 3)
        sim = jnp.einsum('bhqd,bhfd->bhqf', q * scale, k)
        alphas = jax.nn.softmax(sim, axis=-1)
        out = jnp.einsum('bhqf,bhfd->bhqd', alphas, v)
        out = out.transpose(0, 2, 1, 3).reshape(b, Nz, H * Dh)
        return out @ Wout

    def _L1_ffn_ref(x, Wg, W1, W2, W3):
        import jax, jax.numpy as jnp
        import numpy as np
        EMB_DIM = 256
        HIDDEN = int(2 / 3 * 4 * EMB_DIM)
        NUM_EXPERTS = 8
        TOP_K = 2
        B, S = (4, 256)
        gate_logits = jnp.einsum('bsd,ed->bse', x, Wg)
        top_v, top_i = jax.lax.top_k(gate_logits, TOP_K)
        mask = jnp.any(top_i[..., :, None] == jnp.arange(NUM_EXPERTS), axis=-2)
        sparse_logits = jnp.where(mask, gate_logits, -jnp.inf)
        gating = jax.nn.softmax(sparse_logits, axis=-1)
        h1 = jnp.einsum('bsd,ehd->bseh', x, W1)
        h2 = jnp.einsum('bsd,ehd->bseh', x, W2)
        hidden = jax.nn.silu(h1) * h2
        expert_out = jnp.einsum('bseh,edh->bsed', hidden, W3)
        return jnp.einsum('bsed,bse->bsd', expert_out, gating)
    x = x + jnp.tanh(g_xattn[0]) * _L0_xattn_ref(_layernorm(x, axis=-1), ctx_1024, ctx_1024, L0_xattn_Wq, L0_xattn_Wk, L0_xattn_Wv)
    x = x + jnp.tanh(g_ffn[0]) * _L0_ffn_ref(_layernorm(x, axis=-1), L0_ffn_router_w, L0_ffn_router_b, L0_ffn_w1, L0_ffn_w2)
    x = x + jnp.tanh(g_xattn[1]) * _L1_xattn_ref(ctx_1024, _layernorm(x, axis=-1), L1_xattn_ln_media_w, L1_xattn_ln_media_b, L1_xattn_ln_lat_w, L1_xattn_ln_lat_b, L1_xattn_Wq, L1_xattn_Wk, L1_xattn_Wv, L1_xattn_Wout)
    x = x + jnp.tanh(g_ffn[1]) * _L1_ffn_ref(_layernorm(x, axis=-1), L1_ffn_Wg, L1_ffn_W1, L1_ffn_W2, L1_ffn_W3)
    return x

_drawn_inputs = setup_inputs


def setup_inputs(seed=0):
    import zlib

    import numpy as np

    out = dict(_drawn_inputs(seed))
    spreads = {'g_ffn': (-1.0, 0.6),
     'L0_ffn_router_b': (0.0, 0.8),
     'L1_xattn_ln_media_w': (1.0, 0.6),
     'L1_xattn_ln_media_b': (0.0, 0.8),
     'L1_xattn_ln_lat_w': (1.0, 0.6),
     'L1_xattn_ln_lat_b': (0.0, 0.8)}
    factors = {'L0_ffn_router_w': 8.0,
     'L0_ffn_w1': 8.0,
     'L0_ffn_w2': 8.0,
     'L1_xattn_Wq': 8.0,
     'L1_xattn_Wk': 8.0,
     'L1_xattn_Wv': 8.0,
     'L1_xattn_Wout': 8.0,
     'L1_ffn_Wg': 8.0,
     'L1_ffn_W1': 8.0,
     'L1_ffn_W2': 8.0,
     'L1_ffn_W3': 8.0}
    for name, (base, spread) in spreads.items():
        noise = np.random.default_rng([zlib.crc32(name.encode()), seed]).standard_normal(out[name].shape)
        drawn = base * np.exp(spread * noise) if base else spread * noise
        out[name] = jnp.asarray(drawn.astype(out[name].dtype))
    for name, factor in factors.items():
        out[name] = (out[name] * factor).astype(out[name].dtype)
    return out
```

```python
from contextlib import ExitStack

import numpy as np

import concourse.bass as bass
from concourse import mybir

F32 = mybir.dt.float32
F32R = mybir.dt.float32r
I32 = mybir.dt.int32
ALU = mybir.AluOpType
ACT = mybir.ActivationFunctionType
AX = mybir.AxisListType.X

P = 128
B, S, D = 4, 512, 256
KC = D // P
T = B * S // P
TB = S // P
E = 8
F0, F1 = 1024, 682
H, DH = 8, 64
INNER = H * DH
KEYS = 2 * S
KT = KEYS // P
EPS = 1e-5
BIG = 3.0e38
SLOTS0 = T + E - 1
SLOTS1 = 2 * T + E - 1


def chunks(width):
    return [(c, min(P, width - c)) for c in range(0, width, P)]


C_IDENT, C_TRI, C_CAUSAL, C_ONES, C_REV, C_SLOT = 0, P, 2 * P, 3 * P, 4 * P, 4 * P + T * E
C_END = C_SLOT + 64


def shape_constants():
    k, m = np.arange(P)[:, None], np.arange(P)[None, :]
    c = np.zeros((P, C_END), np.float32)
    c[:, C_IDENT:C_IDENT + P] = k == m
    c[:, C_TRI:C_TRI + P] = k < m
    c[:, C_CAUSAL:C_CAUSAL + P] = m >= k
    c[:, C_ONES:C_ONES + P] = 1.0
    c[:, C_REV:C_REV + T * E] = np.tile(E - np.arange(E), T)[None]
    c[:, C_SLOT:C_END] = np.arange(64)[None]
    return c


def xpos_tables():
    f = np.float32
    base = (np.arange(0, D, 2, dtype=f) + f(0.4 * D)) / f(1.4 * D)
    pos = np.arange(S, dtype=f)
    freqs = f(1.0) / f(10000.0) ** (np.arange(D // 2, dtype=f) / f(D // 2))
    angle = (pos[:, None] * freqs[None, :]).astype(np.float64)
    scale = base[None, :].astype(np.float64) ** (pos[:, None] / 512.0)
    gamma = 0.96875 ** pos.astype(np.float64)[:, None]
    cos, sin = np.cos(angle), np.sin(angle)
    t = [cos * scale * gamma, sin * scale * gamma, cos / scale / gamma, sin / scale / gamma]
    return np.ascontiguousarray(np.stack([a.T for a in t], 1).astype(f))


class Chain:

    def __init__(self, eng, sem):
        self.eng, self.sem, self.n = eng, sem, 0

    def __call__(self, ins):
        ins.then_inc(self.sem, 1)
        self.n += 1
        self.eng.wait_ge(self.sem, self.n)


class Program:
    def __init__(self, nc, ins, out, ctx):
        self.nc, self.ins, self.out = nc, ins, out
        self.n_sems = 0
        sb = lambda name, shape, dt=F32: ctx.enter_context(nc.sbuf_tensor(name, shape, dt))
        self.X = sb("X", [P, T, D])
        self.XN = sb("XN", [P, T, D])
        self.const = sb("const", [P, C_END])
        self.gates = sb("gates", [P, 4])
        self.tg = sb("tg", [P, 4])
        self.lnw = sb("lnw", [P, 4, KC])
        self.gate_w = sb("gate_w", [P, 2, T])
        self.dest = sb("dest", [P, 2, T], I32)
        self.slot_expert = sb("slot_expert", [P, 64], I32)
        self.stats = sb("stats", [P, T, 6])
        self.ln_tmp = sb("ln_tmp", [P, 4, T])
        self.mean = sb("mean", [P, T])
        self.rstd = sb("rstd", [P, T])
        self.std = sb("std", [P, T])
        self.zeros = sb("zeros", [P, 2048])
        self.ps = ctx.enter_context(nc.psum_tensor("ps", [P, 8, 512], F32))
        self.ident = self.const[:, C_IDENT:C_IDENT + P]
        dram = lambda name, shape: nc.dram_tensor(name, shape, F32, kind="Internal").ap()
        self.rows = [dram("rows0", ((SLOTS0 + 1) * P, D)), dram("rows1", ((SLOTS1 + 1) * P, D))]
        self.made = [dram("made0", (SLOTS0 * P, D)), dram("made1", (SLOTS1 * P, D))]
        self.kv_dram = dram("kv_t", (B, P, KC, KEYS))
        self.ctx = ctx
        self.s_zero = self.sem("s_zero")
        self.s_zeroed = [self.sem("s_zeroed0"), self.sem("s_zeroed1")]

    def sem(self, name):
        self.n_sems += 1
        return self.ctx.enter_context(self.nc.semaphore(name))

    def bank(self, i, n=1):
        return self.ps[:, i, :] if n == 1 else self.ps[:, i:i + n, :].rearrange("p b c -> p (b c)")

    def ln_stats(self, e, src, s_stat, link, s_var, s_std, std_n=1):
        with e.Fori(0, T) as t:
            e.bn_stats(self.stats[:, bass.ds(t, 1), :].rearrange("p a c -> p (a c)"),
                       src[:, bass.ds(t, 1), :].rearrange("p a c -> p (a c)")).then_inc(s_stat, 1)
        e.wait_ge(s_stat, T * std_n)
        m_even, m_odd = self.stats[:, :, 1], self.stats[:, :, 4]
        v_even, v_odd = self.stats[:, :, 2], self.stats[:, :, 5]
        total, diff, diff2, var = (self.ln_tmp[:, i, :] for i in range(4))
        link(e.tensor_tensor(total, m_even, m_odd, ALU.add))
        link(e.tensor_tensor(diff, m_even, m_odd, ALU.subtract))
        link(e.scalar_tensor_tensor(diff2, diff, 0.25, diff, ALU.mult, ALU.mult))
        link(e.tensor_tensor(var, v_even, v_odd, ALU.add))
        link(e.tensor_scalar(self.mean[:], total, 0.5, None, ALU.mult))
        link(e.scalar_tensor_tensor(total, var, 1.0 / D, diff2, ALU.mult, ALU.add))
        link(e.tensor_scalar(var, total, EPS, None, ALU.add))
        e.sem_inc(s_var, 1)
        e.wait_ge(s_std, std_n)
        link(e.reciprocal(self.rstd[:], self.std[:]))

    def ln_sqrt(self, act, s_var, s_std, n=1):
        act.wait_ge(s_var, n)
        act.activation(self.std[:], self.ln_tmp[:, 3, :], ACT.Sqrt).then_inc(s_std, 1)

    def normalise(self, e, out, src, t):
        return e.tensor_scalar(out, src, self.mean[:, t:t + 1], self.rstd[:, t:t + 1],
                               ALU.subtract, ALU.mult)

    def retention(self):
        nc, ins, X, ps = self.nc, self.ins, self.X, self.ps
        with ExitStack() as ctx:
            sb = lambda name, shape: ctx.enter_context(nc.sbuf_tensor(name, shape, F32))
            XT = sb("r_XT", [P, KC, T * P])
            CT = sb("r_CT", [P, KC, T * P])
            tab = sb("r_tab", [P, 4, S])
            Wq = sb("r_Wq", [P, KC, D])
            Wk = sb("r_Wk", [P, KC, D])
            Wv = sb("r_Wv", [P, KC, D])
            tmp = sb("r_tmp", [P, 4, S])
            qR = sb("r_qR", [P, 2, S])
            kR = sb("r_kR", [P, 2, S])
            V = sb("r_V", [P, TB, D])
            ST = sb("r_ST", [P, TB, S])
            s_x, s_c, s_ct, s_w, s_g = (self.sem("r_" + n) for n in ("x", "c", "ct", "w", "g"))
            s_stat, s_chain, s_var, s_std = (self.sem("r_" + n) for n in ("stat", "chain", "var", "std"))
            s_norm, s_turned, s_xt = (self.sem("r_" + n) for n in ("norm", "turned", "xt"))

            with nc.Block() as block:
                @block.sync
                def _(sp):
                    sp.dma_start(X[:], ins["x"].rearrange("(t p) d -> p t d", p=P)).then_inc(s_x, 16)
                    sp.dma_start(self.const[:], ins["const"]).then_inc(s_c, 16)
                    for w, name in ((Wq, "Wq0"), (Wk, "Wk0"), (Wv, "Wv0")):
                        sp.dma_start(w[:], ins[name].rearrange("(k p) n -> p k n", p=P)).then_inc(s_w, 16)
                    sp.dma_start(tab[:], ins["tab"]).then_inc(s_w, 16)
                    sp.dma_start(CT[:], ins["ctxT"].rearrange("(k p) n -> p k n", p=P)).then_inc(s_ct, 16)
                    sp.wait_ge(self.s_zero, 1)
                    for rows, sem, n in ((self.rows[0], self.s_zeroed[0], SLOTS0 + 1),
                                         (self.rows[1], self.s_zeroed[1], SLOTS1 + 1)):
                        flat = rows.rearrange("(t p) d -> p t d", p=P)
                        z = self.zeros[:].rearrange("p (t d) -> p t d", d=D)
                        for a in range(0, n, 8):
                            sp.dma_start(flat[:, a:a + 8, :], z).then_inc(sem, 16)

                @block.scalar
                def _(act):
                    for i, name in enumerate(("g_xattn", "g_ffn")):
                        act.dma_start(self.gates[:, 2 * i:2 * i + 2],
                                      ins[name].rearrange("(a n) -> a n", a=1).broadcast_to([P, 2])).then_inc(s_g, 16)
                    act.dma_start(self.lnw[:], ins["lnw"]).then_inc(s_g, 16)
                    act.wait_ge(s_g, 48)
                    act.activation(self.tg[:], self.gates[:], ACT.Tanh)
                    self.ln_sqrt(act, s_var, s_std)
                    for t in range(T):
                        act.wait_ge(s_turned, t + 1)
                        act.copy(XT[:, :, t * P:(t + 1) * P],
                                 self.ps[:, t % 4, 0:D].rearrange("p (k c) -> p k c", k=KC)).then_inc(s_xt, 1)

                @block.vector
                def _(e):
                    link = Chain(e, s_chain)
                    e.memset(self.zeros[:], 0.0).then_inc(self.s_zero, 1)
                    e.wait_ge(s_x, 16)
                    self.ln_stats(e, X, s_stat, link, s_var, s_std)
                    for t in range(T):
                        self.normalise(e, self.XN[:, t, :], X[:, t, :], t).then_inc(s_norm, 1)

                @block.tensor
                def _(pe):
                    pe.wait_ge(s_c, 16)
                    for t in range(T):
                        pe.wait_ge(s_norm, t + 1)
                        if t >= 4:
                            pe.wait_ge(s_xt, t - 3)
                        for k in range(KC):
                            mm = pe.transpose(ps[:, t % 4, k * P:(k + 1) * P],
                                              self.XN[:, t, k * P:(k + 1) * P], self.ident)
                        mm.then_inc(s_turned, 1)

            names = ("q_ps", "k_ps", "v_ps", "rot", "v_sb", "s_ps", "diag", "rest", "o_ps", "x_new", "ch")
            q_ps, k_ps, v_ps, rot, v_sb, s_ps, diag, rest, o_ps, x_new, s_ch = (self.sem("r2_" + n) for n in names)
            with nc.Block() as block:
                @block.tensor
                def _(pe):
                    pe.wait_ge(s_w, 64)
                    pe.wait_ge(s_ct, 16)
                    for b in range(B):
                        if b:
                            pe.wait_ge(diag, TB * b)
                            pe.wait_ge(rest, (TB - 1) * b)
                        for w, src, bank, sem in ((Wq, XT, 0, q_ps), (Wk, CT, 2, k_ps)):
                            for half in range(2):
                                for k in range(KC):
                                    mm = pe.matmul(ps[:, bank + half, :], w[:, k, half * P:(half + 1) * P],
                                                   src[:, k, b * S:(b + 1) * S], start=k == 0, stop=k == KC - 1)
                            mm.then_inc(sem, 1)
                        for j in range(TB):
                            if b and j % 2 == 0:
                                pe.wait_ge(v_sb, 2 * (b - 1) + j // 2 + 1)
                            for k in range(KC):
                                mm = pe.matmul(ps[:, 4 + j // 2, (j % 2) * D:(j % 2 + 1) * D],
                                               CT[:, k, (b * TB + j) * P:(b * TB + j + 1) * P],
                                               Wv[:, k, :], start=k == 0, stop=k == KC - 1)
                            if j % 2:
                                mm.then_inc(v_ps, 1)
                        pe.wait_ge(rot, 2 * (b + 1))
                        for j in range(TB):
                            for half in range(2):
                                mm = pe.matmul(ps[:, j, 0:S - j * P], kR[:, half, j * P:(j + 1) * P],
                                               qR[:, half, j * P:S], start=half == 0, stop=half == 1)
                            mm.then_inc(s_ps, 1)
                        pe.wait_ge(v_sb, 2 * (b + 1))
                        for i in range(TB):
                            pe.wait_ge(diag, TB * b + i + 1)
                            if i:
                                pe.wait_ge(rest, (TB - 1) * b + i)
                            if TB * b + i >= 2:
                                pe.wait_ge(x_new, TB * b + i - 1)
                            for j in range(i + 1):
                                mm = pe.matmul(ps[:, 6 + i % 2, 0:D], ST[:, j, (i - j) * P:(i - j + 1) * P],
                                               V[:, j, :], start=j == 0, stop=j == i)
                            mm.then_inc(o_ps, 1)

                @block.scalar
                def _(act):
                    for b in range(B):
                        if b:
                            act.wait_ge(o_ps, TB * b)
                        for h in range(2):
                            act.wait_ge(v_ps, 2 * b + h + 1)
                            act.copy(V[:, 2 * h:2 * h + 2, :],
                                     ps[:, 4 + h, :].rearrange("p (j d) -> p j d", j=2)).then_inc(v_sb, 1)
                        for j in range(TB - 1):
                            act.wait_ge(s_ps, TB * b + j + 1)
                            act.copy(ST[:, j, P:S - j * P], ps[:, j, P:S - j * P]).then_inc(rest, 1)

                @block.vector
                def _(e):
                    link = Chain(e, s_ch)
                    for b in range(B):
                        for n, (sem, bank, dst) in enumerate(((q_ps, 0, qR), (k_ps, 2, kR))):
                            even, odd = ps[:, bank, :], ps[:, bank + 1, :]
                            cos, sin = tab[:, 2 * n, :], tab[:, 2 * n + 1, :]
                            e.wait_ge(sem, b + 1)
                            if b and n == 0:
                                e.wait_ge(s_ps, TB * b)
                            e.tensor_tensor(tmp[:, 0, :], even, cos, ALU.mult)
                            e.tensor_tensor(tmp[:, 1, :], odd, sin, ALU.mult)
                            e.tensor_tensor(tmp[:, 2, :], odd, cos, ALU.mult)
                            link(e.tensor_tensor(tmp[:, 3, :], even, sin, ALU.mult))
                            link(e.tensor_tensor(dst[:, 0, :], tmp[:, 0, :], tmp[:, 1, :], ALU.subtract))
                            link(e.tensor_tensor(dst[:, 1, :], tmp[:, 2, :], tmp[:, 3, :], ALU.add))
                            e.sem_inc(rot, 1)
                        for j in range(TB):
                            e.wait_ge(s_ps, TB * b + j + 1)
                            if j < TB - 1:
                                e.wait_ge(rest, (TB - 1) * b + j + 1)
                            if b:
                                e.wait_ge(o_ps, TB * b)
                            e.tensor_tensor(ST[:, j, 0:P], ps[:, j, 0:P],
                                            self.const[:, C_CAUSAL:C_CAUSAL + P], ALU.mult).then_inc(diag, 1)
                        for i in range(TB):
                            t = TB * b + i
                            e.wait_ge(o_ps, t + 1)
                            e.scalar_tensor_tensor(X[:, t, :], ps[:, 6 + i % 2, 0:D], self.tg[:, 0:1],
                                                   X[:, t, :], ALU.mult, ALU.add).then_inc(x_new, 1)

    def route(self, layer, top, slots):
        nc, ins, X, XN, ps = self.nc, self.ins, self.X, self.XN, self.ps
        with ExitStack() as ctx:
            pre = f"t{layer}_"
            sb = lambda name, shape, dt=F32: ctx.enter_context(nc.sbuf_tensor(pre + name, shape, dt))
            xt = sb("xt", [P, T, KC, P])
            rw = sb("rw", [P, KC, E])
            rb = sb("rb", [P, E])
            names = ("L", "eq", "pr", "oh1", "oh2", "ohs", "L2", "incl", "incl2", "cnt", "row", "sel", "sh")
            L, eq, pr, oh1, oh2, ohs, L2, incl, incl2, cnt, row, sel, sh = (sb(n, [P, T, E]) for n in names)
            m1, m2, pm, den, gt = (sb(n, [P, T]) for n in ("m1", "m2", "pm", "den", "gt"))
            tot, end, end2 = (sb(n, [P, E]) for n in ("tot", "end", "end2"))
            toti = sb("toti", [P, E], I32)
            cmp = sb("cmp", [P, 64, E])
            se = sb("se", [P, 64])
            s_w, s_stat, s_ch, s_var, s_std, s_norm, s_turned, s_xt, s_log, s_oh, s_rank, s_exp, s_shift, s_dest, s_sc = (
                self.sem(pre + n) for n in ("w", "stat", "ch", "var", "std", "norm", "turned", "xt", "log",
                                            "oh", "rank", "exp", "shift", "dest", "sc"))
            rev = self.const[:, C_REV:C_REV + T * E].rearrange("p (t e) -> p t e", e=E)
            wide = lambda a: a.unsqueeze(2).broadcast_to([P, T, E])
            flat = lambda a: a[:].rearrange("p t e -> p (t e)")
            BL, BR, BC = 4, 5, 6

            with nc.Block() as block:
                @block.sync
                def _(sp):
                    sp.dma_start(rw[:], ins[f"rw{layer}"].rearrange("(k p) n -> p k n", p=P)).then_inc(s_w, 16)
                    if layer == 0:
                        sp.dma_start(rb[:], ins["rb0"].rearrange("(a n) -> a n", a=1).broadcast_to([P, E])).then_inc(s_w, 16)

                @block.tensor
                def _(pe):
                    for t in range(T + 1):
                        if t < T:
                            pe.wait_ge(s_norm, t + 1)
                            if t >= 4:
                                pe.wait_ge(s_xt, t - 3)
                            for k in range(KC):
                                mm = pe.transpose(ps[:, t % 4, k * P:(k + 1) * P], XN[:, t, k * P:(k + 1) * P], self.ident)
                            mm.then_inc(s_turned, 1)
                        if t == 0:
                            pe.wait_ge(s_w, 32 if layer == 0 else 16)
                            continue
                        pe.wait_ge(s_xt, t)
                        for k in range(KC):
                            mm = pe.matmul(ps[:, BL, (t - 1) * E:t * E], xt[:, t - 1, k, :], rw[:, k, :],
                                           start=k == 0, stop=k == KC - 1)
                        mm.then_inc(s_log, 1)
                    pe.wait_ge(s_oh, 1)
                    pe.matmul(ps[:, BR, 0:T * E], self.const[:, C_TRI:C_TRI + P], flat(ohs), start=True, stop=True)
                    pe.matmul(ps[:, BC, 0:T * E], self.const[:, C_ONES:C_ONES + P], flat(ohs),
                              start=True, stop=True).then_inc(s_rank, 1)

                @block.scalar
                def _(act):
                    self.ln_sqrt(act, s_var, s_std)
                    for t in range(T):
                        act.wait_ge(s_turned, t + 1)
                        act.copy(xt[:, t, :, :], ps[:, t % 4, 0:D].rearrange("p (k c) -> p k c", k=KC)).then_inc(s_xt, 1)
                    act.wait_ge(s_shift, 1)
                    if top == 1:
                        act.activation(flat(sh), flat(pr), ACT.Exp).then_inc(s_exp, 1)
                    else:
                        act.activation(pm[:], den[:], ACT.Exp).then_inc(s_exp, 1)

                @block.vector
                def _(e):
                    link = Chain(e, s_ch)
                    self.ln_stats(e, X, s_stat, link, s_var, s_std)
                    for t in range(T):
                        self.normalise(e, XN[:, t, :], X[:, t, :], t).then_inc(s_norm, 1)
                    e.wait_ge(s_log, T)
                    logits = ps[:, BL, 0:T * E].rearrange("p (t e) -> p t e", e=E)
                    if layer == 0:
                        link(e.tensor_tensor(L[:], logits, rb[:].unsqueeze(1).broadcast_to([P, T, E]), ALU.add))
                    else:
                        link(e.tensor_copy(L[:], logits))

                    def first_max(src, m, oh):
                        link(e.tensor_reduce(m[:], src[:], AX, ALU.max))
                        link(e.tensor_tensor(eq[:], src[:], wide(m[:]), ALU.is_equal))
                        link(e.tensor_tensor(pr[:], eq[:], rev, ALU.mult))
                        link(e.tensor_reduce(pm[:], pr[:], AX, ALU.max))
                        link(e.tensor_tensor(oh[:], rev, wide(pm[:]), ALU.is_equal))

                    first_max(L, m1, oh1)
                    hot = oh1
                    if top == 2:
                        link(e.scalar_tensor_tensor(L2[:], oh1[:], -BIG, L[:], ALU.mult, ALU.add))
                        first_max(L2, m2, oh2)
                        hot = ohs
                        link(e.tensor_tensor(ohs[:], oh1[:], oh2[:], ALU.add))
                    else:
                        link(e.tensor_copy(ohs[:], oh1[:]))
                    e.sem_inc(s_oh, 1)
                    tanh = self.tg[:, 2 + layer:3 + layer]
                    if top == 1:
                        link(e.tensor_tensor(pr[:], L[:], wide(m1[:]), ALU.subtract))
                        e.sem_inc(s_shift, 1)
                        e.wait_ge(s_exp, 1)
                        link(e.tensor_reduce(den[:], sh[:], AX, ALU.add))
                        link(e.reciprocal(gt[:], den[:]))
                        link(e.tensor_scalar(self.gate_w[:, 0, :], gt[:], tanh, None, ALU.mult))
                    else:
                        link(e.tensor_tensor(den[:], m2[:], m1[:], ALU.subtract))
                        e.sem_inc(s_shift, 1)
                        e.wait_ge(s_exp, 1)
                        link(e.tensor_scalar(den[:], pm[:], 1.0, None, ALU.add))
                        link(e.reciprocal(gt[:], den[:]))
                        link(e.tensor_scalar(self.gate_w[:, 0, :], gt[:], tanh, None, ALU.mult))
                        link(e.tensor_tensor(self.gate_w[:, 1, :], self.gate_w[:, 0, :], pm[:], ALU.mult))
                    e.wait_ge(s_rank, 1)
                    link(e.tensor_copy(flat(cnt), ps[:, BC, 0:T * E]))
                    src, dst = cnt, incl
                    for step in (1, 2, 4, 8):
                        e.tensor_copy(dst[:, 0:step, :], src[:, 0:step, :])
                        link(e.tensor_tensor(dst[:, step:, :], src[:, step:, :], src[:, :T - step, :], ALU.add))
                        src, dst = dst, (incl2 if dst is incl else incl)
                    link(e.tensor_scalar(tot[:], src[:, T - 1, :], float(P - 1), None, ALU.add))
                    link(e.tensor_copy(toti[:], tot[:]))
                    link(e.tensor_scalar(toti[:], toti[:], 7, None, ALU.arith_shift_right))
                    link(e.tensor_copy(tot[:], toti[:]))
                    a, b2 = tot, end
                    for step in (1, 2, 4):
                        e.tensor_copy(b2[:, 0:step], a[:, 0:step])
                        link(e.tensor_tensor(b2[:, step:], a[:, step:], a[:, :E - step], ALU.add))
                        a, b2 = b2, (end2 if b2 is end else end)
                    link(e.tensor_tensor(b2[:], a[:], tot[:], ALU.subtract))
                    link(e.tensor_scalar(b2[:], b2[:], float(P), None, ALU.mult))
                    link(e.tensor_tensor(flat(row), ps[:, BR, 0:T * E], flat(src), ALU.add))
                    link(e.tensor_tensor(row[:], row[:], cnt[:], ALU.subtract))
                    link(e.tensor_tensor(row[:], row[:], b2[:].unsqueeze(1).broadcast_to([P, T, E]), ALU.add))
                    for n, oh in enumerate((oh1, oh2)[:top]):
                        link(e.tensor_tensor(sel[:], row[:], oh[:], ALU.mult))
                        link(e.tensor_reduce(pm[:], sel[:], AX, ALU.add))
                        link(e.tensor_copy(self.dest[:, n, :], pm[:]))
                    e.sem_inc(s_dest, 1)
                    link(e.tensor_tensor(cmp[:], self.const[:, C_SLOT:C_SLOT + 64].unsqueeze(2).broadcast_to([P, 64, E]),
                                         a[:].unsqueeze(1).broadcast_to([P, 64, E]), ALU.is_ge))
                    link(e.tensor_reduce(se[:], cmp[:], AX, ALU.add))
                    link(e.tensor_scalar(se[:], se[:], float(E - 1), None, ALU.min))
                    link(e.tensor_copy(self.slot_expert[:], se[:]))

                @block.gpsimd
                def _(pool):
                    pool.wait_ge(self.s_zeroed[layer], 16 * ((slots + 1) // 8))
                    pool.wait_ge(s_dest, 1)
                    for n in range(top):
                        for t in range(T):
                            pool.indirect_dma_start(
                                self.rows[layer], bass.IndirectOffsetOnAxis(ap=self.dest[:, n, t:t + 1], axis=0),
                                XN[:, t, :], None).then_inc(s_sc, 16)
                    pool.wait_ge(s_sc, 16 * T * top)

    def experts(self, layer, slots, half_w):
        nc, ins, ps = self.nc, self.ins, self.ps
        up, cks = 4 * half_w, chunks(half_w)
        packed = up + len(cks) * D
        units = 2 * slots
        W_dram, rows, made = ins[f"We{layer}"], self.rows[layer], self.made[layer]
        with ExitStack() as ctx:
            pre = f"e{layer}_"
            sb = lambda name, shape: ctx.enter_context(nc.sbuf_tensor(pre + name, shape, F32))
            W = [sb(f"W{i}", [P, packed]) for i in range(4)]
            xin = [sb(f"xin{i}", [P, D]) for i in range(2)]
            xT = [sb(f"xT{i}", [P, KC, P]) for i in range(2)]
            sil = [sb(f"sil{i}", [P, half_w]) for i in range(2)]
            act_ = [sb(f"act{i}", [P, half_w]) for i in range(2)]
            aT = [sb(f"aT{i}", [P, len(cks), P]) for i in range(2)]
            y = [sb(f"y{i}", [P, D]) for i in range(2)]
            w_in = [self.sem(pre + f"w_in{i}") for i in range(4)]
            x_in = [self.sem(pre + f"x_in{i}") for i in range(2)]
            y_out = [self.sem(pre + f"y_out{i}") for i in range(2)]
            (x_turned, x_ready, h_ready, sil_ready, act_ready, a_turned, a_ready, y_part, y_read) = (
                self.sem(pre + n) for n in ("x_turned", "x_ready", "h_ready", "sil_ready", "act_ready",
                                            "a_turned", "a_ready", "y_part", "y_read"))
            up_w = lambda n: W[n % 4][:, 0:up].rearrange("p (k g c) -> p k g c", k=KC, g=2)
            down_w = lambda n: W[n % 4][:, up:].rearrange("p (c d) -> p c d", d=D)
            BT, BY, BX = 4, 6, 7

            with nc.Block() as block:
                @block.sync
                def _(sp):
                    def weights(s, n):
                        ex = sp.value_load(self.slot_expert[0:1, bass.ds(s, 1)], min_val=0, max_val=E - 1)
                        for hf in range(2):
                            yield hf, W_dram[bass.ds(ex * 2 + hf, 1), :, :].rearrange("a p c -> p (a c)")

                    for s in range(2):
                        sp.dma_start(xin[s][:], rows[s * P:(s + 1) * P, :]).then_inc(x_in[s], 16)
                        for hf, src in weights(s, 2 * s):
                            sp.dma_start(W[2 * s + hf][:], src).then_inc(w_in[2 * s + hf], 16)
                    def fetch(s, u):
                        sp.wait_ge(x_turned, s - 1)
                        sp.dma_start(xin[u][:], rows[bass.ds(s * P, P), :]).then_inc(x_in[u], 16)
                        for hf, src in weights(s, 2 * u):
                            sp.wait_ge(y_part, s * 2 + hf - 3)
                            sp.dma_start(W[2 * u + hf][:], src).then_inc(w_in[2 * u + hf], 16)
                    with sp.Fori(0, (slots - 3) // 2) as i:
                        for u in range(2):
                            fetch(i * 2 + (2 + u), u)
                    fetch(slots - 1, 0)
                    sp.wait_ge(x_turned, slots - 1)
                    sp.dma_start(xin[1][:], rows[slots * P:(slots + 1) * P, :]).then_inc(x_in[1], 16)

                @block.tensor
                def _(pe):
                    def turn_x(s, par, dma):
                        pe.wait_ge(x_in[par], dma * 16)
                        if not (isinstance(s, int) and s < 1):
                            pe.wait_ge(x_ready, s)
                        for k in range(KC):
                            mm = pe.transpose(ps[:, BX, k * P:(k + 1) * P], xin[par][:, k * P:(k + 1) * P], self.ident)
                        mm.then_inc(x_turned, 1)

                    def hidden(n, j, s, dma):
                        pe.wait_ge(w_in[j], dma * 16)
                        pe.wait_ge(x_ready, s + 1)
                        if not (isinstance(n, int) and n < 2):
                            pe.wait_ge(act_ready, n - 1)
                        for g in range(2):
                            for k in range(KC):
                                mm = pe.matmul(ps[:, 2 * (j % 2) + g, 0:half_w], xT[j // 2][:, k, :],
                                               up_w(j)[:, k, g, :], start=k == 0, stop=k == KC - 1)
                        mm.then_inc(h_ready, 1)

                    def turn_a(n, j):
                        pe.wait_ge(act_ready, n + 1)
                        if not (isinstance(n, int) and n < 2):
                            pe.wait_ge(a_ready, n - 1)
                        for c, (c0, cw) in enumerate(cks):
                            mm = pe.transpose(ps[0:cw, BT + j % 2, c * P:(c + 1) * P], act_[j % 2][:, c0:c0 + cw], self.ident)
                        mm.then_inc(a_turned, 1)

                    def down(n, j, s):
                        pe.wait_ge(a_ready, n + 1)
                        if j % 2 == 0 and not (isinstance(s, int) and s < 1):
                            pe.wait_ge(y_read, s)
                        for c, (c0, cw) in enumerate(cks):
                            mm = pe.matmul(ps[:, BY, 0:D], aT[j % 2][0:cw, c, :], down_w(j)[0:cw, c, :],
                                           start=j % 2 == 0 and c == 0, stop=j % 2 == 1 and c == len(cks) - 1)
                        mm.then_inc(y_part, 1)

                    turn_x(0, 0, 1)
                    hidden(0, 0, 0, 1)
                    hidden(1, 1, 0, 1)
                    turn_x(1, 1, 1)
                    turn_a(0, 0)
                    def four_units(i):
                        for v in range(4):
                            n, j = i * 4 + (2 + v), (2 + v) % 4
                            s = i * 2 + (1 + v // 2)
                            hidden(n, j, s, i + (1 if j >= 2 else 2))
                            if v % 2:
                                turn_x(s + 1, v // 2, i + 2)
                            turn_a(n - 1, (j + 3) % 4)
                            down(n - 2, (j + 2) % 4, s - 1)
                    four_units(0)
                    with pe.Fori(1, (units - 2) // 4) as i:
                        four_units(i)
                    n = units - 1
                    turn_a(n, n % 4)
                    down(n - 1, (n - 1) % 4, slots - 1)
                    down(n, n % 4, slots - 1)

                @block.scalar
                def _(act):
                    def silu(n, j):
                        act.wait_ge(h_ready, n + 1)
                        if not (isinstance(n, int) and n < 2):
                            act.wait_ge(act_ready, n - 1)
                        act.activation(sil[j % 2][:], ps[:, 2 * (j % 2), 0:half_w], ACT.Silu).then_inc(sil_ready, 1)

                    def copy_a(n, j):
                        act.wait_ge(a_turned, n + 1)
                        if not (isinstance(n, int) and n < 2):
                            act.wait_ge(y_part, n - 1)
                        full = len([1 for _, cw in cks if cw == P])
                        ins_ = act.copy(aT[j % 2][:, 0:full, :],
                                        ps[:, BT + j % 2, 0:full * P].rearrange("p (c t) -> p c t", t=P))
                        if full < len(cks):
                            cw = cks[-1][1]
                            ins_ = act.copy(aT[j % 2][0:cw, full, :], ps[0:cw, BT + j % 2, full * P:(full + 1) * P])
                        ins_.then_inc(a_ready, 1)

                    silu(0, 0)
                    for n in (1, 2):
                        silu(n, n)
                        copy_a(n - 1, n - 1)
                    with act.Fori(0, (units - 4) // 2) as i:
                        for v in range(2):
                            silu(i * 2 + (3 + v), 1 + v)
                            copy_a(i * 2 + (2 + v), v)
                    silu(units - 1, 1)
                    copy_a(units - 2, 0)
                    copy_a(units - 1, 1)

                @block.vector
                def _(e):
                    def copy_x(s, par):
                        e.wait_ge(x_turned, s + 1)
                        if not (isinstance(s, int) and s < 2):
                            e.wait_ge(h_ready, s * 2 - 2)
                        e.tensor_copy(xT[par][:], ps[:, BX, 0:D].rearrange("p (k t) -> p k t", k=KC)).then_inc(x_ready, 1)

                    def gate(n, j):
                        e.wait_ge(sil_ready, n + 1)
                        if not (isinstance(n, int) and n < 2):
                            e.wait_ge(a_turned, n - 1)
                        e.tensor_tensor(act_[j % 2][:], sil[j % 2][:], ps[:, 2 * (j % 2) + 1, 0:half_w],
                                        ALU.mult).then_inc(act_ready, 1)

                    def copy_y(s, par, dma):
                        e.wait_ge(y_part, s * 2 + 2)
                        if dma is not None:
                            e.wait_ge(y_out[par], dma * 16)
                        e.tensor_copy(y[par][:], ps[:, BY, 0:D]).then_inc(y_read, 1)

                    copy_x(0, 0)
                    gate(0, 0)
                    copy_x(1, 1)
                    gate(1, 1)
                    gate(2, 0)
                    copy_x(2, 0)
                    gate(3, 1)
                    copy_y(0, 0, None)
                    gate(4, 0)
                    copy_x(3, 1)
                    gate(5, 1)
                    copy_y(1, 1, None)
                    with e.Fori(0, (slots - 3) // 2) as i:
                        for u in range(2):
                            s = i * 2 + (3 + u)
                            gate(s * 2, 0)
                            copy_x(s + 1, u)
                            gate(s * 2 + 1, 1)
                            copy_y(s - 1, u, i + 1)
                    copy_y(slots - 1, 0, (slots - 1) // 2)

                @block.gpsimd
                def _(pool):
                    with pool.Fori(0, (slots - 1) // 2) as i:
                        for u in range(2):
                            pool.wait_ge(y_read, i * 2 + (u + 1))
                            pool.dma_start(made[bass.ds(i * (2 * P) + u * P, P), :], y[u][:]).then_inc(y_out[u], 16)
                    pool.wait_ge(y_read, slots)
                    pool.dma_start(made[(slots - 1) * P:slots * P, :], y[0][:]).then_inc(y_out[0], 16)
                    pool.wait_ge(y_out[0], 16 * ((slots + 1) // 2))
                    pool.wait_ge(y_out[1], 16 * ((slots - 1) // 2))

    def combine(self, layer, top, store):
        nc, X = self.nc, self.X
        pre = f"c{layer}_"
        RING = 8
        with ExitStack() as ctx:
            G = [ctx.enter_context(nc.sbuf_tensor(pre + f"G{i}", [P, D], F32)) for i in range(RING)]
            s_in = [self.sem(pre + f"in{i}") for i in range(RING)]
            s_used, s_out = self.sem(pre + "used"), self.sem(pre + "out")
            with nc.Block() as block:
                @block.gpsimd
                def _(pool):
                    for t in range(T):
                        for n in range(top):
                            m = t * top + n
                            if m >= RING:
                                pool.wait_ge(s_used, m - RING + 1)
                            pool.indirect_dma_start(
                                G[m % RING][:], None, self.made[layer],
                                bass.IndirectOffsetOnAxis(ap=self.dest[:, n, t:t + 1], axis=0)).then_inc(s_in[m % RING], 16)

                @block.vector
                def _(e):
                    for t in range(T):
                        for n in range(top):
                            m = t * top + n
                            e.wait_ge(s_in[m % RING], 16 * (m // RING + 1))
                            if n:
                                e.wait_ge(s_used, m)
                            e.scalar_tensor_tensor(X[:, t, :], G[m % RING][:], self.gate_w[:, n, t:t + 1],
                                                   X[:, t, :], ALU.mult, ALU.add).then_inc(s_used, 1)

                if store:
                    @block.sync
                    def _(sp):
                        out = self.out.rearrange("(t p) d -> p t d", p=P)
                        for t in range(0, T, 4):
                            sp.wait_ge(s_used, (t + 4) * top)
                            sp.dma_start(out[:, t:t + 4, :], X[:, t:t + 4, :]).then_inc(s_out, 16)
                        sp.wait_ge(s_out, 16 * (T // 4))

    def latents(self):
        nc, ins, X, XN, ps = self.nc, self.ins, self.X, self.XN, self.ps
        with ExitStack() as ctx:
            sb = lambda name, shape: ctx.enter_context(nc.sbuf_tensor(name, shape, F32))
            C = sb("l_C", [P, T, D])
            C2 = sb("l_C2", [P, T, D])
            Z = sb("l_Z", [P, T, D])
            kv = sb("l_kv", [P, B, KC, KEYS])
            s_c, s_stat, s_ch, s_var, s_std, s_norm, s_turned, s_kv, s_out = (
                self.sem("l_" + n) for n in ("c", "stat", "ch", "var", "std", "norm", "turned", "kv", "out"))
            with nc.Block() as block:
                @block.sync
                def _(sp):
                    sp.dma_start(C[:], ins["ctx"].rearrange("(t p) d -> p t d", p=P)).then_inc(s_c, 16)
                    sp.wait_ge(s_kv, 2 * T)
                    for b in range(B):
                        sp.dma_start(self.kv_dram[b], kv[:, b, :, :]).then_inc(s_out, 16)
                    sp.wait_ge(s_out, 16 * B)

                @block.vector
                def _(e):
                    link = Chain(e, s_ch)
                    self.ln_stats(e, X, s_stat, link, s_var, s_std, 1)
                    for t in range(T - 1):
                        self.normalise(e, XN[:, t, :], X[:, t, :], t)
                    link(self.normalise(e, XN[:, T - 1, :], X[:, T - 1, :], T - 1))
                    self.ln_stats(e, XN, s_stat, link, s_var, s_std, 2)
                    for t in range(T - 1):
                        self.normalise(e, Z[:, t, :], XN[:, t, :], t).then_inc(s_norm, 1)
                    self.normalise(e, Z[:, T - 1, :], XN[:, T - 1, :], T - 1).then_inc(s_norm, 1)
                    e.wait_ge(s_norm, T)
                    e.wait_ge(s_c, 16)
                    self.ln_stats(e, C, s_stat, link, s_var, s_std, 3)
                    for t in range(T):
                        self.normalise(e, C2[:, t, :], C[:, t, :], t).then_inc(s_norm, 1)

                @block.tensor
                def _(pe):
                    for m in range(2 * T):
                        src, t = (Z, m) if m < T else (C2, m - T)
                        pe.wait_ge(s_norm, m + 1)
                        if m >= 4:
                            pe.wait_ge(s_kv, m - 3)
                        for k in range(KC):
                            mm = pe.transpose(ps[:, m % 4, k * P:(k + 1) * P], src[:, t, k * P:(k + 1) * P], self.ident)
                        mm.then_inc(s_turned, 1)

                @block.scalar
                def _(act):
                    self.ln_sqrt(act, s_var, s_std, 1)
                    self.ln_sqrt(act, s_var, s_std, 2)

                    def affine(m):
                        latent, t = (1, m) if m < T else (0, m - T)
                        b, j = t // TB, t % TB
                        act.wait_ge(s_turned, m + 1)
                        for k in range(KC):
                            ins_ = act.activation(kv[:, b, k, latent * S + j * P:latent * S + (j + 1) * P],
                                                  ps[:, m % 4, k * P:(k + 1) * P], ACT.Identity,
                                                  bias=self.lnw[:, 2 * latent + 1, k:k + 1],
                                                  scale=self.lnw[:, 2 * latent, k:k + 1])
                        ins_.then_inc(s_kv, 1)

                    for m in range(T):
                        affine(m)
                    self.ln_sqrt(act, s_var, s_std, 3)
                    for m in range(T, 2 * T):
                        affine(m)

    def perceiver(self):
        nc, ins, X, ps = self.nc, self.ins, self.X, self.ps
        STEPS = H * TB
        with ExitStack() as ctx:
            sb = lambda name, shape, dt=F32: ctx.enter_context(nc.sbuf_tensor("p_" + name, shape, dt))
            kvT = sb("kvT", [P, KC, KEYS])
            Wq = sb("Wq", [P, KC, H, P])
            Wk = sb("Wk", [P, KC, H, P])
            Wv = sb("Wv", [P, KC, INNER])
            Wo = sb("Wo", [P, H, D])
            V2 = sb("V2", [P, KT, H, P], F32R)
            K2 = [sb(f"K2{i}", [P, KEYS], F32R) for i in range(2)]
            Qh = [sb(f"Qh{i}", [P, S], F32R) for i in range(2)]
            Ql = [sb(f"Ql{i}", [P, S], F32R) for i in range(2)]
            Pr = [sb(f"Pr{i}", [P, KEYS]) for i in range(3)]
            Pn = [sb(f"Pn{i}", [P, KEYS]) for i in range(2)]
            Ph = [sb(f"Ph{i}", [P, KT, 2 * P], F32R) for i in range(2)]
            Pl = [sb(f"Pl{i}", [P, KT, 2 * P], F32R) for i in range(2)]
            AT = sb("AT", [P, H, S])
            nmax = sb("nmax", [P, STEPS])
            nbias = sb("nbias", [P, STEPS])
            den = sb("den", [P, STEPS])
            rden = sb("rden", [P, STEPS])
            names = ("w", "kv_in", "proj", "proj_h", "proj_l", "v_ps", "v_h", "v_l", "s_ps", "max", "bias", "exp",
                     "rden", "norm", "turn", "ph", "pl", "o_ps", "o_sb", "y_ps", "y_add")
            (s_w, s_kv, proj, proj_h, proj_l, v_ps, v_h, v_l, s_ps, s_max, s_bias, s_exp, s_rden, s_norm,
             s_turn, s_ph, s_pl, o_ps, o_sb, y_ps, y_add) = (self.sem("p_" + n) for n in names)
            BO, BP, BTA = 6, 7, 4
            PROJ = 3 * H
            TURN = 2 * STEPS
            PAIRS = STEPS // 2

            with nc.Block() as block:
                @block.sync
                def _(sp):
                    for w, name in ((Wq, "Wq1"), (Wk, "Wk1")):
                        sp.dma_start(w[:], ins[name].rearrange("(k p) h n -> p k h n", p=P)).then_inc(s_w, 16)
                    sp.dma_start(Wv[:], ins["Wv1"].rearrange("(k p) n -> p k n", p=P)).then_inc(s_w, 16)
                    sp.dma_start(Wo[:], ins["Wo1"]).then_inc(s_w, 16)
                    sp.dma_start(kvT[:], self.kv_dram[0]).then_inc(s_kv, 16)
                    with sp.Fori(1, B) as b:
                        sp.wait_ge(proj, b * PROJ)
                        sp.dma_start(kvT[:], self.kv_dram[bass.ds(b, 1)].rearrange("a p k n -> p (a k) n")).then_inc(s_kv, 16)

                @block.tensor
                def _(pe):
                    def project(b, m):
                        h, part = m // 3, m % 3
                        pe.wait_ge(proj_l, b * PROJ + m + 1)
                        w = Wq if part == 2 else Wk
                        a = S if part == 2 else part * S
                        for k in range(KC):
                            mm = pe.matmul(ps[:, BP, :], w[:, k, h, :], kvT[:, k, a:a + S], start=k == 0, stop=k == KC - 1)
                        mm.then_inc(proj, 1)

                    def scores(b, t):
                        h, q = t // TB, t % TB
                        pe.wait_ge(proj_l, b * PROJ + 3 * h + 4)
                        if t >= 2:
                            pe.wait_ge(s_exp, b * STEPS + t - 1)
                        for c in range(2):
                            for n, Q in enumerate((Qh, Ql)):
                                mm = pe.matmul(ps[:, 2 * (t % 2) + c, :], Q[h % 2][:, q * P:(q + 1) * P],
                                               K2[h % 2][:, c * 512:(c + 1) * 512], start=n == 0, stop=n == 1)
                        mm.then_inc(s_ps, 1)

                    def turn(b, t):
                        pe.wait_ge(s_norm, b * STEPS + t + 1)
                        for g in range(2):
                            pe.wait_ge(s_pl, b * TURN + 2 * t + g + 1)
                            for c in range(4):
                                mm = pe.transpose(ps[:, BTA + g, c * P:(c + 1) * P],
                                                  Pn[t % 2][:, (4 * g + c) * P:(4 * g + c + 1) * P], self.ident)
                            mm.then_inc(s_turn, 1)

                    def attend(b, p):
                        h = p // 2
                        pe.wait_ge(s_pl, b * TURN + 4 * p + 6)
                        pe.wait_ge(o_sb, b * PAIRS + p + 1)
                        for c in range(KT):
                            for n, A in enumerate((Ph, Pl)):
                                mm = pe.matmul(ps[:, BO, 0:2 * P], V2[:, c, h, :], A[p % 2][:, c, :],
                                               start=c == 0 and n == 0, stop=c == KT - 1 and n == 1)
                        mm.then_inc(o_ps, 1)

                    pe.wait_ge(s_w, 64)
                    with pe.Fori(0, B) as b:
                        pe.wait_ge(s_kv, b * 16 + 16)
                        for c in range(KT):
                            if c >= 4:
                                pe.wait_ge(v_l, b * KT + c - 3)
                            if c == 0:
                                pe.wait_ge(y_add, b * TB + 1)
                            for k in range(KC):
                                mm = pe.matmul(ps[:, c % 4, :], kvT[:, k, c * P:(c + 1) * P], Wv[:, k, :],
                                               start=k == 0, stop=k == KC - 1)
                            mm.then_inc(v_ps, 1)
                            if 2 <= c < 5:
                                project(b, c - 2)
                        pe.wait_ge(v_l, b * KT + KT)
                        for t in range(STEPS + 4):
                            if t < STEPS:
                                scores(b, t)
                                h, q = t // TB, t % TB
                                if h + 1 < H and q < 3:
                                    project(b, 3 * (h + 1) + q)
                            if 2 <= t < STEPS + 2:
                                turn(b, t - 2)
                            if t >= 4 and t % 2 == 0:
                                attend(b, (t - 4) // 2)
                        pe.wait_ge(o_sb, b * PAIRS + PAIRS + 1)
                        for q in range(TB):
                            for h in range(H):
                                mm = pe.matmul(ps[:, q, 0:D], AT[:, h, q * P:(q + 1) * P], Wo[:, h, :],
                                               start=h == 0, stop=h == H - 1)
                            mm.then_inc(y_ps, 1)

                @block.scalar
                def _(act):
                    def split_high(b, m):
                        h, part = m // 3, m % 3
                        act.wait_ge(proj, b * PROJ + m + 1)
                        if part != 1:
                            act.wait_ge(s_ps, b * STEPS + TB * (h - 1)) if h >= 2 else None
                        dst = Qh[h % 2][:] if part == 2 else K2[h % 2][:, part * S:(part + 1) * S]
                        act.copy(dst, ps[:, BP, :]).then_inc(proj_h, 1)

                    def softmax_exp(b, t):
                        act.wait_ge(s_bias, b * STEPS + t + 1)
                        act.wait_ge(s_norm, b * STEPS + t + 1 - 3) if t >= 3 else None
                        act.activation(Pr[t % 3][:], self.bank(2 * (t % 2), 2), ACT.Exp, bias=nbias[:, t:t + 1],
                                       scale=DH ** -0.5, accum_out=den[:, t:t + 1]).then_inc(s_exp, 1)

                    def turned_high(b, t):
                        for g in range(2):
                            act.wait_ge(s_turn, b * TURN + 2 * t + g + 1)
                            if t >= 4 and t % 2 == 0 and g == 0:
                                act.wait_ge(o_ps, b * PAIRS + t // 2 - 1)
                            act.copy(Ph[(t // 2) % 2][:, 4 * g:4 * g + 4, (t % 2) * P:(t % 2 + 1) * P],
                                     ps[:, BTA + g, :].rearrange("p (c q) -> p c q", q=P)).then_inc(s_ph, 1)

                    with act.Fori(0, B) as b:
                        act.wait_ge(o_sb, b * PAIRS + 1)
                        act.wait_ge(y_add, b * TB + 1)
                        for c in range(KT):
                            act.wait_ge(v_ps, b * KT + c + 1)
                            act.copy(V2[:, c, :, 0:DH], ps[:, c % 4, :].rearrange("p (h d) -> p h d", d=DH)).then_inc(v_h, 1)
                            if 2 <= c < 5:
                                split_high(b, c - 2)
                        for t in range(STEPS + 2):
                            if t < STEPS:
                                softmax_exp(b, t)
                                h, q = t // TB, t % TB
                                if h + 1 < H and q < 3:
                                    split_high(b, 3 * (h + 1) + q)
                            if t >= 2:
                                turned_high(b, t - 2)

                @block.vector
                def _(e):
                    def split_low(b, m):
                        h, part = m // 3, m % 3
                        e.wait_ge(proj_h, b * PROJ + m + 1)
                        if part == 2:
                            e.wait_ge(s_ps, b * STEPS + TB * (h - 1)) if h >= 2 else None
                            e.tensor_tensor(Ql[h % 2][:], ps[:, BP, :], Qh[h % 2][:].bitcast(F32),
                                            ALU.subtract).then_inc(proj_l, 1)
                        else:
                            low = K2[h % 2][DH:P, part * S:(part + 1) * S]
                            e.tensor_tensor(low, ps[DH:P, BP, :], low.bitcast(F32), ALU.subtract).then_inc(proj_l, 1)

                    def row_max(b, t):
                        e.wait_ge(s_ps, b * STEPS + t + 1)
                        e.tensor_reduce(nmax[:, t:t + 1], self.bank(2 * (t % 2), 2), AX, ALU.max).then_inc(s_max, 1)
                        e.wait_ge(s_max, b * STEPS + t + 1)
                        e.tensor_scalar(nbias[:, t:t + 1], nmax[:, t:t + 1], -(DH ** -0.5), None,
                                        ALU.mult).then_inc(s_bias, 1)

                    def inverse(b, t):
                        e.wait_ge(s_exp, b * STEPS + t + 1)
                        e.reciprocal(rden[:, t:t + 1], den[:, t:t + 1]).then_inc(s_rden, 1)

                    def turned_low(b, t):
                        for g in range(2):
                            e.wait_ge(s_ph, b * TURN + 2 * t + g + 1)
                            if t >= 4 and t % 2 == 0 and g == 0:
                                e.wait_ge(o_ps, b * PAIRS + t // 2 - 1)
                            dst = (slice(None), slice(4 * g, 4 * g + 4), slice((t % 2) * P, (t % 2 + 1) * P))
                            e.tensor_tensor(Pl[(t // 2) % 2][dst], ps[:, BTA + g, :].rearrange("p (c q) -> p c q", q=P),
                                            Ph[(t // 2) % 2][dst].bitcast(F32), ALU.subtract).then_inc(s_pl, 1)

                    def copy_o(b, p):
                        h, q = p // 2, p % 2
                        e.wait_ge(o_ps, b * PAIRS + p + 1)
                        e.tensor_copy(AT[:, h, q * 2 * P:(q + 1) * 2 * P], ps[:, BO, 0:2 * P]).then_inc(o_sb, 1)

                    e.sem_inc(proj_l, 1)
                    e.sem_inc(s_pl, 2)
                    e.sem_inc(o_sb, 1)
                    e.sem_inc(y_add, 1)
                    with e.Fori(0, B) as b:
                        for c in range(KT):
                            e.wait_ge(v_h, b * KT + c + 1)
                            e.tensor_tensor(V2[:, c, :, DH:P], ps[:, c % 4, :].rearrange("p (h d) -> p h d", d=DH),
                                            V2[:, c, :, 0:DH].bitcast(F32), ALU.subtract).then_inc(v_l, 1)
                            if 2 <= c < 5:
                                split_low(b, c - 2)
                        for t in range(STEPS + 4):
                            if t < STEPS:
                                row_max(b, t)
                            if 1 <= t < STEPS + 1:
                                inverse(b, t - 1)
                            if t < STEPS:
                                h, q = t // TB, t % TB
                                if h + 1 < H and q < 3:
                                    split_low(b, 3 * (h + 1) + q)
                            if 2 <= t < STEPS + 2:
                                turned_low(b, t - 2)
                            if t >= 5 and t % 2 == 1:
                                copy_o(b, (t - 5) // 2)
                        for q in range(TB):
                            e.wait_ge(y_ps, b * TB + q + 1)
                            x = X[:, bass.ds(b * TB + q, 1), :].rearrange("p a d -> p (a d)")
                            e.scalar_tensor_tensor(x, ps[:, q, 0:D], self.tg[:, 1:2], x, ALU.mult, ALU.add).then_inc(y_add, 1)

                @block.gpsimd
                def _(pool):
                    with pool.Fori(0, B) as b:
                        for t in range(STEPS):
                            pool.wait_ge(s_rden, b * STEPS + t + 1)
                            if t >= 2:
                                pool.wait_ge(s_turn, b * TURN + 2 * (t - 1))
                            pool.tensor_tensor(Pn[t % 2][:], Pr[t % 3][:], rden[:, t:t + 1].broadcast_to([P, KEYS]),
                                               ALU.mult).then_inc(s_norm, 1)


def build(nc, ins, out, stop=99):
    with ExitStack() as ctx:
        p = Program(nc, ins, out, ctx)
        stages = [
            p.retention,
            lambda: p.route(0, 1, SLOTS0),
            lambda: p.experts(0, SLOTS0, F0 // 2),
            lambda: p.combine(0, 1, False),
            p.latents,
            p.perceiver,
            lambda: p.route(1, 2, SLOTS1),
            lambda: p.experts(1, SLOTS1, F1 // 2),
            lambda: p.combine(1, 2, True),
        ]
        for stage in stages[:stop]:
            stage()
        if stop < len(stages):
            s = p.sem("dbg")
            with nc.Block() as block:
                @block.sync
                def _(sp):
                    sp.dma_start(out.rearrange("(t p) d -> p t d", p=P), p.X[:]).then_inc(s, 16)
                    sp.wait_ge(s, 16)


def laid_out(inputs):
    a = {k: np.asarray(v) for k, v in inputs.items()}
    split = np.concatenate([np.arange(0, D, 2), np.arange(1, D, 2)])
    twice = lambda w: np.repeat(w.reshape(D, H, 1, DH), 2, axis=2).reshape(D, H, P)

    def packed(up, down, f):
        hw = f // 2
        nck = len(chunks(hw))
        u = up.reshape(E, KC, P, 2, 2, hw).transpose(0, 4, 2, 1, 3, 5).reshape(E, 2, P, KC * 2 * hw)
        d = down.reshape(E, 2, hw, D)
        d = np.concatenate([d, np.zeros((E, 2, nck * P - hw, D), d.dtype)], 2)
        d = d.reshape(E, 2, nck, P, D).transpose(0, 1, 3, 2, 4).reshape(E, 2, P, nck * D)
        return np.concatenate([u, d], 3).reshape(2 * E, P, -1)

    w1 = a["L0_ffn_w1"].reshape(E, D, 2, F0)
    up1 = np.stack([a["L1_ffn_W1"].transpose(0, 2, 1), a["L1_ffn_W2"].transpose(0, 2, 1)], 2)
    ln = [a[f"L1_xattn_ln_{n}"].reshape(KC, P).T for n in ("media_w", "media_b", "lat_w", "lat_b")]
    out = {
        "x": a["x"].reshape(B * S, D),
        "ctx": a["ctx_1024"].reshape(B * S, D),
        "ctxT": a["ctx_1024"].reshape(B * S, D).T,
        "g_xattn": a["g_xattn"], "g_ffn": a["g_ffn"],
        "const": shape_constants(), "tab": xpos_tables(),
        "lnw": np.stack(ln, 1),
        "Wq0": a["L0_xattn_Wq"][split].T, "Wk0": a["L0_xattn_Wk"][split].T, "Wv0": a["L0_xattn_Wv"].T,
        "rw0": a["L0_ffn_router_w"], "rb0": a["L0_ffn_router_b"],
        "We0": packed(w1, a["L0_ffn_w2"], F0),
        "Wq1": twice(a["L1_xattn_Wq"]), "Wk1": twice(a["L1_xattn_Wk"]), "Wv1": a["L1_xattn_Wv"],
        "Wo1": np.repeat(a["L1_xattn_Wout"].reshape(H, 1, DH, D), 2, axis=1).reshape(H, P, D).transpose(1, 0, 2),
        "rw1": a["L1_ffn_Wg"].T,
        "We1": packed(up1, a["L1_ffn_W3"].transpose(0, 2, 1), F1),
    }
    return {k: np.ascontiguousarray(v) for k, v in out.items()}


def kernel(**inputs):
    import concourse.bacc as bacc
    from concourse.bass_utils import run_bass_kernel_spmd

    nc = bacc.Bacc("TRN2", target_bir_lowering=False, num_devices=1)
    arrays, ins = {}, {}
    for name, a in laid_out(inputs).items():
        arrays[f"in_{name}"] = a
        ins[name] = nc.dram_tensor(f"in_{name}", a.shape, mybir.dt.from_np(a.dtype), kind="ExternalInput").ap()
    out = nc.dram_tensor("out", (B * S, D), F32, kind="ExternalOutput").ap()
    build(nc, ins, out)
    r = run_bass_kernel_spmd(nc, [arrays], core_ids=[0])
    return r.results[0]["out"].reshape(B, S, D)
```

```python
from contextlib import ExitStack

import numpy as np

import concourse.bass as bass
from concourse import mybir

F32 = mybir.dt.float32
F32R = mybir.dt.float32r
I32 = mybir.dt.int32
ALU = mybir.AluOpType
ACT = mybir.ActivationFunctionType
AX = mybir.AxisListType.X

P = 128
B, S, D = 4, 512, 256
KC = D // P
T = B * S // P
TB = S // P
E = 8
F0, F1 = 1024, 682
F1_PAD = 684
H, DH = 8, 64
INNER = H * DH
KEYS = 2 * S
KT = KEYS // P
EPS = 1e-5
BIG = 3.0e38
EARLY = 5
SLOTS0 = T + E - 1
SLOTS1 = 2 * T + E - 1


def chunks(width):
    return [(c, min(P, width - c)) for c in range(0, width, P)]


WIDTHS = {"ident": P, "tri": P, "causal": P, "ones": P, "iota": P, "rev": T * E, "slot": 64, "token": T, "pad": 64}
COL = dict(zip(WIDTHS, np.cumsum([0, *WIDTHS.values()])))
C_END = sum(WIDTHS.values())


def shape_constants():
    k, m = np.arange(P)[:, None], np.arange(P)[None, :]
    parts = {
        "ident": k == m, "tri": k < m, "causal": m >= k, "ones": np.ones((P, P)), "iota": m + 0 * k,
        "rev": np.tile(E - np.arange(E), T)[None] + 0 * k, "slot": np.arange(64)[None] + 0 * k,
        "token": np.arange(T)[None] * P + k, "pad": np.arange(64)[None] * P + k,
    }
    return np.concatenate([parts[n].astype(np.float32) for n in WIDTHS], 1)


def xpos_tables():
    f = np.float32
    base = (np.arange(0, D, 2, dtype=f) + f(0.4 * D)) / f(1.4 * D)
    pos = np.arange(S, dtype=f)
    freqs = f(1.0) / f(10000.0) ** (np.arange(D // 2, dtype=f) / f(D // 2))
    angle = (pos[:, None] * freqs[None, :]).astype(np.float64)
    scale = base[None, :].astype(np.float64) ** (pos[:, None] / 512.0)
    gamma = 0.96875 ** pos.astype(np.float64)[:, None]
    cos, sin = np.cos(angle), np.sin(angle)
    t = [cos * scale * gamma, sin * scale * gamma, cos / scale / gamma, sin / scale / gamma]
    return np.ascontiguousarray(np.stack([a.T for a in t], 1).astype(f))


class Count:

    def __init__(self, sem):
        self.sem, self.n = sem, 0


class Chain:

    def __init__(self, eng, count):
        self.eng, self.count = eng, count

    def __call__(self, ins):
        ins.then_inc(self.count.sem, 1)
        self.count.n += 1
        self.eng.wait_ge(self.count.sem, self.count.n)


class Program:
    def __init__(self, nc, ins, out, ctx):
        self.nc, self.ins, self.out = nc, ins, out
        self.n_sems = 0
        sb = lambda name, shape, dt=F32: ctx.enter_context(nc.sbuf_tensor(name, shape, dt))
        self.X = sb("X", [P, T, D])
        self.const = sb("const", [P, C_END])
        self.gates = sb("gates", [P, 4])
        self.tg = sb("tg", [P, 4])
        self.lnw = sb("lnw", [P, 4, KC])
        self.gather_idx = sb("gather_idx", [P, 64], I32)
        self.scatter_idx = sb("scatter_idx", [P, 64], I32)
        self.slot_gate = sb("slot_gate", [P, 64])
        self.slot_expert = sb("slot_expert", [P, 64], I32)
        self.stats = sb("stats", [P, T, 6])
        self.ln_tmp = sb("ln_tmp", [P, 4, T])
        self.mean = sb("mean", [P, T])
        self.rstd = sb("rstd", [P, T])
        self.std = sb("std", [P, T])
        self.ps = ctx.enter_context(nc.psum_tensor("ps", [P, 8, 512], F32))
        self.ident = self.const_of("ident")
        dram = lambda name, shape, dt=F32: nc.dram_tensor(name, shape, dt, kind="Internal").ap()
        self.normed = [dram("normed0", (T * P, D)), dram("normed1", (T * P, D))]
        self.made = [dram("made0", (T * P + SLOTS0 * P, D)), dram("made1", (2 * T * P + SLOTS1 * P, D))]
        self.kv_dram = dram("kv_t", (B, P, 2, KC, KEYS))
        self.ctx = ctx
        self.carried = self.sem("carried")
        self.chain, self.ln_stat, self.ln_std = Count(self.sem("chain")), Count(self.sem("ln_stat")), Count(self.sem("ln_std"))
        self.ln_var, self.ln_passes = self.sem("ln_var"), 0

    def sem(self, name):
        self.n_sems += 1
        return self.ctx.enter_context(self.nc.semaphore(name))

    def const_of(self, name):
        return self.const[:, COL[name]:COL[name] + WIDTHS[name]]

    def bank(self, i, n=1):
        return self.ps[:, i, :] if n == 1 else self.ps[:, i:i + n, :].rearrange("p b c -> p (b c)")

    def ln_stats(self, e, src, link):
        for t in range(T):
            e.bn_stats(self.stats[:, t, :], src[:, t, :]).then_inc(self.ln_stat.sem, 1)
        self.ln_stat.n += T
        e.wait_ge(self.ln_stat.sem, self.ln_stat.n)
        m_even, m_odd = self.stats[:, :, 1], self.stats[:, :, 4]
        v_even, v_odd = self.stats[:, :, 2], self.stats[:, :, 5]
        total, diff, diff2, var = (self.ln_tmp[:, i, :] for i in range(4))
        link(e.tensor_tensor(total, m_even, m_odd, ALU.add))
        link(e.tensor_tensor(diff, m_even, m_odd, ALU.subtract))
        link(e.scalar_tensor_tensor(diff2, diff, 0.25, diff, ALU.mult, ALU.mult))
        link(e.tensor_tensor(var, v_even, v_odd, ALU.add))
        link(e.tensor_scalar(self.mean[:], total, 0.5, None, ALU.mult))
        link(e.scalar_tensor_tensor(total, var, 1.0 / D, diff2, ALU.mult, ALU.add))
        link(e.tensor_scalar(var, total, EPS, None, ALU.add))
        e.sem_inc(self.ln_var, 1)
        self.ln_passes += 1
        e.wait_ge(self.ln_std.sem, self.ln_passes)
        link(e.reciprocal(self.rstd[:], self.std[:]))

    def ln_sqrt(self, act):
        self.ln_std.n += 1
        act.wait_ge(self.ln_var, self.ln_std.n)
        act.activation(self.std[:], self.ln_tmp[:, 3, :], ACT.Sqrt).then_inc(self.ln_std.sem, 1)

    def normalise(self, e, out, src, t):
        return e.tensor_scalar(out, src, self.mean[:, t:t + 1], self.rstd[:, t:t + 1],
                               ALU.subtract, ALU.mult)

    def retention(self):
        nc, ins, X, ps = self.nc, self.ins, self.X, self.ps
        with ExitStack() as ctx:
            sb = lambda name, shape: ctx.enter_context(nc.sbuf_tensor(name, shape, F32))
            XN = sb("r_XN", [P, T, D])
            XT = sb("r_XT", [P, KC, T * P])
            CT = sb("r_CT", [P, KC, T * P])
            tab = sb("r_tab", [P, 4, S])
            Wq = sb("r_Wq", [P, KC, D])
            Wk = sb("r_Wk", [P, KC, D])
            Wv = sb("r_Wv", [P, KC, D])
            tmp = sb("r_tmp", [P, 4, S])
            qR = sb("r_qR", [P, 2, S])
            kR = sb("r_kR", [P, 2, S])
            V = sb("r_V", [P, TB, D])
            ST = sb("r_ST", [P, TB, S])
            s_x, s_c, s_ct, s_w, s_g = (self.sem("r_" + n) for n in ("x", "c", "ct", "w", "g"))
            s_norm, s_turned, s_xt = (self.sem("r_" + n) for n in ("norm", "turned", "xt"))

            with nc.Block() as block:
                @block.sync
                def _(sp):
                    sp.dma_start(X[:], ins["x"].rearrange("(t p) d -> p t d", p=P)).then_inc(s_x, 16)
                    sp.dma_start(self.const[:], ins["const"]).then_inc(s_c, 16)
                    for w, name in ((Wq, "Wq0"), (Wk, "Wk0"), (Wv, "Wv0")):
                        sp.dma_start(w[:], ins[name].rearrange("(k p) n -> p k n", p=P)).then_inc(s_w, 16)
                    sp.dma_start(tab[:], ins["tab"]).then_inc(s_w, 16)
                    sp.dma_start(CT[:], ins["ctxT"].rearrange("(k p) n -> p k n", p=P)).then_inc(s_ct, 16)

                @block.scalar
                def _(act):
                    for i, name in enumerate(("g_xattn", "g_ffn")):
                        act.dma_start(self.gates[:, 2 * i:2 * i + 2],
                                      ins[name].rearrange("(a n) -> a n", a=1).broadcast_to([P, 2])).then_inc(s_g, 16)
                    act.dma_start(self.lnw[:], ins["lnw"]).then_inc(s_g, 16)
                    act.wait_ge(s_g, 48)
                    act.activation(self.tg[:], self.gates[:], ACT.Tanh)
                    self.ln_sqrt(act)
                    for t in range(T):
                        act.wait_ge(s_turned, t + 1)
                        act.copy(XT[:, :, t * P:(t + 1) * P],
                                 self.ps[:, t % 4, 0:D].rearrange("p (k c) -> p k c", k=KC)).then_inc(s_xt, 1)

                @block.vector
                def _(e):
                    link = Chain(e, self.chain)
                    e.wait_ge(s_x, 16)
                    self.ln_stats(e, X, link)
                    for t in range(T):
                        self.normalise(e, XN[:, t, :], X[:, t, :], t).then_inc(s_norm, 1)

                @block.tensor
                def _(pe):
                    pe.wait_ge(s_c, 16)
                    for t in range(T):
                        pe.wait_ge(s_norm, t + 1)
                        if t >= 4:
                            pe.wait_ge(s_xt, t - 3)
                        for k in range(KC):
                            mm = pe.transpose(ps[:, t % 4, k * P:(k + 1) * P],
                                              XN[:, t, k * P:(k + 1) * P], self.ident)
                        mm.then_inc(s_turned, 1)

            names = ("q_ps", "k_ps", "v_ps", "rot", "v_sb", "s_ps", "diag", "rest", "o_ps", "x_new")
            q_ps, k_ps, v_ps, rot, v_sb, s_ps, diag, rest, o_ps, x_new = (self.sem("r2_" + n) for n in names)
            with nc.Block() as block:
                @block.tensor
                def _(pe):
                    pe.wait_ge(s_w, 64)
                    pe.wait_ge(s_ct, 16)
                    for b in range(B):
                        if b:
                            pe.wait_ge(diag, TB * b)
                            pe.wait_ge(rest, (TB - 1) * b)
                        for w, src, bank, sem in ((Wq, XT, 0, q_ps), (Wk, CT, 2, k_ps)):
                            for half in range(2):
                                for k in range(KC):
                                    mm = pe.matmul(ps[:, bank + half, :], w[:, k, half * P:(half + 1) * P],
                                                   src[:, k, b * S:(b + 1) * S], start=k == 0, stop=k == KC - 1)
                            mm.then_inc(sem, 1)
                        for j in range(TB):
                            if b and j % 2 == 0:
                                pe.wait_ge(v_sb, 2 * (b - 1) + j // 2 + 1)
                            for k in range(KC):
                                mm = pe.matmul(ps[:, 4 + j // 2, (j % 2) * D:(j % 2 + 1) * D],
                                               CT[:, k, (b * TB + j) * P:(b * TB + j + 1) * P],
                                               Wv[:, k, :], start=k == 0, stop=k == KC - 1)
                            if j % 2:
                                mm.then_inc(v_ps, 1)
                        pe.wait_ge(rot, 2 * (b + 1))
                        for j in range(TB):
                            for half in range(2):
                                mm = pe.matmul(ps[:, j, 0:S - j * P], kR[:, half, j * P:(j + 1) * P],
                                               qR[:, half, j * P:S], start=half == 0, stop=half == 1)
                            mm.then_inc(s_ps, 1)
                        pe.wait_ge(v_sb, 2 * (b + 1))
                        for i in range(TB):
                            pe.wait_ge(diag, TB * b + i + 1)
                            if i:
                                pe.wait_ge(rest, (TB - 1) * b + i)
                            if TB * b + i >= 2:
                                pe.wait_ge(x_new, TB * b + i - 1)
                            for j in range(i + 1):
                                mm = pe.matmul(ps[:, 6 + i % 2, 0:D], ST[:, j, (i - j) * P:(i - j + 1) * P],
                                               V[:, j, :], start=j == 0, stop=j == i)
                            mm.then_inc(o_ps, 1)

                @block.scalar
                def _(act):
                    for b in range(B):
                        if b:
                            act.wait_ge(o_ps, TB * b)
                        for h in range(2):
                            act.wait_ge(v_ps, 2 * b + h + 1)
                            act.copy(V[:, 2 * h:2 * h + 2, :],
                                     ps[:, 4 + h, :].rearrange("p (j d) -> p j d", j=2)).then_inc(v_sb, 1)
                        for j in range(TB - 1):
                            act.wait_ge(s_ps, TB * b + j + 1)
                            act.copy(ST[:, j, P:S - j * P], ps[:, j, P:S - j * P]).then_inc(rest, 1)

                @block.vector
                def _(e):
                    link = Chain(e, self.chain)
                    for b in range(B):
                        for n, (sem, bank, dst) in enumerate(((q_ps, 0, qR), (k_ps, 2, kR))):
                            even, odd = ps[:, bank, :], ps[:, bank + 1, :]
                            cos, sin = tab[:, 2 * n, :], tab[:, 2 * n + 1, :]
                            e.wait_ge(sem, b + 1)
                            if b and n == 0:
                                e.wait_ge(s_ps, TB * b)
                            e.tensor_tensor(tmp[:, 0, :], even, cos, ALU.mult)
                            e.tensor_tensor(tmp[:, 1, :], odd, sin, ALU.mult)
                            e.tensor_tensor(tmp[:, 2, :], odd, cos, ALU.mult)
                            link(e.tensor_tensor(tmp[:, 3, :], even, sin, ALU.mult))
                            link(e.tensor_tensor(dst[:, 0, :], tmp[:, 0, :], tmp[:, 1, :], ALU.subtract))
                            link(e.tensor_tensor(dst[:, 1, :], tmp[:, 2, :], tmp[:, 3, :], ALU.add))
                            e.sem_inc(rot, 1)
                        for j in range(TB):
                            e.wait_ge(s_ps, TB * b + j + 1)
                            if j < TB - 1:
                                e.wait_ge(rest, (TB - 1) * b + j + 1)
                            if b:
                                e.wait_ge(o_ps, TB * b)
                            e.tensor_tensor(ST[:, j, 0:P], ps[:, j, 0:P],
                                            self.const_of("causal"), ALU.mult).then_inc(diag, 1)
                        for i in range(TB):
                            t = TB * b + i
                            e.wait_ge(o_ps, t + 1)
                            e.scalar_tensor_tensor(X[:, t, :], ps[:, 6 + i % 2, 0:D], self.tg[:, 0:1],
                                                   X[:, t, :], ALU.mult, ALU.add).then_inc(x_new, 1)

    def route(self, layer, top, slots):
        nc, ins, X, ps = self.nc, self.ins, self.X, self.ps
        with ExitStack() as ctx:
            pre = f"t{layer}_"
            sb = lambda name, shape, dt=F32: ctx.enter_context(nc.sbuf_tensor(pre + name, shape, dt))
            spare = self.W_all[:, 2 * EARLY:, :].rearrange("p e c -> p (e c)") if layer == 1 else None
            used = [0]

            def table(name, shape):
                if layer == 0:
                    return sb(name, shape)[:]
                size = int(np.prod(shape[1:]))
                at = used[0]
                used[0] += size
                letters = "abc"[:len(shape) - 1]
                form = f"p ({' '.join(letters)}) -> p {' '.join(letters)}"
                return spare[:, at:at + size].rearrange(form, **dict(zip(letters, shape[1:])))

            XN = sb("XN", [P, T, D])
            xt = table("xt", [P, T, KC, P])
            rw = sb("rw", [P, KC, E])
            rb = sb("rb", [P, E])
            names = ("L", "eq", "pr", "oh1", "oh2", "ohs", "L2", "incl", "incl2", "cnt", "row", "sel", "sh")
            L, eq, pr, oh1, oh2, ohs, L2, incl, incl2, cnt, row, sel, sh = (sb(n, [P, T, E]) for n in names)
            m1, m2, pm, den, gt = (sb(n, [P, T]) for n in ("m1", "m2", "pm", "den", "gt"))
            tot, end, end2 = (sb(n, [P, E]) for n in ("tot", "end", "end2"))
            toti = sb("toti", [P, E], I32)
            gate = [sb(f"gate{n}", [P, T]) for n in range(top)]
            place = sb("place", [P, 2, T], I32)
            where = sb("where", [P, 2, T])
            ids = sb("ids", [P, T])
            in_row = [table(f"in_row{n}", [P, T, P]) for n in range(top)]
            in_slot = [table(f"in_slot{n}", [P, 3, T, slots]) for n in range(top)]
            made_of = sb("made_of", [P, slots])
            free = sb("free", [P, slots])
            cmp = sb("cmp", [P, 64, E])
            se = sb("se", [P, 64])
            s_w, s_norm, s_turned, s_xt, s_log, s_oh, s_rank, s_exp, s_shift, s_hot, s_map, s_out = (
                self.sem(pre + n) for n in ("w", "norm", "turned", "xt", "log",
                                            "oh", "rank", "exp", "shift", "hot", "map", "out"))
            s_down = self.sem(pre + "down")
            if layer == 0:
                C = sb("C", [P, T, D])
                self.kv_buffers(ctx, "media")
            rev = self.const_of("rev").rearrange("p (t e) -> p t e", e=E)
            wide = lambda a: a.unsqueeze(2).broadcast_to([P, T, E])
            flat = lambda a: a[:].rearrange("p t e -> p (t e)")
            BL, BR, BC, BM = 4, 5, 6, 7

            with nc.Block() as block:
                @block.sync
                def _(sp):
                    sp.dma_start(rw[:], ins[f"rw{layer}"].rearrange("(k p) n -> p k n", p=P)).then_inc(s_w, 16)
                    if layer == 0:
                        sp.dma_start(rb[:], ins["rb0"].rearrange("(a n) -> a n", a=1).broadcast_to([P, E])).then_inc(s_w, 16)
                    if layer == 1:
                        for ex in range(EARLY):
                            sp.dma_start(self.W_all[:, 2 * ex:2 * ex + 2, :],
                                         ins["We1"][2 * ex:2 * ex + 2].rearrange("a p c -> p a c")).then_inc(self.w1_in, 16)
                    if layer == 0:
                        sp.dma_start(C[:], ins["ctx"].rearrange("(t p) d -> p t d", p=P)).then_inc(self.kv_c, 16)
                        src = ins["We0"][:, :, 2 * KC * (F0 // 2):].rearrange("a p c -> p a c")
                        sp.dma_start(self.W_down[:], src).then_inc(s_down, 16)
                    rows = self.normed[layer].rearrange("(t p) d -> p t d", p=P)
                    for t in range(0, T, 4):
                        sp.wait_ge(s_norm, t + 4)
                        sp.dma_start(rows[:, t:t + 4, :], XN[:, t:t + 4, :]).then_inc(s_out, 16)
                    sp.wait_ge(s_out, 16 * (T // 4))
                    if layer == 0:
                        sp.wait_ge(s_down, 16)
                        self.kv_store(sp, 0)
                    else:
                        sp.wait_ge(self.w1_in, 16 * EARLY)

                @block.tensor
                def _(pe):
                    for t in range(T + 1):
                        if t < T:
                            pe.wait_ge(s_norm, t + 1)
                            if t >= 4:
                                pe.wait_ge(s_xt, t - 3)
                            for k in range(KC):
                                mm = pe.transpose(ps[:, t % 4, k * P:(k + 1) * P], XN[:, t, k * P:(k + 1) * P], self.ident)
                            mm.then_inc(s_turned, 1)
                        if t == 0:
                            pe.wait_ge(s_w, 32 if layer == 0 else 16)
                            continue
                        pe.wait_ge(s_xt, t)
                        for k in range(KC):
                            mm = pe.matmul(ps[:, BL, (t - 1) * E:t * E], xt[:, t - 1, k, :], rw[:, k, :],
                                           start=k == 0, stop=k == KC - 1)
                        mm.then_inc(s_log, 1)
                    pe.wait_ge(s_oh, 1)
                    pe.matmul(ps[:, BR, 0:T * E], self.const_of("tri"), flat(ohs), start=True, stop=True)
                    pe.matmul(ps[:, BC, 0:T * E], self.const_of("ones"), flat(ohs),
                              start=True, stop=True).then_inc(s_rank, 1)
                    if layer == 0:
                        self.kv_turn(pe, C)
                    for n in range(top):
                        pe.wait_ge(s_hot, n + 1)
                        for t in range(T):
                            mm = pe.matmul(ps[:, BM, 0:3 * slots].rearrange("p (a s) -> p a s", s=slots),
                                           in_row[n][:, t, :], in_slot[n][:, :, t, :],
                                           start=n == 0 and t == 0, stop=n == top - 1 and t == T - 1)
                    mm.then_inc(s_map, 1)

                @block.scalar
                def _(act):
                    self.ln_sqrt(act)
                    for t in range(T):
                        act.wait_ge(s_turned, t + 1)
                        act.copy(xt[:, t, :, :], ps[:, t % 4, 0:D].rearrange("p (k c) -> p k c", k=KC)).then_inc(s_xt, 1)
                        if layer == 0 and t == T // 2:
                            self.ln_sqrt(act)
                    act.wait_ge(s_shift, 1)
                    if top == 1:
                        act.activation(flat(sh), flat(pr), ACT.Exp).then_inc(s_exp, 1)
                    else:
                        act.activation(pm[:], den[:], ACT.Exp).then_inc(s_exp, 1)
                    if layer == 0:
                        self.kv_affine(act, 0)

                @block.vector
                def _(e):
                    link = Chain(e, self.chain)
                    self.ln_stats(e, X, link)
                    for t in range(T):
                        self.normalise(e, XN[:, t, :], X[:, t, :], t).then_inc(s_norm, 1)
                    if layer == 0:
                        e.wait_ge(self.kv_c, 16)
                        self.ln_stats(e, C, link)
                        for t in range(T):
                            self.normalise(e, C[:, t, :], C[:, t, :], t).then_inc(self.kv_norm, 1)
                    e.wait_ge(s_log, T)
                    logits = ps[:, BL, 0:T * E].rearrange("p (t e) -> p t e", e=E)
                    if layer == 0:
                        link(e.tensor_tensor(L[:], logits, rb[:].unsqueeze(1).broadcast_to([P, T, E]), ALU.add))
                    else:
                        link(e.tensor_copy(L[:], logits))

                    def first_max(src, m, oh):
                        link(e.tensor_reduce(m[:], src[:], AX, ALU.max))
                        link(e.tensor_tensor(eq[:], src[:], wide(m[:]), ALU.is_equal))
                        link(e.tensor_tensor(pr[:], eq[:], rev, ALU.mult))
                        link(e.tensor_reduce(pm[:], pr[:], AX, ALU.max))
                        link(e.tensor_tensor(oh[:], rev, wide(pm[:]), ALU.is_equal))

                    first_max(L, m1, oh1)
                    hot = oh1
                    if top == 2:
                        link(e.scalar_tensor_tensor(L2[:], oh1[:], -BIG, L[:], ALU.mult, ALU.add))
                        first_max(L2, m2, oh2)
                        hot = ohs
                        link(e.tensor_tensor(ohs[:], oh1[:], oh2[:], ALU.add))
                    else:
                        link(e.tensor_copy(ohs[:], oh1[:]))
                    e.sem_inc(s_oh, 1)
                    tanh = self.tg[:, 2 + layer:3 + layer]
                    if top == 1:
                        link(e.tensor_tensor(pr[:], L[:], wide(m1[:]), ALU.subtract))
                        e.sem_inc(s_shift, 1)
                        e.wait_ge(s_exp, 1)
                        link(e.tensor_reduce(den[:], sh[:], AX, ALU.add))
                        link(e.reciprocal(gt[:], den[:]))
                        link(e.tensor_scalar(gate[0][:], gt[:], tanh, None, ALU.mult))
                    else:
                        link(e.tensor_tensor(den[:], m2[:], m1[:], ALU.subtract))
                        e.sem_inc(s_shift, 1)
                        e.wait_ge(s_exp, 1)
                        link(e.tensor_scalar(den[:], pm[:], 1.0, None, ALU.add))
                        link(e.reciprocal(gt[:], den[:]))
                        link(e.tensor_scalar(gate[0][:], gt[:], tanh, None, ALU.mult))
                        link(e.tensor_tensor(gate[1][:], gate[0][:], pm[:], ALU.mult))
                    e.wait_ge(s_rank, 1)
                    link(e.tensor_copy(flat(cnt), ps[:, BC, 0:T * E]))
                    src, dst = cnt, incl
                    for step in (1, 2, 4, 8):
                        e.tensor_copy(dst[:, 0:step, :], src[:, 0:step, :])
                        link(e.tensor_tensor(dst[:, step:, :], src[:, step:, :], src[:, :T - step, :], ALU.add))
                        src, dst = dst, (incl2 if dst is incl else incl)
                    link(e.tensor_scalar(tot[:], src[:, T - 1, :], float(P - 1), None, ALU.add))
                    link(e.tensor_copy(toti[:], tot[:]))
                    link(e.tensor_scalar(toti[:], toti[:], 7, None, ALU.arith_shift_right))
                    link(e.tensor_copy(tot[:], toti[:]))
                    a, b2 = tot, end
                    for step in (1, 2, 4):
                        e.tensor_copy(b2[:, 0:step], a[:, 0:step])
                        link(e.tensor_tensor(b2[:, step:], a[:, step:], a[:, :E - step], ALU.add))
                        a, b2 = b2, (end2 if b2 is end else end)
                    link(e.tensor_tensor(b2[:], a[:], tot[:], ALU.subtract))
                    link(e.tensor_scalar(b2[:], b2[:], float(P), None, ALU.mult))
                    link(e.tensor_tensor(flat(row), ps[:, BR, 0:T * E], flat(src), ALU.add))
                    link(e.tensor_tensor(row[:], row[:], cnt[:], ALU.subtract))
                    link(e.tensor_tensor(row[:], row[:], b2[:].unsqueeze(1).broadcast_to([P, T, E]), ALU.add))
                    slot_no = self.const_of("slot")[:, 0:slots].unsqueeze(1).broadcast_to([P, T, slots])
                    for n, oh in enumerate((oh1, oh2)[:top]):
                        link(e.tensor_tensor(sel[:], row[:], oh[:], ALU.mult))
                        link(e.tensor_reduce(pm[:], sel[:], AX, ALU.add))
                        link(e.tensor_copy(place[:, 0, :], pm[:]))
                        e.tensor_scalar(place[:, 1, :], place[:, 0, :], 7, None, ALU.arith_shift_right)
                        e.tensor_scalar(ids[:], self.const_of("token"), float(n * T * P), None, ALU.add)
                        link(e.tensor_scalar(place[:, 0, :], place[:, 0, :], P - 1, None, ALU.bitwise_and))
                        link(e.tensor_copy(where[:], place[:]))
                        e.tensor_tensor(in_row[n], self.const_of("iota").unsqueeze(1).broadcast_to([P, T, P]),
                                        where[:, 0, :].unsqueeze(2).broadcast_to([P, T, P]), ALU.is_equal)
                        link(e.tensor_tensor(in_slot[n][:, 2, :, :], slot_no,
                                             where[:, 1, :].unsqueeze(2).broadcast_to([P, T, slots]), ALU.is_equal))
                        for v, value in ((0, ids[:]), (1, gate[n][:])):
                            ins_ = e.tensor_tensor(in_slot[n][:, v, :, :], in_slot[n][:, 2, :, :],
                                                   value.unsqueeze(2).broadcast_to([P, T, slots]), ALU.mult)
                        link(ins_)
                        e.sem_inc(s_hot, 1)
                    link(e.tensor_tensor(cmp[:], self.const_of("slot").unsqueeze(2).broadcast_to([P, 64, E]),
                                         a[:].unsqueeze(1).broadcast_to([P, 64, E]), ALU.is_ge))
                    link(e.tensor_reduce(se[:], cmp[:], AX, ALU.add))
                    link(e.tensor_scalar(se[:], se[:], float(E - 1), None, ALU.min))
                    link(e.tensor_copy(self.slot_expert[:], se[:]))
                    link(e.memset(self.gather_idx[:], 0))
                    if layer == 0:
                        self.kv_low(e)
                    e.wait_ge(s_map, 1)
                    mapped = lambda v: ps[:, BM, v * slots:(v + 1) * slots]
                    link(e.tensor_copy(self.slot_gate[:, 0:slots], mapped(1)))
                    link(e.tensor_copy(self.gather_idx[:, 0:slots], mapped(0)))
                    link(e.tensor_scalar(self.gather_idx[:, 0:slots], self.gather_idx[:, 0:slots], T * P - 1, None,
                                         ALU.bitwise_and))
                    link(e.tensor_scalar(free[:], mapped(2), -1.0, 1.0, ALU.mult, ALU.add))
                    link(e.scalar_tensor_tensor(free[:], self.const_of("pad")[:, 0:slots], float(top * T * P), free[:],
                                                ALU.add, ALU.mult))
                    link(e.tensor_tensor(made_of[:], mapped(0), free[:], ALU.add))
                    link(e.tensor_copy(self.scatter_idx[:, 0:slots], made_of[:]))

    def experts(self, layer, slots, half_w):
        nc, ins, ps = self.nc, self.ins, self.ps
        cks = chunks(half_w)
        edges = np.cumsum([0, KC * half_w, KC * half_w, len(cks) * D])
        A, G, DN = (slice(int(edges[i]), int(edges[i + 1])) for i in range(3))
        packed = int(edges[-1])
        units = 2 * slots
        resident = layer == 1
        W_dram = ins[f"We{layer}"]
        with ExitStack() as ctx:
            pre = f"e{layer}_"
            sb = lambda name, shape, dt=F32: ctx.enter_context(nc.sbuf_tensor(pre + name, shape, dt))
            if resident:
                W = self.W_all
            else:
                W = [sb(f"W{i}", [P, DN.start]) for i in range(4)]
            Ws = [sb(f"Ws{i}", [P, 2, packed], F32R) for i in range(2)]
            xT = [sb(f"xT{i}", [P, 2, KC, P], F32R) for i in range(2)]
            aT = [sb(f"aT{i}", [P, 2, len(cks), P], F32R) for i in range(2)]
            NX, NY = 2, 1 if resident else 2
            xin = [sb(f"xin{i}", [P, D]) for i in range(NX)]
            act_ = [sb(f"act{i}", [P, half_w]) for i in range(2)]
            y = [sb(f"y{i}", [P, D]) for i in range(NY)]
            from_tok = [sb(f"from{i}", [P, 1], I32) for i in range(NX)]
            to_row = [sb(f"to{i}", [P, 1], I32) for i in range(NY)]
            x_in = [self.sem(pre + f"x_in{i}") for i in range(NX)]
            y_out = [self.sem(pre + f"y_out{i}") for i in range(NY)]
            w_in = [self.w1_in] if resident else [self.sem(pre + f"w_in{i}") for i in range(4)]
            (from_ready, to_ready, x_turned, x_high, x_low, A_high, A_low, G_high, G_low,
             D_high, D_low, A_done, G_done, D_done, sil_ready, act_ready, a_turned, a_high, a_low, y_read) = (
                self.sem(pre + n) for n in (
                    "from_ready", "to_ready", "x_turned", "x_high", "x_low", "A_high",
                    "A_low", "G_high", "G_low", "D_high", "D_low", "A_done", "G_done", "D_done", "sil_ready",
                    "act_ready", "a_turned", "a_high", "a_low", "y_read"))
            BT, BY, BX = 4, 6, 7

            def every(eng, unit):
                for n in range(4):
                    unit(n, n, n // 2)
                with eng.Fori(1, (units - 2) // 4) as i:
                    for v in range(4):
                        unit(i * 4 + v, v, i * 2 + v // 2)
                for n in (units - 2, units - 1):
                    unit(n, n % 4, n // 2)

            first = lambda n, count: isinstance(n, int) and n < count
            x_before = lambda s, par: (s - par) * 8
            y_before = lambda s, par: (s - par) * 8 if NY == 2 else s * 16
            exists = lambda n: not isinstance(n, int) or n < units

            def raw(eng, ex, j, piece):
                if resident:
                    return W[:, bass.ds(ex * 2 + j % 2, 1), piece].rearrange("p a c -> p (a c)")
                if piece is DN:
                    return self.W_down[:, bass.ds(ex * 2 + j % 2, 1), :].rearrange("p a c -> p (a c)")
                return W[j][:, piece]

            def expert_of(eng, s, needed=True):
                return eng.value_load(self.slot_expert[0:1, bass.ds(s, 1)], min_val=0, max_val=E - 1) if needed else None

            with nc.Block() as block:
                @block.sync
                def _(sp):
                    if resident:
                        sp.wait_ge(x_turned, 2)
                        for ex in range(EARLY, E):
                            sp.wait_ge(w_in[0], 16 * ex)
                            sp.dma_start(W[:, 2 * ex:2 * ex + 2, :],
                                         W_dram[2 * ex:2 * ex + 2].rearrange("a p c -> p a c")).then_inc(w_in[0], 16)
                        return

                    def fetch(n, j, s):
                        if j % 2 == 0:
                            for hf in range(2):
                                ex = sp.value_load(self.slot_expert[0:1, bass.ds(s, 1)], min_val=0, max_val=E - 1)
                                if not first(n, 4):
                                    sp.wait_ge(G_low, n + hf - 3)
                                    sp.wait_ge(D_low, n + hf - 3)
                                sp.dma_start(W[j + hf][:], W_dram[bass.ds(ex * 2 + hf, 1), :, 0:DN.start].rearrange(
                                    "a p c -> p (a c)")).then_inc(w_in[j + hf], 16)
                    every(sp, fetch)

                @block.tensor
                def _(pe):
                    def exact(out, lhs, rhs, ks, start=True, stop=True):
                        parts = [(i, j, k) for i, j in ((0, 0), (0, 1), (1, 0)) for k in ks]
                        for m, (i, j, k) in enumerate(parts):
                            mm = pe.matmul(out, lhs(i, k), rhs(j, k), start=start and m == 0,
                                           stop=stop and m == len(parts) - 1)
                        return mm

                    def up(j, g, piece):
                        w = Ws[j % 2][:, :, piece].rearrange("p h (k c) -> p h k c", k=KC)
                        return exact(ps[:, 2 * (j % 2) + g, 0:half_w], lambda i, k: xT[j // 2][:, i, k, :],
                                     lambda i, k: w[:, i, k, :], range(KC))

                    def product_G(n, j):
                        pe.wait_ge(G_low, n + 1)
                        if not first(n, 2):
                            pe.wait_ge(act_ready, n - 1)
                        up(j, 1, G).then_inc(G_done, 1)

                    def product_A(n, j, s):
                        pe.wait_ge(A_low, n + 1)
                        if not first(n, 2):
                            pe.wait_ge(sil_ready, n - 1)
                        if j % 2 == 0:
                            pe.wait_ge(x_low, s + 1)
                        up(j, 0, A).then_inc(A_done, 1)

                    def product_D(n, j, s):
                        pe.wait_ge(a_low, n + 1)
                        pe.wait_ge(D_low, n + 1)
                        if j % 2 == 0 and not first(s, 1):
                            pe.wait_ge(y_read, s)
                        w = Ws[j % 2][:, :, DN].rearrange("p h (c d) -> p h c d", d=D)
                        for c, (c0, cw) in enumerate(cks):
                            mm = exact(ps[:, BY, 0:D], lambda i, k: aT[j % 2][0:cw, i, k, :], lambda i, k: w[0:cw, i, k, :],
                                       [c], start=j % 2 == 0 and c == 0, stop=j % 2 == 1 and c == len(cks) - 1)
                        mm.then_inc(D_done, 1)

                    def turn_a(n, j):
                        pe.wait_ge(act_ready, n + 1)
                        for c, (c0, cw) in enumerate(cks):
                            mm = pe.transpose(ps[0:cw, BT + j % 2, c * P:(c + 1) * P], act_[j % 2][:, c0:c0 + cw], self.ident)
                        mm.then_inc(a_turned, 1)

                    def turn_x(s, par):
                        pe.wait_ge(x_in[par], x_before(s, par) + 16)
                        for k in range(KC):
                            mm = pe.transpose(ps[:, BX, k * P:(k + 1) * P], xin[par][:, k * P:(k + 1) * P], self.ident)
                        mm.then_inc(x_turned, 1)

                    def unit(n, j, s):
                        product_G(n, j)
                        if j % 2 == 0 and exists(n + 2):
                            turn_x(s + 1, (j // 2 + 1) % 2)
                        if exists(n + 1):
                            product_A(n + 1, (j + 1) % 4, s + 1 if j % 2 else s)
                        if not first(n, 1):
                            product_D(n - 1, (j + 3) % 4, s if j % 2 else s - 1)
                        turn_a(n, j)

                    turn_x(0, 0)
                    product_A(0, 0, 0)
                    every(pe, unit)
                    product_D(units - 1, (units - 1) % 4, slots - 1)

                @block.scalar
                def _(act):
                    def high(n, j, ex, piece, sem):
                        if resident or piece is DN:
                            act.sem_inc(self.carried, 1)
                        act.copy(Ws[j % 2][:, 0, piece], raw(act, ex, j, piece)).then_inc(sem, 1)

                    def silu(n, j):
                        act.wait_ge(A_done, n + 1)
                        act.activation(act_[j % 2][:], ps[:, 2 * (j % 2), 0:half_w], ACT.Silu).then_inc(sil_ready, 1)

                    def high_a(n, j):
                        act.wait_ge(a_turned, n + 1)
                        if not first(n, 2):
                            act.wait_ge(D_done, n - 1)
                        full = len([1 for _, cw in cks if cw == P])
                        copied = act.copy(aT[j % 2][:, 0, 0:full, :],
                                          ps[:, BT + j % 2, 0:full * P].rearrange("p (c t) -> p c t", t=P))
                        if full < len(cks):
                            cw = cks[-1][1]
                            copied = act.copy(aT[j % 2][0:cw, 0, full, :], ps[0:cw, BT + j % 2, full * P:(full + 1) * P])
                        copied.then_inc(a_high, 1)

                    def high_x(s, par):
                        act.wait_ge(x_turned, s + 1)
                        act.copy(xT[par][:, 0], ps[:, BX, 0:D].rearrange("p (k t) -> p k t", k=KC)).then_inc(x_high, 1)

                    def unit(n, j, s):
                        ex = expert_of(act, s)
                        ex_next = expert_of(act, s + 1, resident and exists(n + 2))
                        if not first(n, 1):
                            high_a(n - 1, (j + 3) % 4)
                        if not first(n, 2):
                            act.wait_ge(D_done, n - 1)
                        high(n, j, ex, DN, D_high)
                        if exists(n + 2):
                            nxt = (j + 2) % 4
                            if resident:
                                act.wait_ge(w_in[0], ex_next * 16 + 16)
                            else:
                                act.wait_ge(w_in[nxt], (n - j) * 4 + (16 if j < 2 else 32))
                            act.wait_ge(A_done, n + 1)
                            high(n + 2, nxt, ex_next, A, A_high)
                            if j % 2 == 0:
                                high_x(s + 1, (j // 2 + 1) % 2)
                            act.wait_ge(G_done, n + 1)
                            high(n + 2, nxt, ex_next, G, G_high)
                        if exists(n + 1):
                            silu(n + 1, (j + 1) % 4)

                    ex = expert_of(act, 0, resident)
                    for n in range(2):
                        act.wait_ge(w_in[0 if resident else n], ex * 16 + 16 if resident else 16)
                        high(n, n, ex, A, A_high)
                        high(n, n, ex, G, G_high)
                        if n == 0:
                            high_x(0, 0)
                    silu(0, 0)
                    every(act, unit)
                    high_a(units - 1, (units - 1) % 4)

                @block.vector
                def _(e):
                    def low(j, ex, piece, sem):
                        e.tensor_tensor(Ws[j % 2][:, 1, piece], raw(e, ex, j, piece), Ws[j % 2][:, 0, piece].bitcast(F32),
                                        ALU.subtract).then_inc(sem, 1)

                    def low_x(s, par):
                        e.wait_ge(x_high, s + 1)
                        e.tensor_tensor(xT[par][:, 1], ps[:, BX, 0:D].rearrange("p (k t) -> p k t", k=KC),
                                        xT[par][:, 0].bitcast(F32), ALU.subtract).then_inc(x_low, 1)

                    def low_a(n, j):
                        e.wait_ge(a_high, n + 1)
                        full = len([1 for _, cw in cks if cw == P])
                        parts = [(P, slice(0, full), full)] + [(cw, slice(full, full + 1), 1) for _, cw in cks[full:]]
                        for cw, c, nc_ in parts:
                            sub = e.tensor_tensor(
                                aT[j % 2][0:cw, 1, c, :],
                                ps[0:cw, BT + j % 2, c.start * P:c.stop * P].rearrange("p (c t) -> p c t", t=P),
                                aT[j % 2][0:cw, 0, c, :].bitcast(F32), ALU.subtract)
                        sub.then_inc(a_low, 1)

                    def gate(n, j):
                        e.wait_ge(G_done, n + 1)
                        e.wait_ge(sil_ready, n + 1)
                        e.tensor_tensor(act_[j % 2][:], act_[j % 2][:], ps[:, 2 * (j % 2) + 1, 0:half_w],
                                        ALU.mult).then_inc(act_ready, 1)

                    def weighted_y(s, par):
                        e.wait_ge(D_done, s * 2 + 2)
                        if not first(s, NY):
                            e.wait_ge(y_out[par % NY], y_before(s, par))
                        e.tensor_scalar(y[par % NY][:], ps[:, BY, 0:D], self.slot_gate[:, bass.ds(s, 1)], None,
                                        ALU.mult).then_inc(y_read, 1)

                    def unit(n, j, s):
                        ex = expert_of(e, s + 1, resident and exists(n + 2))
                        if not first(n, 1):
                            low_a(n - 1, (j + 3) % 4)
                        gate(n, j)
                        if exists(n + 2):
                            e.wait_ge(A_high, n + 3)
                            low((j + 2) % 4, ex, A, A_low)
                            if j % 2 == 0:
                                low_x(s + 1, (j // 2 + 1) % 2)
                            e.wait_ge(G_high, n + 3)
                            low((j + 2) % 4, ex, G, G_low)
                        if j % 2 == 0 and not first(s, 1):
                            weighted_y(s - 1, (j // 2 + 1) % 2)

                    ex = expert_of(e, 0, resident)
                    for n in range(2):
                        e.wait_ge(A_high, n + 1)
                        low(n, ex, A, A_low)
                        e.wait_ge(G_high, n + 1)
                        low(n, ex, G, G_low)
                        if n == 0:
                            low_x(0, 0)
                    every(e, unit)
                    low_a(units - 1, (units - 1) % 4)
                    weighted_y(slots - 1, (slots - 1) % 2)

                @block.gpsimd
                def _(pool):
                    def gather(s, par):
                        if not first(s, 2):
                            pool.wait_ge(x_turned, s - 1)
                        pool.tensor_copy(from_tok[par][:], self.gather_idx[:, bass.ds(s, 1)]).then_inc(from_ready, 1)
                        pool.wait_ge(from_ready, s + 1)
                        pool.sem_inc(self.carried, 1)
                        pool.indirect_dma_start(xin[par][:], None, self.normed[layer],
                                                bass.IndirectOffsetOnAxis(ap=from_tok[par][:], axis=0)).then_inc(x_in[par], 16)

                    def scatter(s, par):
                        u = par % NY
                        pool.wait_ge(y_read, s + 1)
                        pool.tensor_copy(to_row[u][:], self.scatter_idx[:, bass.ds(s, 1)]).then_inc(to_ready, 1)
                        pool.wait_ge(to_ready, s + 1)
                        pool.sem_inc(self.carried, 1)
                        pool.indirect_dma_start(self.made[layer], bass.IndirectOffsetOnAxis(ap=to_row[u][:], axis=0),
                                                y[u][:], None).then_inc(y_out[u], 16)

                    def unit(n, j, s):
                        ex = expert_of(pool, s)
                        if j % 2 == 0 and exists(n + 2):
                            gather(s + 2, j // 2)
                        if j % 2 == 1 and not first(s, 1):
                            scatter(s - 1, (j // 2 + 1) % 2)
                        pool.wait_ge(D_high, n + 1)
                        pool.sem_inc(self.carried, 1)
                        pool.tensor_tensor(Ws[j % 2][:, 1, DN], raw(pool, ex, j, DN), Ws[j % 2][:, 0, DN].bitcast(F32),
                                           ALU.subtract).then_inc(D_low, 1)

                    gather(0, 0)
                    gather(1, 1)
                    every(pool, unit)
                    scatter(slots - 1, (slots - 1) % 2)
                    for u in range(NY):
                        pool.wait_ge(y_out[u], 16 * len(range(u, slots, NY)))
                    pool.wait_ge(x_in[slots % 2], 16 * (slots // 2 + 1))

    def add_outputs(self, e, m, top, Z, s_z, s_new):
        t, n = m // top, m % top
        e.wait_ge(s_z[t // 4], 16 * top)
        if n:
            e.wait_ge(s_new, m)
        e.tensor_tensor(self.X[:, t, :], self.X[:, t, :], Z[n][:, t, :], ALU.add).then_inc(s_new, 1)

    def load_outputs(self, sp, layer, top, Z, s_z):
        for g in range(T // 4):
            for n in range(top):
                src = self.made[layer][n * T * P:(n + 1) * T * P, :].rearrange("(t p) d -> p t d", p=P)
                sp.dma_start(Z[n][:, 4 * g:4 * g + 4, :], src[:, 4 * g:4 * g + 4, :]).then_inc(s_z[g], 16)

    def kv_buffers(self, ctx, name):
        self.kv_name = name
        self.kv_val = ctx.enter_context(self.nc.sbuf_tensor(name + "_val", [P, B, KC, S], F32))
        self.kv_high = ctx.enter_context(self.nc.sbuf_tensor(name + "_high", [P, B, KC, S], F32R))
        (self.kv_c, self.kv_norm, self.kv_turned, self.kv_tile, self.kv_h, self.kv_l, self.kv_out) = (
            self.sem(name + "_" + n) for n in ("c", "norm", "turned", "tile", "high", "low", "out"))

    def kv_turn(self, pe, src):
        for m in range(T):
            pe.wait_ge(self.kv_norm, m + 1)
            if m >= 4:
                pe.wait_ge(self.kv_tile, m - 3)
            for k in range(KC):
                mm = pe.transpose(self.ps[:, m % 4, k * P:(k + 1) * P], src[:, m, k * P:(k + 1) * P], self.ident)
            mm.then_inc(self.kv_turned, 1)

    def kv_affine(self, act, latent):
        for m in range(T):
            b, j = m // TB, m % TB
            act.wait_ge(self.kv_turned, m + 1)
            for k in range(KC):
                last = act.activation(self.kv_val[:, b, k, j * P:(j + 1) * P], self.ps[:, m % 4, k * P:(k + 1) * P],
                                      ACT.Identity, bias=self.lnw[:, 2 * latent + 1, k:k + 1],
                                      scale=self.lnw[:, 2 * latent, k:k + 1])
            last.then_inc(self.kv_tile, 1)
            if j == TB - 1:
                act.wait_ge(self.kv_tile, m + 1)
                act.copy(self.kv_high[:, b], self.kv_val[:, b]).then_inc(self.kv_h, 1)

    def kv_low(self, e):
        for b in range(B):
            e.wait_ge(self.kv_h, b + 1)
            e.tensor_tensor(self.kv_val[:, b].bitcast(F32R), self.kv_val[:, b], self.kv_high[:, b].bitcast(F32),
                            ALU.subtract).then_inc(self.kv_l, 1)

    def kv_store(self, sp, latent):
        half = slice(latent * S, (latent + 1) * S)
        for b in range(B):
            sp.wait_ge(self.kv_l, b + 1)
            sp.dma_start(self.kv_dram[b][:, 0, :, half], self.kv_high[:, b].bitcast(F32)).then_inc(self.kv_out, 16)
            sp.dma_start(self.kv_dram[b][:, 1, :, half], self.kv_val[:, b]).then_inc(self.kv_out, 16)
        sp.wait_ge(self.kv_out, 32 * B)

    def finish(self):
        nc, X, top = self.nc, self.X, 2
        with ExitStack() as ctx:
            Z = [ctx.enter_context(nc.sbuf_tensor(f"f_Z{n}", [P, T, D], F32)) for n in range(top)]
            s_z = [self.sem(f"f_z{g}") for g in range(T // 4)]
            s_new, s_out = self.sem("f_new"), self.sem("f_out")
            with nc.Block() as block:
                @block.vector
                def _(e):
                    for m in range(T * top):
                        self.add_outputs(e, m, top, Z, s_z, s_new)

                @block.sync
                def _(sp):
                    self.load_outputs(sp, 1, top, Z, s_z)
                    out = self.out.rearrange("(t p) d -> p t d", p=P)
                    for t in range(0, T, 4):
                        sp.wait_ge(s_new, (t + 4) * top)
                        sp.dma_start(out[:, t:t + 4, :], X[:, t:t + 4, :]).then_inc(s_out, 16)
                    sp.wait_ge(s_out, 16 * (T // 4))

    def latents(self):
        nc, ins, X, ps = self.nc, self.ins, self.X, self.ps
        with ExitStack() as ctx:
            sb = lambda name, shape, dt=F32: ctx.enter_context(nc.sbuf_tensor(name, shape, dt))
            Z = sb("l_Z", [P, T, D])
            XN = sb("l_XN", [P, T, D])
            W_raw = sb("l_W", [P, 3, KC, INNER])
            self.kv_buffers(ctx, "latent")
            s_z = [self.sem(f"l_z{g}") for g in range(T // 4)]
            s_new, s_w, w_high = self.sem("l_new"), self.sem("l_w"), self.sem("l_w_high")
            with nc.Block() as block:
                @block.sync
                def _(sp):
                    self.load_outputs(sp, 0, 1, [Z], s_z)
                    sp.dma_start(W_raw[:], ins["Wvkq1"]).then_inc(s_w, 16)
                    self.kv_store(sp, 1)

                @block.vector
                def _(e):
                    link = Chain(e, self.chain)
                    for t in range(T):
                        self.add_outputs(e, t, 1, [Z], s_z, s_new)
                    e.wait_ge(s_new, T)
                    self.ln_stats(e, X, link)
                    for t in range(T - 1):
                        self.normalise(e, XN[:, t, :], X[:, t, :], t)
                    link(self.normalise(e, XN[:, T - 1, :], X[:, T - 1, :], T - 1))
                    self.ln_stats(e, XN, link)
                    for t in range(T):
                        self.normalise(e, Z[:, t, :], XN[:, t, :], t).then_inc(self.kv_norm, 1)
                    for w in range(3):
                        e.wait_ge(w_high, w + 1)
                        e.tensor_tensor(self.W_att[:, 1, w], W_raw[:, w], self.W_att[:, 0, w].bitcast(F32), ALU.subtract)
                    self.kv_low(e)

                @block.tensor
                def _(pe):
                    self.kv_turn(pe, Z)

                @block.scalar
                def _(act):
                    act.wait_ge(s_w, 16)
                    for w in range(3):
                        act.copy(self.W_att[:, 0, w], W_raw[:, w]).then_inc(w_high, 1)
                    self.ln_sqrt(act)
                    self.ln_sqrt(act)
                    self.kv_affine(act, 1)

    def perceiver(self):
        nc, ins, X, ps = self.nc, self.ins, self.X, self.ps
        STEPS = H * TB
        with ExitStack() as ctx:
            sb = lambda name, shape, dt=F32: ctx.enter_context(nc.sbuf_tensor("p_" + name, shape, dt))
            kv = sb("kv", [P, 2, KC, KEYS], F32R)
            W = self.W_att
            WV, WK, WQ = range(3)
            Wo = sb("Wo", [P, H, D])
            V2 = sb("V2", [P, KT, H, P], F32R)
            kHL = sb("kHL", [P, 2, KEYS], F32R)
            qHL = sb("qHL", [P, 2, S], F32R)
            K2 = [[sb(f"K2{i}{j}", [P, KEYS], F32R) for j in range(2)] for i in range(2)]
            Q2 = [[sb(f"Q2{i}{j}", [P, 2, S], F32R) for j in range(2)] for i in range(2)]
            Pr = [sb(f"Pr{i}", [P, KEYS]) for i in range(3)]
            Ph = [sb(f"Ph{i}", [P, KT, 2 * P], F32R) for i in range(2)]
            Pl = [sb(f"Pl{i}", [P, KT, 2 * P], F32R) for i in range(2)]
            AT = sb("AT", [P, H, S])
            nmax = sb("nmax", [P, STEPS])
            den = sb("den", [P, STEPS])
            rden = sb("rden", [P, STEPS])
            names = ("kv_in", "proj", "proj_h", "proj_l", "v_ps", "v_h", "v_l", "s_ps", "max",
                     "exp", "rden", "norm", "turn", "ph", "pl", "o_ps", "o_sb", "y_ps", "y_add")
            (s_kv, proj, proj_h, proj_l, v_ps, v_h, v_l, s_ps, s_max, s_exp, s_rden, s_norm,
             s_turn, s_ph, s_pl, o_ps, o_sb, y_ps, y_add) = (self.sem("p_" + n) for n in names)
            kq_in = [self.sem(f"p_kq_in{i}") for i in range(2)]
            s_wo = self.sem("p_wo")
            BO, BP, BTA = 6, 7, 4
            HP = H // 2
            PROJ = 3 * HP
            KQ = 8 * 16
            TURN = 2 * STEPS
            DOUBLES = STEPS // 2
            project_at = {8 * p + 2 * i: 3 * (p + 1) + i for p in range(HP - 1) for i in range(3)}

            with nc.Block() as block:
                @block.sync
                def _(sp):
                    sp.dma_start(kv[:].bitcast(F32), self.kv_dram[0]).then_inc(s_kv, 16)
                    sp.dma_start(Wo[:], ins["Wo1"]).then_inc(s_wo, 16)

                    def stack(b):
                        for p in range(HP):
                            arrived = kq_in[p % 2]
                            sp.wait_ge(proj_l, b * PROJ + 3 * p + 3)
                            for j in range(2):
                                for part in range(2):
                                    half = (part + j) % 2
                                    sp.dma_start(K2[p % 2][j][half * DH:(half + 1) * DH, :].bitcast(F32),
                                                 kHL[j * DH:(j + 1) * DH, part, :].bitcast(F32)).then_inc(arrived, 16)
                            sp.wait_ge(proj_l, b * PROJ + 3 * p + 4)
                            for j in range(2):
                                for half in range(2):
                                    sp.dma_start(Q2[p % 2][j][half * DH:(half + 1) * DH, :, :].bitcast(F32),
                                                 qHL[j * DH:(j + 1) * DH, :, :].bitcast(F32)).then_inc(arrived, 16)

                    with sp.Fori(0, B - 1) as b:
                        stack(b)
                        sp.dma_start(kv[:].bitcast(F32), self.kv_dram[bass.ds(b + 1, 1)].rearrange(
                            "a p h k n -> p (a h) k n")).then_inc(s_kv, 16)
                    stack(B - 1)

                @block.tensor
                def _(pe):
                    def exact(out, lhs, rhs):
                        parts = [(i, j, k) for i, j in ((0, 0), (0, 1), (1, 0)) for k in range(KC)]
                        for n, (i, j, k) in enumerate(parts):
                            mm = pe.matmul(out, lhs(i, k), rhs(j, k), start=n == 0, stop=n == len(parts) - 1)
                        return mm

                    def project(b, m):
                        p, part = m // 3, m % 3
                        w, a = (WQ, S) if part == 2 else (WK, part * S)
                        pe.wait_ge(proj_l, b * PROJ + m + 1)
                        exact(ps[:, BP, :], lambda i, k: W[:, i, w, k, p * P:(p + 1) * P],
                              lambda j, k: kv[:, j, k, a:a + S]).then_inc(proj, 1)

                    def scores(b, t):
                        h, q = t // TB, t % TB
                        p, j = h // 2, h % 2
                        if t % (2 * TB) == 0:
                            pe.wait_ge(kq_in[p % 2], b * (HP // 2 * KQ) + (p // 2 + 1) * KQ)
                        if t >= 2:
                            pe.wait_ge(s_exp, b * STEPS + t - 1)
                        for c in range(2):
                            for part in range(2):
                                mm = pe.matmul(ps[:, 2 * (t % 2) + c, :], Q2[p % 2][j][:, part, q * P:(q + 1) * P],
                                               K2[p % 2][j][:, c * 512:(c + 1) * 512], start=part == 0, stop=part == 1)
                        mm.then_inc(s_ps, 1)

                    def turn(b, t):
                        pe.wait_ge(s_norm, b * STEPS + t + 1)
                        for g in range(2):
                            pe.wait_ge(s_pl, b * TURN + 2 * t + g + 1)
                            for c in range(4):
                                mm = pe.transpose(ps[:, BTA + g, c * P:(c + 1) * P],
                                                  Pr[t % 3][:, (4 * g + c) * P:(4 * g + c + 1) * P], self.ident)
                            mm.then_inc(s_turn, 1)

                    def attend(b, d):
                        h = d // 2
                        pe.wait_ge(s_pl, b * TURN + 4 * d + 6)
                        pe.wait_ge(o_sb, b * DOUBLES + d + 1)
                        for c in range(KT):
                            for n, A in enumerate((Ph, Pl)):
                                mm = pe.matmul(ps[:, BO, 0:2 * P], V2[:, c, h, :], A[d % 2][:, c, :],
                                               start=c == 0 and n == 0, stop=c == KT - 1 and n == 1)
                        mm.then_inc(o_ps, 1)

                    pe.wait_ge(s_wo, 16)
                    with pe.Fori(0, B) as b:
                        pe.wait_ge(s_kv, b * 16 + 16)
                        pe.wait_ge(y_add, b * TB + 1)
                        for c in range(KT):
                            if c >= 4:
                                pe.wait_ge(v_l, b * KT + c - 3)
                            exact(ps[:, c % 4, :], lambda i, k: kv[:, i, k, c * P:(c + 1) * P],
                                  lambda j, k: W[:, j, WV, k, :]).then_inc(v_ps, 1)
                            if c < 3:
                                project(b, c)
                        pe.wait_ge(v_l, b * KT + KT)
                        for t in range(STEPS + 4):
                            if t < STEPS:
                                scores(b, t)
                            if t in project_at:
                                project(b, project_at[t])
                            if 2 <= t < STEPS + 2:
                                turn(b, t - 2)
                            if t >= 4 and t % 2 == 0:
                                attend(b, (t - 4) // 2)
                        pe.wait_ge(o_sb, b * DOUBLES + DOUBLES + 1)
                        for q in range(TB):
                            for h in range(H):
                                mm = pe.matmul(ps[:, q, 0:D], AT[:, h, q * P:(q + 1) * P], Wo[:, h, :],
                                               start=h == 0, stop=h == H - 1)
                            mm.then_inc(y_ps, 1)

                @block.scalar
                def _(act):
                    def split_high(b, m):
                        act.wait_ge(proj, b * PROJ + m + 1)
                        if m % 3 == 2:
                            act.mul(qHL[:, 0, :], ps[:, BP, :], DH ** -0.5).then_inc(proj_h, 1)
                        else:
                            act.copy(kHL[:, 0, m % 3 * S:(m % 3 + 1) * S], ps[:, BP, :]).then_inc(proj_h, 1)

                    def softmax_exp(b, t):
                        act.wait_ge(s_max, b * STEPS + t + 1)
                        if t >= 3:
                            act.wait_ge(s_turn, b * TURN + 2 * (t - 2))
                        act.activation(Pr[t % 3][:], self.bank(2 * (t % 2), 2), ACT.Exp, bias=nmax[:, t:t + 1],
                                       scale=1.0, accum_out=den[:, t:t + 1]).then_inc(s_exp, 1)

                    def turned_high(b, t):
                        for g in range(2):
                            act.wait_ge(s_turn, b * TURN + 2 * t + g + 1)
                            if t >= 4 and t % 2 == 0 and g == 0:
                                act.wait_ge(o_ps, b * DOUBLES + t // 2 - 1)
                            act.copy(Ph[(t // 2) % 2][:, 4 * g:4 * g + 4, (t % 2) * P:(t % 2 + 1) * P],
                                     ps[:, BTA + g, :].rearrange("p (c q) -> p c q", q=P)).then_inc(s_ph, 1)

                    with act.Fori(0, B) as b:
                        act.wait_ge(o_sb, b * DOUBLES + 1)
                        act.wait_ge(y_add, b * TB + 1)
                        for c in range(KT):
                            act.wait_ge(v_ps, b * KT + c + 1)
                            act.copy(V2[:, c, :, 0:DH], ps[:, c % 4, :].rearrange("p (h d) -> p h d", d=DH)).then_inc(v_h, 1)
                            if c < 3:
                                split_high(b, c)
                        for t in range(STEPS + 2):
                            if t >= 2:
                                turned_high(b, t - 2)
                            if t < STEPS:
                                softmax_exp(b, t)
                            if t in project_at:
                                split_high(b, project_at[t])

                @block.vector
                def _(e):
                    def split_low(b, m):
                        e.wait_ge(proj_h, b * PROJ + m + 1)
                        if m % 3 == 2:
                            e.scalar_tensor_tensor(qHL[:, 1, :], ps[:, BP, :], DH ** -0.5, qHL[:, 0, :].bitcast(F32),
                                                   ALU.mult, ALU.subtract).then_inc(proj_l, 1)
                        else:
                            half = slice(m % 3 * S, (m % 3 + 1) * S)
                            e.tensor_tensor(kHL[:, 1, half], ps[:, BP, :], kHL[:, 0, half].bitcast(F32),
                                            ALU.subtract).then_inc(proj_l, 1)

                    def row_max(b, t):
                        e.wait_ge(s_ps, b * STEPS + t + 1)
                        e.tensor_reduce(nmax[:, t:t + 1], self.bank(2 * (t % 2), 2), AX, ALU.max,
                                        negate=True).then_inc(s_max, 1)

                    def inverse(b, t):
                        e.wait_ge(s_exp, b * STEPS + t + 1)
                        e.reciprocal(rden[:, t:t + 1], den[:, t:t + 1]).then_inc(s_rden, 1)

                    def turned_low(b, t):
                        for g in range(2):
                            e.wait_ge(s_ph, b * TURN + 2 * t + g + 1)
                            if t >= 4 and t % 2 == 0 and g == 0:
                                e.wait_ge(o_ps, b * DOUBLES + t // 2 - 1)
                            dst = (slice(None), slice(4 * g, 4 * g + 4), slice((t % 2) * P, (t % 2 + 1) * P))
                            e.tensor_tensor(Pl[(t // 2) % 2][dst], ps[:, BTA + g, :].rearrange("p (c q) -> p c q", q=P),
                                            Ph[(t // 2) % 2][dst].bitcast(F32), ALU.subtract).then_inc(s_pl, 1)

                    def copy_o(b, d):
                        h, q = d // 2, d % 2
                        e.wait_ge(o_ps, b * DOUBLES + d + 1)
                        e.tensor_copy(AT[:, h, q * 2 * P:(q + 1) * 2 * P], ps[:, BO, 0:2 * P]).then_inc(o_sb, 1)

                    e.sem_inc(proj_l, 1)
                    e.sem_inc(s_pl, 2)
                    e.sem_inc(o_sb, 1)
                    e.sem_inc(y_add, 1)
                    with e.Fori(0, B) as b:
                        for c in range(KT):
                            e.wait_ge(v_h, b * KT + c + 1)
                            e.tensor_tensor(V2[:, c, :, DH:P], ps[:, c % 4, :].rearrange("p (h d) -> p h d", d=DH),
                                            V2[:, c, :, 0:DH].bitcast(F32), ALU.subtract).then_inc(v_l, 1)
                            if c < 3:
                                split_low(b, c)
                        for t in range(STEPS + 4):
                            if 1 <= t < STEPS + 1:
                                inverse(b, t - 1)
                            if t < STEPS:
                                row_max(b, t)
                            if 2 <= t < STEPS + 2:
                                turned_low(b, t - 2)
                            if t in project_at:
                                split_low(b, project_at[t])
                            if t >= 5 and t % 2 == 1:
                                copy_o(b, (t - 5) // 2)
                        for q in range(TB):
                            e.wait_ge(y_ps, b * TB + q + 1)
                            x = X[:, bass.ds(b * TB + q, 1), :].rearrange("p a d -> p (a d)")
                            e.scalar_tensor_tensor(x, ps[:, q, 0:D], self.tg[:, 1:2], x, ALU.mult, ALU.add).then_inc(y_add, 1)

                @block.gpsimd
                def _(pool):
                    with pool.Fori(0, B) as b:
                        for t in range(STEPS):
                            pool.wait_ge(s_rden, b * STEPS + t + 1)
                            pool.tensor_tensor(Pr[t % 3][:], Pr[t % 3][:], rden[:, t:t + 1].broadcast_to([P, KEYS]),
                                               ALU.mult).then_inc(s_norm, 1)


def build(nc, ins, out, stop=99):
    with ExitStack() as ctx:
        p = Program(nc, ins, out, ctx)
        def layer_0_ffn():
            with ExitStack() as inner:
                p.W_down = inner.enter_context(nc.sbuf_tensor("W_down", [P, 2 * E, F0 // 2 // P * D], F32))
                p.route(0, 1, SLOTS0)
                p.experts(0, SLOTS0, F0 // 2)

        def layer_1_ffn():
            with ExitStack() as inner:
                half_w = F1_PAD // 2
                p.W_all = inner.enter_context(nc.sbuf_tensor(
                    "W_all", [P, 2 * E, 2 * KC * half_w + len(chunks(half_w)) * D], F32))
                p.w1_in = p.sem("w1_in")
                p.route(1, 2, SLOTS1)
                p.experts(1, SLOTS1, half_w)

        def attention():
            with ExitStack() as inner:
                p.W_att = inner.enter_context(nc.sbuf_tensor("W_att", [P, 2, 3, KC, INNER], F32R))
                p.latents()
                p.perceiver()

        stages = [
            p.retention,
            lambda: None,
            layer_0_ffn,
            lambda: None,
            attention,
            lambda: None,
            layer_1_ffn,
            p.finish,
        ]
        for stage in stages[:stop]:
            stage()
        if stop < len(stages):
            s = p.sem("dbg")
            with nc.Block() as block:
                @block.sync
                def _(sp):
                    sp.dma_start(out.rearrange("(t p) d -> p t d", p=P), p.X[:]).then_inc(s, 16)
                    sp.wait_ge(s, 16)


def laid_out(inputs):
    a = {k: np.asarray(v) for k, v in inputs.items()}
    split = np.concatenate([np.arange(0, D, 2), np.arange(1, D, 2)])

    def packed(up, down, f):
        hw = f // 2
        nck = len(chunks(hw))
        u = up.reshape(E, KC, P, 2, 2, hw).transpose(0, 4, 2, 3, 1, 5).reshape(E, 2, P, 2 * KC * hw)
        d = down.reshape(E, 2, hw, D)
        d = np.concatenate([d, np.zeros((E, 2, nck * P - hw, D), d.dtype)], 2)
        d = d.reshape(E, 2, nck, P, D).transpose(0, 1, 3, 2, 4).reshape(E, 2, P, nck * D)
        return np.concatenate([u, d], 3).reshape(2 * E, P, -1)

    w1 = a["L0_ffn_w1"].reshape(E, D, 2, F0)
    up1 = np.stack([a["L1_ffn_W1"].transpose(0, 2, 1), a["L1_ffn_W2"].transpose(0, 2, 1)], 2)
    pad = F1_PAD - F1
    up1 = np.pad(up1, ((0, 0), (0, 0), (0, 0), (0, pad)))
    down1 = np.pad(a["L1_ffn_W3"].transpose(0, 2, 1), ((0, 0), (0, pad), (0, 0)))
    ln = [a[f"L1_xattn_ln_{n}"].reshape(KC, P).T for n in ("media_w", "media_b", "lat_w", "lat_b")]
    out = {
        "x": a["x"].reshape(B * S, D),
        "ctx": a["ctx_1024"].reshape(B * S, D),
        "ctxT": a["ctx_1024"].reshape(B * S, D).T,
        "g_xattn": a["g_xattn"], "g_ffn": a["g_ffn"],
        "const": shape_constants(), "tab": xpos_tables(),
        "lnw": np.stack(ln, 1),
        "Wq0": a["L0_xattn_Wq"][split].T, "Wk0": a["L0_xattn_Wk"][split].T, "Wv0": a["L0_xattn_Wv"].T,
        "rw0": a["L0_ffn_router_w"], "rb0": a["L0_ffn_router_b"],
        "We0": packed(w1, a["L0_ffn_w2"], F0),
        "Wvkq1": np.stack([a[f"L1_xattn_W{n}"].reshape(KC, P, INNER) for n in "vkq"]).transpose(2, 0, 1, 3),
        "Wo1": np.repeat(a["L1_xattn_Wout"].reshape(H, 1, DH, D), 2, axis=1).reshape(H, P, D).transpose(1, 0, 2),
        "rw1": a["L1_ffn_Wg"].T,
        "We1": packed(up1, down1, F1_PAD),
    }
    return {k: np.ascontiguousarray(v) for k, v in out.items()}


def kernel(**inputs):
    import concourse.bacc as bacc
    from concourse.bass_utils import run_bass_kernel_spmd

    nc = bacc.Bacc("TRN2", target_bir_lowering=False, num_devices=1)
    arrays, ins = {}, {}
    for name, a in laid_out(inputs).items():
        arrays[f"in_{name}"] = a
        ins[name] = nc.dram_tensor(f"in_{name}", a.shape, mybir.dt.from_np(a.dtype), kind="ExternalInput").ap()
    out = nc.dram_tensor("out", (B * S, D), F32, kind="ExternalOutput").ap()
    build(nc, ins, out)
    r = run_bass_kernel_spmd(nc, [arrays], core_ids=[0])
    return r.results[0]["out"].reshape(B, S, D)
```

```python
from contextlib import ExitStack

import numpy as np

import concourse.bass as bass
from concourse import mybir

F32 = mybir.dt.float32
F32R = mybir.dt.float32r
I32 = mybir.dt.int32
ALU = mybir.AluOpType
ACT = mybir.ActivationFunctionType
AX = mybir.AxisListType.X

P = 128
B, S, D = 4, 512, 256
KC = D // P
T = B * S // P
TB = S // P
E = 8
F0, F1 = 1024, 682
F1_PAD = 684
H, DH = 8, 64
INNER = H * DH
KEYS = 2 * S
KT = KEYS // P
EPS = 1e-5
BIG = 3.0e38
EARLY = 5
SLOTS0 = T + E - 1
SLOTS1 = 2 * T + E - 1


def chunks(width):
    return [(c, min(P, width - c)) for c in range(0, width, P)]


WIDTHS = {"ident": P, "tri": P, "causal": P, "ones": P, "iota": P, "rev": T * E, "slot": 64, "token": T, "pad": 64}
COL = dict(zip(WIDTHS, np.cumsum([0, *WIDTHS.values()])))
C_END = sum(WIDTHS.values())


def shape_constants():
    k, m = np.arange(P)[:, None], np.arange(P)[None, :]
    parts = {
        "ident": k == m, "tri": k < m, "causal": m >= k, "ones": np.ones((P, P)), "iota": m + 0 * k,
        "rev": np.tile(E - np.arange(E), T)[None] + 0 * k, "slot": np.arange(64)[None] + 0 * k,
        "token": np.arange(T)[None] * P + k, "pad": np.arange(64)[None] * P + k,
    }
    return np.concatenate([parts[n].astype(np.float32) for n in WIDTHS], 1)


def xpos_tables():
    f = np.float32
    base = (np.arange(0, D, 2, dtype=f) + f(0.4 * D)) / f(1.4 * D)
    pos = np.arange(S, dtype=f)
    freqs = f(1.0) / f(10000.0) ** (np.arange(D // 2, dtype=f) / f(D // 2))
    angle = (pos[:, None] * freqs[None, :]).astype(np.float64)
    scale = base[None, :].astype(np.float64) ** (pos[:, None] / 512.0)
    gamma = 0.96875 ** pos.astype(np.float64)[:, None]
    cos, sin = np.cos(angle), np.sin(angle)
    t = [cos * scale * gamma, sin * scale * gamma, cos / scale / gamma, sin / scale / gamma]
    return np.ascontiguousarray(np.stack([a.T for a in t], 1).astype(f))


class Count:

    def __init__(self, sem):
        self.sem, self.n = sem, 0


class Chain:

    def __init__(self, eng, count):
        self.eng, self.count = eng, count

    def __call__(self, ins):
        ins.then_inc(self.count.sem, 1)
        self.count.n += 1
        self.eng.wait_ge(self.count.sem, self.count.n)


class Program:
    def __init__(self, nc, ins, out, ctx):
        self.nc, self.ins, self.out = nc, ins, out
        sb = lambda name, shape, dt=F32: ctx.enter_context(nc.sbuf_tensor(name, shape, dt))
        self.X = sb("X", [P, T, D])
        self.const = sb("const", [P, C_END])
        self.gates = sb("gates", [P, 4])
        self.tg = sb("tg", [P, 4])
        self.lnw = sb("lnw", [P, 4, KC])
        self.gather_idx = sb("gather_idx", [P, 64], I32)
        self.scatter_idx = sb("scatter_idx", [P, 64], I32)
        self.slot_gate = sb("slot_gate", [P, 64])
        self.slot_expert = sb("slot_expert", [P, 64], I32)
        self.stats = sb("stats", [P, T, 6])
        self.ln_tmp = sb("ln_tmp", [P, 4, T])
        self.mean = sb("mean", [P, T])
        self.rstd = sb("rstd", [P, T])
        self.std = sb("std", [P, T])
        self.ps = ctx.enter_context(nc.psum_tensor("ps", [P, 8, 512], F32))
        self.ident = self.const_of("ident")
        dram = lambda name, shape, dt=F32: nc.dram_tensor(name, shape, dt, kind="Internal").ap()
        self.normed = [dram("normed0", (T * P, D)), dram("normed1", (T * P, D))]
        self.made = dram("made0", (T * P + SLOTS0 * P, D))
        self.total = dram("total", (T * P + P, D))
        self.kv_dram = dram("kv_t", (B, P, 2, KC, KEYS))
        self.ctx = ctx
        self.carried = self.sem("carried")
        self.chain, self.ln_stat, self.ln_std = Count(self.sem("chain")), Count(self.sem("ln_stat")), Count(self.sem("ln_std"))
        self.ln_var, self.ln_passes = self.sem("ln_var"), 0

    def sem(self, name):
        return self.ctx.enter_context(self.nc.semaphore(name))

    def const_of(self, name):
        return self.const[:, COL[name]:COL[name] + WIDTHS[name]]

    def bank(self, i, n=1):
        return self.ps[:, i, :] if n == 1 else self.ps[:, i:i + n, :].rearrange("p b c -> p (b c)")

    def ln_tiles(self, e, src, tiles):
        for t in tiles:
            e.bn_stats(self.stats[:, t, :], src[:, t, :]).then_inc(self.ln_stat.sem, 1)
            self.ln_stat.n += 1

    def ln_stats(self, e, src, link):
        if src is not None:
            self.ln_tiles(e, src, range(T))
        e.wait_ge(self.ln_stat.sem, self.ln_stat.n)
        m_even, m_odd = self.stats[:, :, 1], self.stats[:, :, 4]
        v_even, v_odd = self.stats[:, :, 2], self.stats[:, :, 5]
        total, diff, diff2, var = (self.ln_tmp[:, i, :] for i in range(4))
        link(e.tensor_tensor(total, m_even, m_odd, ALU.add))
        link(e.tensor_tensor(diff, m_even, m_odd, ALU.subtract))
        link(e.scalar_tensor_tensor(diff2, diff, 0.25, diff, ALU.mult, ALU.mult))
        link(e.tensor_tensor(var, v_even, v_odd, ALU.add))
        link(e.tensor_scalar(self.mean[:], total, 0.5, None, ALU.mult))
        link(e.scalar_tensor_tensor(total, var, 1.0 / D, diff2, ALU.mult, ALU.add))
        link(e.tensor_scalar(var, total, EPS, None, ALU.add))
        e.sem_inc(self.ln_var, 1)
        self.ln_passes += 1
        e.wait_ge(self.ln_std.sem, self.ln_passes)
        link(e.reciprocal(self.rstd[:], self.std[:]))

    def ln_sqrt(self, act):
        self.ln_std.n += 1
        act.wait_ge(self.ln_var, self.ln_std.n)
        act.activation(self.std[:], self.ln_tmp[:, 3, :], ACT.Sqrt).then_inc(self.ln_std.sem, 1)

    def normalise(self, e, out, src, t):
        return e.tensor_scalar(out, src, self.mean[:, t:t + 1], self.rstd[:, t:t + 1],
                               ALU.subtract, ALU.mult)

    def retention(self):
        nc, ins, X, ps = self.nc, self.ins, self.X, self.ps
        with ExitStack() as ctx:
            sb = lambda name, shape: ctx.enter_context(nc.sbuf_tensor(name, shape, F32))
            XN = self.W_down[:].rearrange("p e c -> p (e c)")[:, 0:T * D].rearrange("p (t d) -> p t d", d=D)
            XT = sb("r_XT", [P, KC, T * P])
            CT = sb("r_CT", [P, KC, T * P])
            tab = sb("r_tab", [P, 4, S])
            Wq = sb("r_Wq", [P, KC, D])
            Wk = sb("r_Wk", [P, KC, D])
            Wv = sb("r_Wv", [P, KC, D])
            tmp = sb("r_tmp", [P, 4, S])
            qR = [sb(f"r_qR{i}", [P, 2, S]) for i in range(2)]
            kR = [sb(f"r_kR{i}", [P, 2, S]) for i in range(B)]
            V = sb("r_V", [P, T, D])
            ST = sb("r_ST", [P, TB, S])
            ct_in = [self.sem(f"r_ct{i}") for i in range(3)]
            names = ("x", "c", "wkv", "wq", "tab", "g", "norm", "turned", "xt", "q_ps", "k_ps", "v_ps", "q_rot",
                     "k_rot", "v_sb", "s_ps", "diag", "rest", "o_ps", "x_new")
            (s_x, s_c, s_wkv, s_wq, s_tab, s_g, s_norm, s_turned, s_xt, q_ps, k_ps, v_ps, q_rot,
             k_rot, v_sb, s_ps, diag, rest, o_ps, x_new) = (self.sem("r_" + n) for n in names)
            BV, BTX, BO = 4, 4, 6
            BQ = [6, 4, 4, 4]

            with nc.Block() as block:
                @block.sync
                def _(sp):
                    load_w = lambda w, name, sem: sp.dma_start(
                        w[:], ins[name].rearrange("(k p) n -> p k n", p=P)).then_inc(sem, 16)
                    load_w(Wk, "Wk0", s_wkv)
                    load_w(Wv, "Wv0", s_wkv)
                    ctx_t = ins["ctxT"].rearrange("(k p) n -> p k n", p=P)
                    for b in range(2):
                        cols = slice(b * S, (b + 1) * S)
                        sp.dma_start(CT[:, :, cols], ctx_t[:, :, cols]).then_inc(ct_in[b], 16)
                    sp.dma_start(X[:], ins["x"].rearrange("(t p) d -> p t d", p=P)).then_inc(s_x, 16)
                    sp.dma_start(CT[:, :, 2 * S:], ctx_t[:, :, 2 * S:]).then_inc(ct_in[2], 16)
                    sp.dma_start(tab[:], ins["tab"]).then_inc(s_tab, 16)
                    sp.dma_start(self.const[:], ins["const"]).then_inc(s_c, 16)
                    load_w(Wq, "Wq0", s_wq)
                    sp.dma_start(self.C[:], ins["ctx"].rearrange("(t p) d -> p t d", p=P)).then_inc(self.s_ahead, 16)
                    sp.wait_ge(s_turned, T)
                    sp.dma_start(self.W_down[:], ins["We0"][:, :, 2 * KC * (F0 // 2):].rearrange("a p c -> p a c")
                                 ).then_inc(self.s_ahead, 16)
                    sp.wait_ge(self.s_ahead, 32)

                @block.tensor
                def _(pe):
                    def project_kv(b):
                        pe.wait_ge(ct_in[min(b, 2)], 16)
                        if b >= 2:
                            pe.wait_ge(k_rot, b - 1)
                        for half in range(2):
                            for k in range(KC):
                                mm = pe.matmul(ps[:, 2 * (b % 2) + half, :], Wk[:, k, half * P:(half + 1) * P],
                                               CT[:, k, b * S:(b + 1) * S], start=k == 0, stop=k == KC - 1)
                        mm.then_inc(k_ps, 1)
                        for j in range(TB):
                            if b == 2 and j == 0:
                                pe.wait_ge(s_xt, T)
                            if b and j % 2 == 0:
                                pe.wait_ge(v_sb, 2 * (b - 1) + j // 2 + 1)
                            for k in range(KC):
                                mm = pe.matmul(ps[:, BV + j // 2, (j % 2) * D:(j % 2 + 1) * D],
                                               CT[:, k, (b * TB + j) * P:(b * TB + j + 1) * P],
                                               Wv[:, k, :], start=k == 0, stop=k == KC - 1)
                            if j % 2:
                                mm.then_inc(v_ps, 1)

                    def project_q(b):
                        if b == 1:
                            pe.wait_ge(v_sb, 2 * B)
                        if b > 1:
                            pe.wait_ge(q_rot, b)
                        for half in range(2):
                            for k in range(KC):
                                mm = pe.matmul(ps[:, BQ[b] + half, :], Wq[:, k, half * P:(half + 1) * P],
                                               XT[:, k, b * S:(b + 1) * S], start=k == 0, stop=k == KC - 1)
                        mm.then_inc(q_ps, 1)

                    pe.wait_ge(s_wkv, 32)
                    project_kv(0)
                    project_kv(1)
                    pe.wait_ge(s_c, 16)
                    pe.wait_ge(v_sb, 4)
                    for t in range(T):
                        pe.wait_ge(s_norm, t + 1)
                        if t >= 4:
                            pe.wait_ge(s_xt, t - 3)
                        for k in range(KC):
                            mm = pe.transpose(ps[:, BTX + t % 4, k * P:(k + 1) * P],
                                              XN[:, t, k * P:(k + 1) * P], self.ident)
                        mm.then_inc(s_turned, 1)
                    project_kv(2)
                    pe.wait_ge(s_wq, 16)
                    project_q(0)
                    project_kv(3)
                    for b in range(B):
                        if b + 1 < B:
                            project_q(b + 1)
                        pe.wait_ge(q_rot, b + 1)
                        if b:
                            pe.wait_ge(diag, TB * b)
                            pe.wait_ge(rest, (TB - 1) * b)
                        else:
                            pe.wait_ge(k_rot, B)
                        for j in range(TB):
                            for half in range(2):
                                mm = pe.matmul(ps[:, j, 0:S - j * P], kR[b][:, half, j * P:(j + 1) * P],
                                               qR[b % 2][:, half, j * P:S], start=half == 0, stop=half == 1)
                            mm.then_inc(s_ps, 1)
                        for i in range(TB):
                            pe.wait_ge(diag, TB * b + i + 1)
                            if i:
                                pe.wait_ge(rest, (TB - 1) * b + i)
                            if TB * b + i >= 2:
                                pe.wait_ge(x_new, TB * b + i - 1)
                            for j in range(i + 1):
                                mm = pe.matmul(ps[:, BO + i % 2, 0:D], ST[:, j, (i - j) * P:(i - j + 1) * P],
                                               V[:, b * TB + j, :], start=j == 0, stop=j == i)
                            mm.then_inc(o_ps, 1)

                @block.scalar
                def _(act):
                    def copy_v(b):
                        for h in range(2):
                            act.wait_ge(v_ps, 2 * b + h + 1)
                            act.copy(V[:, b * TB + 2 * h:b * TB + 2 * h + 2, :],
                                     ps[:, BV + h, :].rearrange("p (j d) -> p j d", j=2)).then_inc(v_sb, 1)

                    for i, name in enumerate(("g_xattn", "g_ffn")):
                        act.dma_start(self.gates[:, 2 * i:2 * i + 2],
                                      ins[name].rearrange("(a n) -> a n", a=1).broadcast_to([P, 2])).then_inc(s_g, 16)
                    act.dma_start(self.lnw[:], ins["lnw"]).then_inc(s_g, 16)
                    act.wait_ge(s_g, 48)
                    act.activation(self.tg[:], self.gates[:], ACT.Tanh)
                    copy_v(0)
                    self.ln_sqrt(act)
                    copy_v(1)
                    for t in range(T):
                        act.wait_ge(s_turned, t + 1)
                        act.copy(XT[:, :, t * P:(t + 1) * P],
                                 ps[:, BTX + t % 4, 0:D].rearrange("p (k c) -> p k c", k=KC)).then_inc(s_xt, 1)
                    copy_v(2)
                    copy_v(3)
                    for b in range(B):
                        if b:
                            act.wait_ge(o_ps, TB * b)
                        for j in range(TB - 1):
                            act.wait_ge(s_ps, TB * b + j + 1)
                            act.copy(ST[:, j, P:S - j * P], ps[:, j, P:S - j * P]).then_inc(rest, 1)

                @block.vector
                def _(e):
                    link = Chain(e, self.chain)

                    def rotate(dst, bank, table, sem):
                        even, odd = ps[:, bank, :], ps[:, bank + 1, :]
                        cos, sin = tab[:, table, :], tab[:, table + 1, :]
                        e.tensor_tensor(tmp[:, 0, :], even, cos, ALU.mult)
                        e.tensor_tensor(tmp[:, 1, :], odd, sin, ALU.mult)
                        e.tensor_tensor(tmp[:, 2, :], odd, cos, ALU.mult)
                        link(e.tensor_tensor(tmp[:, 3, :], even, sin, ALU.mult))
                        link(e.tensor_tensor(dst[:, 0, :], tmp[:, 0, :], tmp[:, 1, :], ALU.subtract))
                        link(e.tensor_tensor(dst[:, 1, :], tmp[:, 2, :], tmp[:, 3, :], ALU.add))
                        e.sem_inc(sem, 1)

                    def rotate_k(b):
                        e.wait_ge(k_ps, b + 1)
                        rotate(kR[b], 2 * (b % 2), 2, k_rot)

                    def rotate_q(b):
                        e.wait_ge(q_ps, b + 1)
                        if b >= 2:
                            e.wait_ge(s_ps, TB * (b - 1))
                        rotate(qR[b % 2], BQ[b], 0, q_rot)

                    e.wait_ge(s_x, 16)
                    self.ln_stats(e, X, link)
                    for t in range(T):
                        self.normalise(e, XN[:, t, :], X[:, t, :], t).then_inc(s_norm, 1)
                    e.wait_ge(s_tab, 16)
                    for b in range(3):
                        rotate_k(b)
                    rotate_q(0)
                    rotate_k(3)
                    for b in range(B):
                        if b + 1 < B:
                            rotate_q(b + 1)
                        for j in range(TB):
                            e.wait_ge(s_ps, TB * b + j + 1)
                            if j < TB - 1:
                                e.wait_ge(rest, (TB - 1) * b + j + 1)
                            if b:
                                e.wait_ge(o_ps, TB * b)
                            e.tensor_tensor(ST[:, j, 0:P], ps[:, j, 0:P],
                                            self.const_of("causal"), ALU.mult).then_inc(diag, 1)
                        for i in range(TB):
                            t = TB * b + i
                            e.wait_ge(o_ps, t + 1)
                            e.scalar_tensor_tensor(X[:, t, :], ps[:, BO + i % 2, 0:D], self.tg[:, 0:1],
                                                   X[:, t, :], ALU.mult, ALU.add).then_inc(x_new, 1)
                        e.wait_ge(x_new, TB * (b + 1))
                        self.ln_tiles(e, X, range(TB * b, TB * (b + 1)))

    def route(self, layer, top, slots):
        nc, ins, X, ps = self.nc, self.ins, self.X, self.ps
        with ExitStack() as ctx:
            pre = f"t{layer}_"
            sb = lambda name, shape, dt=F32: ctx.enter_context(nc.sbuf_tensor(pre + name, shape, dt))
            spare = self.W_all[:, 2 * EARLY:, :].rearrange("p e c -> p (e c)") if layer == 1 else None
            used = [0]

            def table(name, shape):
                if layer == 0:
                    return sb(name, shape)[:]
                size = int(np.prod(shape[1:]))
                at = used[0]
                used[0] += size
                letters = "abc"[:len(shape) - 1]
                form = f"p ({' '.join(letters)}) -> p {' '.join(letters)}"
                return spare[:, at:at + size].rearrange(form, **dict(zip(letters, shape[1:])))

            XN = sb("XN", [P, T, D])
            xt = table("xt", [P, T, KC, P])
            rw = sb("rw", [P, KC, E])
            rb = sb("rb", [P, E])
            names = ("L", "eq", "pr", "oh1", "oh2", "ohs", "L2", "incl", "incl2", "cnt", "row", "sel", "sh")
            L, eq, pr, oh1, oh2, ohs, L2, incl, incl2, cnt, row, sel, sh = (sb(n, [P, T, E]) for n in names)
            m1, m2, pm, den, gt = (sb(n, [P, T]) for n in ("m1", "m2", "pm", "den", "gt"))
            tot, end, end2 = (sb(n, [P, E]) for n in ("tot", "end", "end2"))
            toti = sb("toti", [P, E], I32)
            gate = [sb(f"gate{n}", [P, T]) for n in range(top)]
            place = sb("place", [P, 2, T], I32)
            where = sb("where", [P, 2, T])
            in_row = [table(f"in_row{n}", [P, T, P]) for n in range(top)]
            in_slot = [table(f"in_slot{n}", [P, 3, T, slots]) for n in range(top)]
            made_of = sb("made_of", [P, slots])
            free = sb("free", [P, slots])
            cmp = sb("cmp", [P, 64, E])
            se = sb("se", [P, 64])
            s_w, s_norm, s_turned, s_xt, s_log, s_oh, s_rank, s_exp, s_shift, s_hot, s_map, s_out = (
                self.sem(pre + n) for n in ("w", "norm", "turned", "xt", "log",
                                            "oh", "rank", "exp", "shift", "hot", "map", "out"))
            if layer == 1:
                zero = sb("zero", [P, D])
                s_total, s_zero = self.sem(pre + "total"), self.sem(pre + "zero")
            if layer == 0:
                C = self.C
                self.kv_buffers(ctx, "media")
            rev = self.const_of("rev").rearrange("p (t e) -> p t e", e=E)
            wide = lambda a: a.unsqueeze(2).broadcast_to([P, T, E])
            flat = lambda a: a[:].rearrange("p t e -> p (t e)")
            BL, BR, BC, BM = 4, 5, 6, 7

            with nc.Block() as block:
                @block.sync
                def _(sp):
                    sp.dma_start(rw[:], ins[f"rw{layer}"].rearrange("(k p) n -> p k n", p=P)).then_inc(s_w, 16)
                    if layer == 0:
                        sp.dma_start(rb[:], ins["rb0"].rearrange("(a n) -> a n", a=1).broadcast_to([P, E])).then_inc(s_w, 16)
                    if layer == 1:
                        sp.dma_start(self.total[0:T * P, :].rearrange("(t p) d -> p t d", p=P), X[:]).then_inc(s_total, 16)
                        sp.wait_ge(s_zero, 1)
                        sp.dma_start(self.total[T * P:, :], zero[:]).then_inc(s_total, 16)
                        for ex in range(EARLY):
                            sp.dma_start(self.W_all[:, 2 * ex:2 * ex + 2, :],
                                         ins["We1"][2 * ex:2 * ex + 2].rearrange("a p c -> p a c")).then_inc(self.w1_in, 16)
                    rows = self.normed[layer].rearrange("(t p) d -> p t d", p=P)
                    for t in range(0, T, 4):
                        sp.wait_ge(s_norm, t + 4)
                        sp.dma_start(rows[:, t:t + 4, :], XN[:, t:t + 4, :]).then_inc(s_out, 16)
                    sp.wait_ge(s_out, 16 * (T // 4))
                    if layer == 0:
                        self.kv_store(sp, 0)
                    else:
                        sp.wait_ge(self.w1_in, 16 * EARLY)
                        sp.wait_ge(s_total, 32)

                @block.gpsimd
                def _(pool):
                    if layer == 1:
                        pool.memset(zero[:], 0.0).then_inc(s_zero, 1)
                    else:
                        self.kv_low(pool)

                @block.tensor
                def _(pe):
                    for t in range(T + 1):
                        if t < T:
                            pe.wait_ge(s_norm, t + 1)
                            if t >= 4:
                                pe.wait_ge(s_xt, t - 3)
                            for k in range(KC):
                                mm = pe.transpose(ps[:, t % 4, k * P:(k + 1) * P], XN[:, t, k * P:(k + 1) * P], self.ident)
                            mm.then_inc(s_turned, 1)
                        if t == 0:
                            pe.wait_ge(s_w, 32 if layer == 0 else 16)
                            continue
                        pe.wait_ge(s_xt, t)
                        for k in range(KC):
                            mm = pe.matmul(ps[:, BL, (t - 1) * E:t * E], xt[:, t - 1, k, :], rw[:, k, :],
                                           start=k == 0, stop=k == KC - 1)
                        mm.then_inc(s_log, 1)
                    pe.wait_ge(s_oh, 1)
                    pe.matmul(ps[:, BR, 0:T * E], self.const_of("tri"), flat(ohs), start=True, stop=True)
                    pe.matmul(ps[:, BC, 0:T * E], self.const_of("ones"), flat(ohs),
                              start=True, stop=True).then_inc(s_rank, 1)
                    if layer == 0:
                        self.kv_turn(pe, C)
                    for n in range(top):
                        pe.wait_ge(s_hot, n + 1)
                        for t in range(T):
                            mm = pe.matmul(ps[:, BM, 0:3 * slots].rearrange("p (a s) -> p a s", s=slots),
                                           in_row[n][:, t, :], in_slot[n][:, :, t, :],
                                           start=n == 0 and t == 0, stop=n == top - 1 and t == T - 1)
                    mm.then_inc(s_map, 1)

                @block.scalar
                def _(act):
                    self.ln_sqrt(act)
                    for t in range(T):
                        act.wait_ge(s_turned, t + 1)
                        act.copy(xt[:, t, :, :], ps[:, t % 4, 0:D].rearrange("p (k c) -> p k c", k=KC)).then_inc(s_xt, 1)
                        if layer == 0 and t == T // 2:
                            self.ln_sqrt(act)
                    act.wait_ge(s_shift, 1)
                    if top == 1:
                        act.activation(flat(sh), flat(pr), ACT.Exp).then_inc(s_exp, 1)
                    else:
                        act.activation(pm[:], den[:], ACT.Exp).then_inc(s_exp, 1)
                    if layer == 0:
                        self.kv_affine(act, 0)

                @block.vector
                def _(e):
                    link = Chain(e, self.chain)
                    self.ln_stats(e, None, link)
                    for t in range(T):
                        self.normalise(e, XN[:, t, :], X[:, t, :], t).then_inc(s_norm, 1)
                    if layer == 0:
                        self.ln_stats(e, C, link)
                        for t in range(T):
                            self.normalise(e, C[:, t, :], C[:, t, :], t).then_inc(self.kv_norm, 1)
                    e.wait_ge(s_log, T)
                    logits = ps[:, BL, 0:T * E].rearrange("p (t e) -> p t e", e=E)
                    if layer == 0:
                        link(e.tensor_tensor(L[:], logits, rb[:].unsqueeze(1).broadcast_to([P, T, E]), ALU.add))
                    else:
                        link(e.tensor_copy(L[:], logits))

                    def first_max(src, m, oh):
                        link(e.tensor_reduce(m[:], src[:], AX, ALU.max))
                        link(e.tensor_tensor(eq[:], src[:], wide(m[:]), ALU.is_equal))
                        link(e.tensor_tensor(pr[:], eq[:], rev, ALU.mult))
                        link(e.tensor_reduce(pm[:], pr[:], AX, ALU.max))
                        link(e.tensor_tensor(oh[:], rev, wide(pm[:]), ALU.is_equal))

                    first_max(L, m1, oh1)
                    hot = oh1
                    if top == 2:
                        link(e.scalar_tensor_tensor(L2[:], oh1[:], -BIG, L[:], ALU.mult, ALU.add))
                        first_max(L2, m2, oh2)
                        hot = ohs
                        link(e.tensor_tensor(ohs[:], oh1[:], oh2[:], ALU.add))
                    else:
                        link(e.tensor_copy(ohs[:], oh1[:]))
                    e.sem_inc(s_oh, 1)
                    tanh = self.tg[:, 2 + layer:3 + layer]
                    if top == 1:
                        link(e.tensor_tensor(pr[:], L[:], wide(m1[:]), ALU.subtract))
                        e.sem_inc(s_shift, 1)
                        e.wait_ge(s_exp, 1)
                        link(e.tensor_reduce(den[:], sh[:], AX, ALU.add))
                        link(e.reciprocal(gt[:], den[:]))
                        link(e.tensor_scalar(gate[0][:], gt[:], tanh, None, ALU.mult))
                    else:
                        link(e.tensor_tensor(den[:], m2[:], m1[:], ALU.subtract))
                        e.sem_inc(s_shift, 1)
                        e.wait_ge(s_exp, 1)
                        link(e.tensor_scalar(den[:], pm[:], 1.0, None, ALU.add))
                        link(e.reciprocal(gt[:], den[:]))
                        link(e.tensor_scalar(gate[0][:], gt[:], tanh, None, ALU.mult))
                        link(e.tensor_tensor(gate[1][:], gate[0][:], pm[:], ALU.mult))
                    e.wait_ge(s_rank, 1)
                    link(e.tensor_copy(flat(cnt), ps[:, BC, 0:T * E]))
                    src, dst = cnt, incl
                    for step in (1, 2, 4, 8):
                        e.tensor_copy(dst[:, 0:step, :], src[:, 0:step, :])
                        link(e.tensor_tensor(dst[:, step:, :], src[:, step:, :], src[:, :T - step, :], ALU.add))
                        src, dst = dst, (incl2 if dst is incl else incl)
                    link(e.tensor_scalar(tot[:], src[:, T - 1, :], float(P - 1), None, ALU.add))
                    link(e.tensor_copy(toti[:], tot[:]))
                    link(e.tensor_scalar(toti[:], toti[:], 7, None, ALU.arith_shift_right))
                    link(e.tensor_copy(tot[:], toti[:]))
                    a, b2 = tot, end
                    for step in (1, 2, 4):
                        e.tensor_copy(b2[:, 0:step], a[:, 0:step])
                        link(e.tensor_tensor(b2[:, step:], a[:, step:], a[:, :E - step], ALU.add))
                        a, b2 = b2, (end2 if b2 is end else end)
                    link(e.tensor_tensor(b2[:], a[:], tot[:], ALU.subtract))
                    link(e.tensor_scalar(b2[:], b2[:], float(P), None, ALU.mult))
                    link(e.tensor_tensor(flat(row), ps[:, BR, 0:T * E], flat(src), ALU.add))
                    link(e.tensor_tensor(row[:], row[:], cnt[:], ALU.subtract))
                    link(e.tensor_tensor(row[:], row[:], b2[:].unsqueeze(1).broadcast_to([P, T, E]), ALU.add))
                    slot_no = self.const_of("slot")[:, 0:slots].unsqueeze(1).broadcast_to([P, T, slots])
                    for n, oh in enumerate((oh1, oh2)[:top]):
                        link(e.tensor_tensor(sel[:], row[:], oh[:], ALU.mult))
                        link(e.tensor_reduce(pm[:], sel[:], AX, ALU.add))
                        link(e.tensor_copy(place[:, 0, :], pm[:]))
                        e.tensor_scalar(place[:, 1, :], place[:, 0, :], 7, None, ALU.arith_shift_right)
                        link(e.tensor_scalar(place[:, 0, :], place[:, 0, :], P - 1, None, ALU.bitwise_and))
                        link(e.tensor_copy(where[:], place[:]))
                        e.tensor_tensor(in_row[n], self.const_of("iota").unsqueeze(1).broadcast_to([P, T, P]),
                                        where[:, 0, :].unsqueeze(2).broadcast_to([P, T, P]), ALU.is_equal)
                        link(e.tensor_tensor(in_slot[n][:, 2, :, :], slot_no,
                                             where[:, 1, :].unsqueeze(2).broadcast_to([P, T, slots]), ALU.is_equal))
                        for v, value in ((0, self.const_of("token")), (1, gate[n][:])):
                            ins_ = e.tensor_tensor(in_slot[n][:, v, :, :], in_slot[n][:, 2, :, :],
                                                   value.unsqueeze(2).broadcast_to([P, T, slots]), ALU.mult)
                        link(ins_)
                        e.sem_inc(s_hot, 1)
                    link(e.tensor_tensor(cmp[:], self.const_of("slot").unsqueeze(2).broadcast_to([P, 64, E]),
                                         a[:].unsqueeze(1).broadcast_to([P, 64, E]), ALU.is_ge))
                    link(e.tensor_reduce(se[:], cmp[:], AX, ALU.add))
                    link(e.tensor_scalar(se[:], se[:], float(E - 1), None, ALU.min))
                    link(e.tensor_copy(self.slot_expert[:], se[:]))
                    link(e.memset(self.gather_idx[:], 0))
                    e.wait_ge(s_map, 1)
                    mapped = lambda v: ps[:, BM, v * slots:(v + 1) * slots]
                    link(e.tensor_copy(self.slot_gate[:, 0:slots], mapped(1)))
                    link(e.tensor_copy(self.gather_idx[:, 0:slots], mapped(0)))
                    behind = (self.const_of("pad")[:, 0:slots] if layer == 0 else
                              self.const_of("pad")[:, 0:1].broadcast_to([P, slots]))
                    link(e.tensor_scalar(free[:], mapped(2), -1.0, 1.0, ALU.mult, ALU.add))
                    link(e.scalar_tensor_tensor(free[:], behind, float(T * P), free[:], ALU.add, ALU.mult))
                    link(e.tensor_tensor(made_of[:], self.gather_idx[:, 0:slots], free[:], ALU.add))
                    link(e.tensor_copy(self.scatter_idx[:, 0:slots], made_of[:]))

    def experts(self, layer, slots, half_w):
        nc, ins, ps = self.nc, self.ins, self.ps
        cks = chunks(half_w)
        edges = np.cumsum([0, KC * half_w, KC * half_w, len(cks) * D])
        A, G, DN = (slice(int(edges[i]), int(edges[i + 1])) for i in range(3))
        packed = int(edges[-1])
        units = 2 * slots
        resident = layer == 1
        W_dram = ins[f"We{layer}"]
        with ExitStack() as ctx:
            pre = f"e{layer}_"
            sb = lambda name, shape, dt=F32: ctx.enter_context(nc.sbuf_tensor(pre + name, shape, dt))
            if resident:
                W = self.W_all
            else:
                W = [sb(f"W{i}", [P, DN.start]) for i in range(4)]
            Ws = [sb(f"Ws{i}", [P, 2, packed], F32R) for i in range(2)]
            xT = [sb(f"xT{i}", [P, 2, KC, P], F32R) for i in range(2)]
            aT = [sb(f"aT{i}", [P, 2, len(cks), P], F32R) for i in range(2)]
            NX, NY = 2, 1 if resident else 2
            xin = [sb(f"xin{i}", [P, D]) for i in range(NX)]
            act_ = [sb(f"act{i}", [P, half_w]) for i in range(2)]
            y = [sb(f"y{i}", [P, D]) for i in range(NY)]
            from_tok = [sb(f"from{i}", [P, 1], I32) for i in range(NX)]
            to_row = [sb(f"to{i}", [P, 1], I32) for i in range(NY)]
            x_in = [self.sem(pre + f"x_in{i}") for i in range(NX)]
            y_out = [self.sem(pre + f"y_out{i}") for i in range(NY)]
            w_in = [self.w1_in] if resident else [self.sem(pre + f"w_in{i}") for i in range(4)]
            (from_ready, to_ready, x_turned, x_high, x_low, A_high, A_low, G_high, G_low,
             D_high, D_low, A_done, G_done, D_done, sil_ready, act_ready, a_turned, a_high, a_low, y_read) = (
                self.sem(pre + n) for n in (
                    "from_ready", "to_ready", "x_turned", "x_high", "x_low", "A_high",
                    "A_low", "G_high", "G_low", "D_high", "D_low", "A_done", "G_done", "D_done", "sil_ready",
                    "act_ready", "a_turned", "a_high", "a_low", "y_read"))
            BT, BY, BX = 4, 6, 7

            def every(eng, unit):
                for n in range(4):
                    unit(n, n, n // 2)
                with eng.Fori(1, (units - 2) // 4) as i:
                    for v in range(4):
                        unit(i * 4 + v, v, i * 2 + v // 2)
                for n in (units - 2, units - 1):
                    unit(n, n % 4, n // 2)

            first = lambda n, count: isinstance(n, int) and n < count
            x_before = lambda s, par: (s - par) * 8
            y_before = lambda s, par: (s - par) * 8 if NY == 2 else s * 16
            exists = lambda n: not isinstance(n, int) or n < units

            def raw(eng, ex, j, piece):
                if resident:
                    return W[:, bass.ds(ex * 2 + j % 2, 1), piece].rearrange("p a c -> p (a c)")
                if piece is DN:
                    return self.W_down[:, bass.ds(ex * 2 + j % 2, 1), :].rearrange("p a c -> p (a c)")
                return W[j][:, piece]

            def expert_of(eng, s, needed=True):
                return eng.value_load(self.slot_expert[0:1, bass.ds(s, 1)], min_val=0, max_val=E - 1) if needed else None

            with nc.Block() as block:
                @block.sync
                def _(sp):
                    if resident:
                        sp.wait_ge(x_turned, 2)
                        for ex in range(EARLY, E):
                            sp.wait_ge(w_in[0], 16 * ex)
                            sp.dma_start(W[:, 2 * ex:2 * ex + 2, :],
                                         W_dram[2 * ex:2 * ex + 2].rearrange("a p c -> p a c")).then_inc(w_in[0], 16)
                        return

                    def fetch(n, j, s):
                        if j % 2 == 0:
                            for hf in range(2):
                                ex = sp.value_load(self.slot_expert[0:1, bass.ds(s, 1)], min_val=0, max_val=E - 1)
                                if not first(n, 4):
                                    sp.wait_ge(G_low, n + hf - 3)
                                    sp.wait_ge(D_low, n + hf - 3)
                                sp.dma_start(W[j + hf][:], W_dram[bass.ds(ex * 2 + hf, 1), :, 0:DN.start].rearrange(
                                    "a p c -> p (a c)")).then_inc(w_in[j + hf], 16)
                    every(sp, fetch)

                @block.tensor
                def _(pe):
                    def exact(out, lhs, rhs, ks, start=True, stop=True):
                        parts = [(i, j, k) for i, j in ((0, 0), (0, 1), (1, 0)) for k in ks]
                        for m, (i, j, k) in enumerate(parts):
                            mm = pe.matmul(out, lhs(i, k), rhs(j, k), start=start and m == 0,
                                           stop=stop and m == len(parts) - 1)
                        return mm

                    def up(j, g, piece):
                        w = Ws[j % 2][:, :, piece].rearrange("p h (k c) -> p h k c", k=KC)
                        return exact(ps[:, 2 * (j % 2) + g, 0:half_w], lambda i, k: xT[j // 2][:, i, k, :],
                                     lambda i, k: w[:, i, k, :], range(KC))

                    def product_G(n, j):
                        pe.wait_ge(G_low, n + 1)
                        if not first(n, 2):
                            pe.wait_ge(act_ready, n - 1)
                        up(j, 1, G).then_inc(G_done, 1)

                    def product_A(n, j, s):
                        pe.wait_ge(A_low, n + 1)
                        if not first(n, 2):
                            pe.wait_ge(sil_ready, n - 1)
                        if j % 2 == 0:
                            pe.wait_ge(x_low, s + 1)
                        up(j, 0, A).then_inc(A_done, 1)

                    def product_D(n, j, s):
                        pe.wait_ge(a_low, n + 1)
                        pe.wait_ge(D_low, n + 1)
                        if j % 2 == 0 and not first(s, 1):
                            pe.wait_ge(y_read, s)
                        w = Ws[j % 2][:, :, DN].rearrange("p h (c d) -> p h c d", d=D)
                        for c, (c0, cw) in enumerate(cks):
                            mm = exact(ps[:, BY, 0:D], lambda i, k: aT[j % 2][0:cw, i, k, :], lambda i, k: w[0:cw, i, k, :],
                                       [c], start=j % 2 == 0 and c == 0, stop=j % 2 == 1 and c == len(cks) - 1)
                        mm.then_inc(D_done, 1)

                    def turn_a(n, j):
                        pe.wait_ge(act_ready, n + 1)
                        for c, (c0, cw) in enumerate(cks):
                            mm = pe.transpose(ps[0:cw, BT + j % 2, c * P:(c + 1) * P], act_[j % 2][:, c0:c0 + cw], self.ident)
                        mm.then_inc(a_turned, 1)

                    def turn_x(s, par):
                        pe.wait_ge(x_in[par], x_before(s, par) + 16)
                        for k in range(KC):
                            mm = pe.transpose(ps[:, BX, k * P:(k + 1) * P], xin[par][:, k * P:(k + 1) * P], self.ident)
                        mm.then_inc(x_turned, 1)

                    def unit(n, j, s):
                        product_G(n, j)
                        if exists(n + 1):
                            product_A(n + 1, (j + 1) % 4, s + 1 if j % 2 else s)
                        if j % 2 == 0 and exists(n + 2):
                            turn_x(s + 1, (j // 2 + 1) % 2)
                        if not first(n, 1):
                            product_D(n - 1, (j + 3) % 4, s if j % 2 else s - 1)
                        turn_a(n, j)

                    turn_x(0, 0)
                    product_A(0, 0, 0)
                    every(pe, unit)
                    product_D(units - 1, (units - 1) % 4, slots - 1)

                @block.scalar
                def _(act):
                    def high(n, j, ex, piece, sem):
                        if resident or piece is DN:
                            act.sem_inc(self.carried, 1)
                        act.copy(Ws[j % 2][:, 0, piece], raw(act, ex, j, piece)).then_inc(sem, 1)

                    def silu(n, j):
                        act.wait_ge(A_done, n + 1)
                        act.activation(act_[j % 2][:], ps[:, 2 * (j % 2), 0:half_w], ACT.Silu).then_inc(sil_ready, 1)

                    def high_a(n, j):
                        act.wait_ge(a_turned, n + 1)
                        if not first(n, 2):
                            act.wait_ge(D_done, n - 1)
                        full = len([1 for _, cw in cks if cw == P])
                        copied = act.copy(aT[j % 2][:, 0, 0:full, :],
                                          ps[:, BT + j % 2, 0:full * P].rearrange("p (c t) -> p c t", t=P))
                        if full < len(cks):
                            cw = cks[-1][1]
                            copied = act.copy(aT[j % 2][0:cw, 0, full, :], ps[0:cw, BT + j % 2, full * P:(full + 1) * P])
                        copied.then_inc(a_high, 1)

                    def high_x(s, par):
                        act.wait_ge(x_turned, s + 1)
                        act.copy(xT[par][:, 0], ps[:, BX, 0:D].rearrange("p (k t) -> p k t", k=KC)).then_inc(x_high, 1)

                    def unit(n, j, s):
                        ex = expert_of(act, s)
                        ex_next = expert_of(act, s + 1, resident and exists(n + 2))
                        if not first(n, 1):
                            high_a(n - 1, (j + 3) % 4)
                        if not first(n, 2):
                            act.wait_ge(D_done, n - 1)
                        high(n, j, ex, DN, D_high)
                        if exists(n + 2):
                            nxt = (j + 2) % 4
                            if resident:
                                act.wait_ge(w_in[0], ex_next * 16 + 16)
                            else:
                                act.wait_ge(w_in[nxt], (n - j) * 4 + (16 if j < 2 else 32))
                            act.wait_ge(A_done, n + 1)
                            high(n + 2, nxt, ex_next, A, A_high)
                            if j % 2 == 0:
                                high_x(s + 1, (j // 2 + 1) % 2)
                            act.wait_ge(G_done, n + 1)
                            high(n + 2, nxt, ex_next, G, G_high)
                        if exists(n + 1):
                            silu(n + 1, (j + 1) % 4)

                    ex = expert_of(act, 0, resident)
                    for n in range(2):
                        act.wait_ge(w_in[0 if resident else n], ex * 16 + 16 if resident else 16)
                        high(n, n, ex, A, A_high)
                        high(n, n, ex, G, G_high)
                        if n == 0:
                            high_x(0, 0)
                    silu(0, 0)
                    every(act, unit)
                    high_a(units - 1, (units - 1) % 4)

                @block.vector
                def _(e):
                    def low(j, ex, piece, sem):
                        e.tensor_tensor(Ws[j % 2][:, 1, piece], raw(e, ex, j, piece), Ws[j % 2][:, 0, piece].bitcast(F32),
                                        ALU.subtract).then_inc(sem, 1)

                    def low_x(s, par):
                        e.wait_ge(x_high, s + 1)
                        e.tensor_tensor(xT[par][:, 1], ps[:, BX, 0:D].rearrange("p (k t) -> p k t", k=KC),
                                        xT[par][:, 0].bitcast(F32), ALU.subtract).then_inc(x_low, 1)

                    def low_a(n, j):
                        e.wait_ge(a_high, n + 1)
                        full = len([1 for _, cw in cks if cw == P])
                        parts = [(P, slice(0, full), full)] + [(cw, slice(full, full + 1), 1) for _, cw in cks[full:]]
                        for cw, c, nc_ in parts:
                            sub = e.tensor_tensor(
                                aT[j % 2][0:cw, 1, c, :],
                                ps[0:cw, BT + j % 2, c.start * P:c.stop * P].rearrange("p (c t) -> p c t", t=P),
                                aT[j % 2][0:cw, 0, c, :].bitcast(F32), ALU.subtract)
                        sub.then_inc(a_low, 1)

                    def gate(n, j):
                        e.wait_ge(G_done, n + 1)
                        e.wait_ge(sil_ready, n + 1)
                        e.tensor_tensor(act_[j % 2][:], act_[j % 2][:], ps[:, 2 * (j % 2) + 1, 0:half_w],
                                        ALU.mult).then_inc(act_ready, 1)

                    def weighted_y(s, par):
                        e.wait_ge(D_done, s * 2 + 2)
                        if not first(s, NY):
                            e.wait_ge(y_out[par % NY], y_before(s, par))
                        e.tensor_scalar(y[par % NY][:], ps[:, BY, 0:D], self.slot_gate[:, bass.ds(s, 1)], None,
                                        ALU.mult).then_inc(y_read, 1)

                    def unit(n, j, s):
                        ex = expert_of(e, s + 1, resident and exists(n + 2))
                        if not first(n, 1):
                            low_a(n - 1, (j + 3) % 4)
                        gate(n, j)
                        if exists(n + 2):
                            e.wait_ge(A_high, n + 3)
                            low((j + 2) % 4, ex, A, A_low)
                            if j % 2 == 0:
                                low_x(s + 1, (j // 2 + 1) % 2)
                            e.wait_ge(G_high, n + 3)
                            low((j + 2) % 4, ex, G, G_low)
                        if j % 2 == 0 and not first(s, 1):
                            weighted_y(s - 1, (j // 2 + 1) % 2)

                    ex = expert_of(e, 0, resident)
                    for n in range(2):
                        e.wait_ge(A_high, n + 1)
                        low(n, ex, A, A_low)
                        e.wait_ge(G_high, n + 1)
                        low(n, ex, G, G_low)
                        if n == 0:
                            low_x(0, 0)
                    every(e, unit)
                    low_a(units - 1, (units - 1) % 4)
                    weighted_y(slots - 1, (slots - 1) % 2)

                @block.gpsimd
                def _(pool):
                    def gather(s, par):
                        if not first(s, 2):
                            pool.wait_ge(x_turned, s - 1)
                        pool.tensor_copy(from_tok[par][:], self.gather_idx[:, bass.ds(s, 1)]).then_inc(from_ready, 1)
                        pool.wait_ge(from_ready, s + 1)
                        pool.sem_inc(self.carried, 1)
                        pool.indirect_dma_start(xin[par][:], None, self.normed[layer],
                                                bass.IndirectOffsetOnAxis(ap=from_tok[par][:], axis=0)).then_inc(x_in[par], 16)

                    def scatter(s, par):
                        u = par % NY
                        pool.wait_ge(y_read, s + 1)
                        pool.tensor_copy(to_row[u][:], self.scatter_idx[:, bass.ds(s, 1)]).then_inc(to_ready, 1)
                        pool.wait_ge(to_ready, s + 1)
                        pool.sem_inc(self.carried, 1)
                        if layer == 0:
                            move = pool.indirect_dma_start(
                                self.made, bass.IndirectOffsetOnAxis(ap=to_row[u][:], axis=0), y[u][:], None)
                        else:
                            move = pool.indirect_dma_start(
                                self.total, bass.IndirectOffsetOnAxis(ap=to_row[u][:], axis=0), y[u][:], None,
                                compute_op=ALU.add)
                        move.then_inc(y_out[u], 16)

                    def unit(n, j, s):
                        ex = expert_of(pool, s)
                        if j % 2 == 0 and exists(n + 2):
                            gather(s + 2, j // 2)
                        if j % 2 == 1 and not first(s, 1):
                            scatter(s - 1, (j // 2 + 1) % 2)
                        pool.wait_ge(D_high, n + 1)
                        pool.sem_inc(self.carried, 1)
                        pool.tensor_tensor(Ws[j % 2][:, 1, DN], raw(pool, ex, j, DN), Ws[j % 2][:, 0, DN].bitcast(F32),
                                           ALU.subtract).then_inc(D_low, 1)

                    gather(0, 0)
                    gather(1, 1)
                    every(pool, unit)
                    scatter(slots - 1, (slots - 1) % 2)
                    for u in range(NY):
                        pool.wait_ge(y_out[u], 16 * len(range(u, slots, NY)))
                    pool.wait_ge(x_in[slots % 2], 16 * (slots // 2 + 1))

    def add_outputs(self, e, tiles, Z, s_z, s_new):
        for t in tiles:
            e.wait_ge(s_z[t // 4], 16)
            e.tensor_tensor(self.X[:, t, :], self.X[:, t, :], Z[:, t, :], ALU.add).then_inc(s_new, 1)

    def shares(self):
        return [t for t in range(T) if t % 4 != 3], [t for t in range(T) if t % 4 == 3]

    def load_outputs(self, sp, Z, s_z):
        src = self.made[0:T * P, :].rearrange("(t p) d -> p t d", p=P)
        for g in range(T // 4):
            sp.dma_start(Z[:, 4 * g:4 * g + 4, :], src[:, 4 * g:4 * g + 4, :]).then_inc(s_z[g], 16)

    def kv_buffers(self, ctx, name):
        self.kv_val = ctx.enter_context(self.nc.sbuf_tensor(name + "_val", [P, B, KC, S], F32))
        self.kv_high = ctx.enter_context(self.nc.sbuf_tensor(name + "_high", [P, B, KC, S], F32R))
        self.kv_tile2 = self.sem(name + "_tile2")
        (self.kv_norm, self.kv_turned, self.kv_tile, self.kv_h, self.kv_l, self.kv_out) = (
            self.sem(name + "_" + n) for n in ("norm", "turned", "tile", "high", "low", "out"))

    def kv_bank(self, m, k, shared):
        return self.ps[:, 2 * (m % 4) + k, 0:P] if shared else self.ps[:, m % 4, k * P:(k + 1) * P]

    def kv_turn(self, pe, src, shared=False):
        for m in range(T):
            pe.wait_ge(self.kv_norm, m + 1)
            if m >= 4:
                pe.wait_ge(self.kv_tile, m - 3)
                if shared:
                    pe.wait_ge(self.kv_tile2, m - 3)
            for k in range(KC):
                mm = pe.transpose(self.kv_bank(m, k, shared), src[:, m, k * P:(k + 1) * P], self.ident)
            mm.then_inc(self.kv_turned, 1)

    def kv_affine(self, act, latent, shared=False):
        for m in range(T):
            b, j = m // TB, m % TB
            act.wait_ge(self.kv_turned, m + 1)
            for k in range(1 if shared else KC):
                last = act.activation(self.kv_val[:, b, k, j * P:(j + 1) * P], self.kv_bank(m, k, shared),
                                      ACT.Identity, bias=self.lnw[:, 2 * latent + 1, k:k + 1],
                                      scale=self.lnw[:, 2 * latent, k:k + 1])
            last.then_inc(self.kv_tile, 1)
            if j == TB - 1:
                act.wait_ge(self.kv_tile, m + 1)
                if shared:
                    act.wait_ge(self.kv_tile2, m + 1)
                act.copy(self.kv_high[:, b], self.kv_val[:, b]).then_inc(self.kv_h, 1)

    def kv_affine_1(self, e, latent, b):
        for j in range(TB):
            m = b * TB + j
            e.wait_ge(self.kv_turned, m + 1)
            e.tensor_scalar(self.kv_val[:, b, 1, j * P:(j + 1) * P], self.kv_bank(m, 1, True),
                            self.lnw[:, 2 * latent, 1:2], self.lnw[:, 2 * latent + 1, 1:2],
                            ALU.mult, ALU.add).then_inc(self.kv_tile2, 1)

    def kv_low(self, e, batches=range(B)):
        for b in batches:
            e.wait_ge(self.kv_h, b + 1)
            e.tensor_tensor(self.kv_val[:, b].bitcast(F32R), self.kv_val[:, b], self.kv_high[:, b].bitcast(F32),
                            ALU.subtract).then_inc(self.kv_l, 1)

    def kv_store(self, sp, latent, first=0):
        half = slice(latent * S, (latent + 1) * S)
        for b in range(first, B):
            sp.wait_ge(self.kv_l, b + 1)
            sp.dma_start(self.kv_dram[b][:, 0, :, half], self.kv_high[:, b].bitcast(F32)).then_inc(self.kv_out, 16)
            sp.dma_start(self.kv_dram[b][:, 1, :, half], self.kv_val[:, b]).then_inc(self.kv_out, 16)
        sp.wait_ge(self.kv_out, 32 * (B - first))

    def finish(self):
        s_out = self.sem("f_out")
        with self.nc.Block() as block:
            @block.sync
            def _(sp):
                sp.dma_start(self.out, self.total[0:T * P, :]).then_inc(s_out, 16)
                sp.wait_ge(s_out, 16)

    def latents(self):
        nc, ins, X, ps = self.nc, self.ins, self.X, self.ps
        with ExitStack() as ctx:
            sb = lambda name, shape, dt=F32: ctx.enter_context(nc.sbuf_tensor(name, shape, dt))
            Z = sb("l_Z", [P, T, D])
            XN = sb("l_XN", [P, T, D])
            W_raw = sb("l_W", [P, 3, KC, INNER])
            self.kv_buffers(ctx, "latent")
            s_z = [self.sem(f"l_z{g}") for g in range(T // 4)]
            s_new2 = self.sem("l_new2")
            s_new, s_w, w_high = self.sem("l_new"), self.sem("l_w"), self.sem("l_w_high")
            with nc.Block() as block:
                @block.sync
                def _(sp):
                    self.load_outputs(sp, Z, s_z)
                    sp.dma_start(W_raw[:], ins["Wvkq1"]).then_inc(s_w, 16)
                    for part in range(2):
                        sp.dma_start(self.kv_in[:, part, :, 0:S].bitcast(F32),
                                     self.kv_dram[0][:, part, :, 0:S]).then_inc(self.s_kv, 16)
                    sp.wait_ge(self.kv_l, 1)
                    for part, src in enumerate((self.kv_high[:, 0].bitcast(F32), self.kv_val[:, 0])):
                        sp.dma_start(self.kv_in[:, part, :, S:].bitcast(F32), src).then_inc(self.s_kv, 16)
                    self.kv_store(sp, 1, 1)
                    sp.wait_ge(self.s_kv, 64)

                @block.vector
                def _(e):
                    link = Chain(e, self.chain)
                    mine, others = self.shares()
                    self.add_outputs(e, mine, Z, s_z, s_new)
                    e.wait_ge(s_new, len(mine))
                    e.wait_ge(s_new2, len(others))
                    self.ln_stats(e, X, link)
                    for t in range(T - 1):
                        self.normalise(e, XN[:, t, :], X[:, t, :], t)
                    link(self.normalise(e, XN[:, T - 1, :], X[:, T - 1, :], T - 1))
                    self.ln_stats(e, XN, link)
                    for b in range(B + 2):
                        if b < B:
                            for t in range(b * TB, (b + 1) * TB):
                                self.normalise(e, Z[:, t, :], XN[:, t, :], t).then_inc(self.kv_norm, 1)
                        if 1 <= b < B + 1:
                            self.kv_affine_1(e, 1, b - 1)
                        if b >= 2:
                            self.kv_low(e, [b - 2])
                    for w in range(3):
                        e.wait_ge(w_high, w + 1)
                        e.tensor_tensor(self.W_att[:, 1, w], W_raw[:, w], self.W_att[:, 0, w].bitcast(F32), ALU.subtract)

                @block.gpsimd
                def _(pool):
                    self.add_outputs(pool, self.shares()[1], Z, s_z, s_new2)

                @block.tensor
                def _(pe):
                    self.kv_turn(pe, Z, True)

                @block.scalar
                def _(act):
                    act.wait_ge(s_w, 16)
                    for w in range(3):
                        act.copy(self.W_att[:, 0, w], W_raw[:, w]).then_inc(w_high, 1)
                    self.ln_sqrt(act)
                    self.ln_sqrt(act)
                    self.kv_affine(act, 1, True)

    def perceiver(self):
        nc, ins, X, ps = self.nc, self.ins, self.X, self.ps
        STEPS = H * TB
        with ExitStack() as ctx:
            sb = lambda name, shape, dt=F32: ctx.enter_context(nc.sbuf_tensor("p_" + name, shape, dt))
            kv = self.kv_in
            W = self.W_att
            WV, WK, WQ = range(3)
            Wo = sb("Wo", [P, H, D])
            V2 = sb("V2", [P, KT, H, P], F32R)
            kHL = sb("kHL", [P, 2, KEYS], F32R)
            qHL = sb("qHL", [P, 2, S], F32R)
            K2 = [[sb(f"K2{i}{j}", [P, KEYS], F32R) for j in range(2)] for i in range(2)]
            Q2 = [[sb(f"Q2{i}{j}", [P, 2, S], F32R) for j in range(2)] for i in range(2)]
            Pr = [sb(f"Pr{i}", [P, KEYS]) for i in range(3)]
            Ph = [sb(f"Ph{i}", [P, KT, 2 * P], F32R) for i in range(2)]
            Pl = [sb(f"Pl{i}", [P, KT, 2 * P], F32R) for i in range(2)]
            AT = sb("AT", [P, H, S])
            nmax = sb("nmax", [P, STEPS])
            den = sb("den", [P, STEPS])
            rden = sb("rden", [P, STEPS])
            s_kv = self.s_kv
            names = ( "proj", "proj_h", "proj_l", "v_ps", "v_h", "v_l", "s_ps", "max",
                     "exp", "rden", "norm", "turn", "ph", "pl", "o_ps", "o_sb", "y_ps", "y_add")
            ( proj, proj_h, proj_l, v_ps, v_h, v_l, s_ps, s_max, s_exp, s_rden, s_norm,
             s_turn, s_ph, s_pl, o_ps, o_sb, y_ps, y_add) = (self.sem("p_" + n) for n in names)
            kq_in = [self.sem(f"p_kq_in{i}") for i in range(2)]
            s_wo = self.sem("p_wo")
            BO, BP, BTA = 6, 7, 4
            HP = H // 2
            NEXT_AT = 28
            PROJ = 3 * HP
            KQ = 8 * 16
            TURN = 2 * STEPS
            DOUBLES = STEPS // 2
            project_at = {8 * p + 2 * i: 3 * (p + 1) + i for p in range(HP - 1) for i in range(3)}
            project_at |= {NEXT_AT + 2 * i: PROJ + i for i in range(3)}
            made_in = lambda t, last: t in project_at and not (last and project_at[t] >= PROJ)

            def batches(eng, body):
                with eng.Fori(0, B - 1) as b:
                    body(b, False)
                body(B - 1, True)

            score_at = {4: 0, 6: 1}

            with nc.Block() as block:
                @block.sync
                def _(sp):
                    sp.dma_start(Wo[:], ins["Wo1"]).then_inc(s_wo, 16)

                    def stack(b, p):
                        arrived = kq_in[p % 2]
                        sp.wait_ge(proj_l, b * PROJ + 3 * p + 3)
                        for j in range(2):
                            for part in range(2):
                                half = (part + j) % 2
                                sp.dma_start(K2[p % 2][j][half * DH:(half + 1) * DH, :].bitcast(F32),
                                             kHL[j * DH:(j + 1) * DH, part, :].bitcast(F32)).then_inc(arrived, 16)
                        sp.wait_ge(proj_l, b * PROJ + 3 * p + 4)
                        for j in range(2):
                            for half in range(2):
                                sp.dma_start(Q2[p % 2][j][half * DH:(half + 1) * DH, :, :].bitcast(F32),
                                             qHL[j * DH:(j + 1) * DH, :, :].bitcast(F32)).then_inc(arrived, 16)

                    def body(b, last):
                        for p in range(1, HP):
                            stack(b, p)
                        if not last:
                            sp.dma_start(kv[:].bitcast(F32), self.kv_dram[bass.ds(b + 1, 1)].rearrange(
                                "a p h k n -> p (a h) k n")).then_inc(s_kv, 16)
                            stack(b, HP)

                    stack(0, 0)
                    batches(sp, body)

                @block.tensor
                def _(pe):
                    def exact(out, lhs, rhs):
                        parts = [(i, j, k) for i, j in ((0, 0), (0, 1), (1, 0)) for k in range(KC)]
                        for n, (i, j, k) in enumerate(parts):
                            mm = pe.matmul(out, lhs(i, k), rhs(j, k), start=n == 0, stop=n == len(parts) - 1)
                        return mm

                    def project(b, m):
                        p, part = m // 3, m % 3
                        w, a = (WQ, S) if part == 2 else (WK, part * S)
                        if m == PROJ:
                            pe.wait_ge(s_kv, b * 16 + 80)
                        p %= HP
                        pe.wait_ge(proj_l, b * PROJ + m + 1)
                        exact(ps[:, BP, :], lambda i, k: W[:, i, w, k, p * P:(p + 1) * P],
                              lambda j, k: kv[:, j, k, a:a + S]).then_inc(proj, 1)

                    def scores(b, t):
                        h, q = t // TB, t % TB
                        p, j = h // 2, h % 2
                        if t % (2 * TB) == 0:
                            pe.wait_ge(kq_in[p % 2], b * (HP // 2 * KQ) + (p // 2 + 1) * KQ)
                        if t >= 2:
                            pe.wait_ge(s_exp, b * STEPS + t - 1)
                        for c in range(2):
                            for part in range(2):
                                mm = pe.matmul(ps[:, 2 * (t % 2) + c, :], Q2[p % 2][j][:, part, q * P:(q + 1) * P],
                                               K2[p % 2][j][:, c * 512:(c + 1) * 512], start=part == 0, stop=part == 1)
                        mm.then_inc(s_ps, 1)

                    def turn(b, t):
                        pe.wait_ge(s_norm, b * STEPS + t + 1)
                        for g in range(2):
                            pe.wait_ge(s_pl, b * TURN + 2 * t + g + 1)
                            for c in range(4):
                                mm = pe.transpose(ps[:, BTA + g, c * P:(c + 1) * P],
                                                  Pr[t % 3][:, (4 * g + c) * P:(4 * g + c + 1) * P], self.ident)
                            mm.then_inc(s_turn, 1)

                    def attend(b, d):
                        h = d // 2
                        pe.wait_ge(s_pl, b * TURN + 4 * d + 6)
                        pe.wait_ge(o_sb, b * DOUBLES + d + 1)
                        for c in range(KT):
                            for n, A in enumerate((Ph, Pl)):
                                mm = pe.matmul(ps[:, BO, 0:2 * P], V2[:, c, h, :], A[d % 2][:, c, :],
                                               start=c == 0 and n == 0, stop=c == KT - 1 and n == 1)
                        mm.then_inc(o_ps, 1)

                    def body(b, last):
                        for c in range(KT):
                            if c >= 3:
                                pe.wait_ge(v_l, b * KT + c - 2)
                            exact(ps[:, BTA + c % 3, :], lambda i, k: kv[:, i, k, c * P:(c + 1) * P],
                                  lambda j, k: W[:, j, WV, k, :]).then_inc(v_ps, 1)
                            if c in score_at:
                                if score_at[c] == 0:
                                    pe.wait_ge(y_add, b * TB + 1)
                                scores(b, score_at[c])
                        for t in range(STEPS + 4):
                            if 2 <= t < STEPS:
                                scores(b, t)
                            if made_in(t, last):
                                project(b, project_at[t])
                            if t == 2:
                                pe.wait_ge(v_l, b * KT + KT)
                            if 2 <= t < STEPS + 2:
                                turn(b, t - 2)
                            if t >= 4 and t % 2 == 0:
                                attend(b, (t - 4) // 2)
                        pe.wait_ge(o_sb, b * DOUBLES + DOUBLES + 1)
                        pe.wait_ge(s_wo, 16)
                        for q in range(TB):
                            for h in range(H):
                                mm = pe.matmul(ps[:, q, 0:D], AT[:, h, q * P:(q + 1) * P], Wo[:, h, :],
                                               start=h == 0, stop=h == H - 1)
                            mm.then_inc(y_ps, 1)

                    pe.wait_ge(s_kv, 64)
                    for m in range(3):
                        project(0, m)
                    batches(pe, body)

                @block.scalar
                def _(act):
                    def split_high(b, m):
                        act.wait_ge(proj, b * PROJ + m + 1)
                        if m % 3 == 2:
                            act.mul(qHL[:, 0, :], ps[:, BP, :], DH ** -0.5).then_inc(proj_h, 1)
                        else:
                            act.copy(kHL[:, 0, m % 3 * S:(m % 3 + 1) * S], ps[:, BP, :]).then_inc(proj_h, 1)

                    def softmax_exp(b, t):
                        act.wait_ge(s_max, b * STEPS + t + 1)
                        if t >= 3:
                            act.wait_ge(s_turn, b * TURN + 2 * (t - 2))
                        act.activation(Pr[t % 3][:], self.bank(2 * (t % 2), 2), ACT.Exp, bias=nmax[:, t:t + 1],
                                       scale=1.0, accum_out=den[:, t:t + 1]).then_inc(s_exp, 1)

                    def turned_high(b, t):
                        for g in range(2):
                            act.wait_ge(s_turn, b * TURN + 2 * t + g + 1)
                            if t >= 4 and t % 2 == 0 and g == 0:
                                act.wait_ge(o_ps, b * DOUBLES + t // 2 - 1)
                            act.copy(Ph[(t // 2) % 2][:, 4 * g:4 * g + 4, (t % 2) * P:(t % 2 + 1) * P],
                                     ps[:, BTA + g, :].rearrange("p (c q) -> p c q", q=P)).then_inc(s_ph, 1)

                    def body(b, last):
                        for c in range(KT):
                            act.wait_ge(v_ps, b * KT + c + 1)
                            act.copy(V2[:, c, :, 0:DH],
                                     ps[:, BTA + c % 3, :].rearrange("p (h d) -> p h d", d=DH)).then_inc(v_h, 1)
                            if c - 1 in score_at:
                                softmax_exp(b, score_at[c - 1])
                        for t in range(STEPS + 2):
                            if t >= 2:
                                turned_high(b, t - 2)
                            if 2 <= t < STEPS:
                                softmax_exp(b, t)
                            if made_in(t, last):
                                split_high(b, project_at[t])

                    for m in range(3):
                        split_high(0, m)
                    batches(act, body)

                @block.vector
                def _(e):
                    def split_low(b, m):
                        e.wait_ge(proj_h, b * PROJ + m + 1)
                        if m % 3 == 2:
                            e.scalar_tensor_tensor(qHL[:, 1, :], ps[:, BP, :], DH ** -0.5, qHL[:, 0, :].bitcast(F32),
                                                   ALU.mult, ALU.subtract).then_inc(proj_l, 1)
                        else:
                            half = slice(m % 3 * S, (m % 3 + 1) * S)
                            e.tensor_tensor(kHL[:, 1, half], ps[:, BP, :], kHL[:, 0, half].bitcast(F32),
                                            ALU.subtract).then_inc(proj_l, 1)

                    def row_max(b, t):
                        e.wait_ge(s_ps, b * STEPS + t + 1)
                        e.tensor_reduce(nmax[:, t:t + 1], self.bank(2 * (t % 2), 2), AX, ALU.max,
                                        negate=True).then_inc(s_max, 1)

                    def inverse(b, t):
                        e.wait_ge(s_exp, b * STEPS + t + 1)
                        e.reciprocal(rden[:, t:t + 1], den[:, t:t + 1]).then_inc(s_rden, 1)

                    def turned_low(b, t):
                        for g in range(2):
                            e.wait_ge(s_ph, b * TURN + 2 * t + g + 1)
                            if t >= 4 and t % 2 == 0 and g == 0:
                                e.wait_ge(o_ps, b * DOUBLES + t // 2 - 1)
                            dst = (slice(None), slice(4 * g, 4 * g + 4), slice((t % 2) * P, (t % 2 + 1) * P))
                            e.tensor_tensor(Pl[(t // 2) % 2][dst], ps[:, BTA + g, :].rearrange("p (c q) -> p c q", q=P),
                                            Ph[(t // 2) % 2][dst].bitcast(F32), ALU.subtract).then_inc(s_pl, 1)

                    def copy_o(b, d):
                        h, q = d // 2, d % 2
                        e.wait_ge(o_ps, b * DOUBLES + d + 1)
                        e.tensor_copy(AT[:, h, q * 2 * P:(q + 1) * 2 * P], ps[:, BO, 0:2 * P]).then_inc(o_sb, 1)

                    e.sem_inc(proj_l, 1)
                    e.sem_inc(s_pl, 2)
                    e.sem_inc(o_sb, 1)
                    e.sem_inc(y_add, 1)

                    def body(b, last):
                        for c in range(KT):
                            e.wait_ge(v_h, b * KT + c + 1)
                            e.tensor_tensor(V2[:, c, :, DH:P], ps[:, BTA + c % 3, :].rearrange("p (h d) -> p h d", d=DH),
                                            V2[:, c, :, 0:DH].bitcast(F32), ALU.subtract).then_inc(v_l, 1)
                            if c in score_at:
                                row_max(b, score_at[c])
                        inverse(b, 0)
                        for t in range(STEPS + 4):
                            if 2 <= t < STEPS + 1:
                                inverse(b, t - 1)
                            if 2 <= t < STEPS:
                                row_max(b, t)
                            if 2 <= t < STEPS + 2:
                                turned_low(b, t - 2)
                            if made_in(t, last):
                                split_low(b, project_at[t])
                            if t >= 5 and t % 2 == 1:
                                copy_o(b, (t - 5) // 2)
                        if last:
                            e.wait_ge(y_add, (B - 1) * TB + 1)
                            self.ln_tiles(e, X, range(T - TB))
                        for q in range(TB):
                            e.wait_ge(y_ps, b * TB + q + 1)
                            x = (X[:, b * TB + q, :] if last else
                                 X[:, bass.ds(b * TB + q, 1), :].rearrange("p a d -> p (a d)"))
                            e.scalar_tensor_tensor(x, ps[:, q, 0:D], self.tg[:, 1:2], x, ALU.mult, ALU.add).then_inc(y_add, 1)
                        if last:
                            e.wait_ge(y_add, B * TB + 1)
                            self.ln_tiles(e, X, range(T - TB, T))

                    for m in range(3):
                        split_low(0, m)
                    batches(e, body)

                @block.gpsimd
                def _(pool):
                    with pool.Fori(0, B) as b:
                        for t in range(STEPS):
                            pool.wait_ge(s_rden, b * STEPS + t + 1)
                            pool.tensor_tensor(Pr[t % 3][:], Pr[t % 3][:], rden[:, t:t + 1].broadcast_to([P, KEYS]),
                                               ALU.mult).then_inc(s_norm, 1)


def build(nc, ins, out, stop=99):
    with ExitStack() as ctx:
        p = Program(nc, ins, out, ctx)
        def layer_0():
            with ExitStack() as inner:
                p.W_down = inner.enter_context(nc.sbuf_tensor("W_down", [P, 2 * E, F0 // 2 // P * D], F32))
                p.s_ahead = p.sem("ahead")
                with nc.sbuf_tensor("C", [P, T, D], F32) as p.C:
                    p.retention()
                    p.route(0, 1, SLOTS0)
                p.experts(0, SLOTS0, F0 // 2)

        def layer_1_ffn():
            with ExitStack() as inner:
                half_w = F1_PAD // 2
                p.W_all = inner.enter_context(nc.sbuf_tensor(
                    "W_all", [P, 2 * E, 2 * KC * half_w + len(chunks(half_w)) * D], F32))
                p.w1_in = p.sem("w1_in")
                p.route(1, 2, SLOTS1)
                p.experts(1, SLOTS1, half_w)

        def attention():
            with ExitStack() as inner:
                p.W_att = inner.enter_context(nc.sbuf_tensor("W_att", [P, 2, 3, KC, INNER], F32R))
                p.kv_in = inner.enter_context(nc.sbuf_tensor("kv_in", [P, 2, KC, KEYS], F32R))
                p.s_kv = p.sem("s_kv")
                p.latents()
                p.perceiver()

        stages = [layer_0, attention, layer_1_ffn, p.finish]
        for stage in stages[:stop]:
            stage()
        if stop < len(stages):
            s = p.sem("dbg")
            with nc.Block() as block:
                @block.sync
                def _(sp):
                    sp.dma_start(out.rearrange("(t p) d -> p t d", p=P), p.X[:]).then_inc(s, 16)
                    sp.wait_ge(s, 16)


def laid_out(inputs):
    a = {k: np.asarray(v) for k, v in inputs.items()}
    split = np.concatenate([np.arange(0, D, 2), np.arange(1, D, 2)])

    def packed(up, down, f):
        hw = f // 2
        nck = len(chunks(hw))
        u = up.reshape(E, KC, P, 2, 2, hw).transpose(0, 4, 2, 3, 1, 5).reshape(E, 2, P, 2 * KC * hw)
        d = down.reshape(E, 2, hw, D)
        d = np.concatenate([d, np.zeros((E, 2, nck * P - hw, D), d.dtype)], 2)
        d = d.reshape(E, 2, nck, P, D).transpose(0, 1, 3, 2, 4).reshape(E, 2, P, nck * D)
        return np.concatenate([u, d], 3).reshape(2 * E, P, -1)

    w1 = a["L0_ffn_w1"].reshape(E, D, 2, F0)
    up1 = np.stack([a["L1_ffn_W1"].transpose(0, 2, 1), a["L1_ffn_W2"].transpose(0, 2, 1)], 2)
    pad = F1_PAD - F1
    up1 = np.pad(up1, ((0, 0), (0, 0), (0, 0), (0, pad)))
    down1 = np.pad(a["L1_ffn_W3"].transpose(0, 2, 1), ((0, 0), (0, pad), (0, 0)))
    ln = [a[f"L1_xattn_ln_{n}"].reshape(KC, P).T for n in ("media_w", "media_b", "lat_w", "lat_b")]
    out = {
        "x": a["x"].reshape(B * S, D),
        "ctx": a["ctx_1024"].reshape(B * S, D),
        "ctxT": a["ctx_1024"].reshape(B * S, D).T,
        "g_xattn": a["g_xattn"], "g_ffn": a["g_ffn"],
        "const": shape_constants(), "tab": xpos_tables(),
        "lnw": np.stack(ln, 1),
        "Wq0": a["L0_xattn_Wq"][split].T, "Wk0": a["L0_xattn_Wk"][split].T, "Wv0": a["L0_xattn_Wv"].T,
        "rw0": a["L0_ffn_router_w"], "rb0": a["L0_ffn_router_b"],
        "We0": packed(w1, a["L0_ffn_w2"], F0),
        "Wvkq1": np.stack([a[f"L1_xattn_W{n}"].reshape(KC, P, INNER) for n in "vkq"]).transpose(2, 0, 1, 3),
        "Wo1": np.repeat(a["L1_xattn_Wout"].reshape(H, 1, DH, D), 2, axis=1).reshape(H, P, D).transpose(1, 0, 2),
        "rw1": a["L1_ffn_Wg"].T,
        "We1": packed(up1, down1, F1_PAD),
    }
    return {k: np.ascontiguousarray(v) for k, v in out.items()}


def kernel(**inputs):
    import concourse.bacc as bacc
    from concourse.bass_utils import run_bass_kernel_spmd

    nc = bacc.Bacc("TRN2", target_bir_lowering=False, num_devices=1)
    arrays, ins = {}, {}
    for name, a in laid_out(inputs).items():
        arrays[f"in_{name}"] = a
        ins[name] = nc.dram_tensor(f"in_{name}", a.shape, mybir.dt.from_np(a.dtype), kind="ExternalInput").ap()
    out = nc.dram_tensor("out", (B * S, D), F32, kind="ExternalOutput").ap()
    build(nc, ins, out)
    r = run_bass_kernel_spmd(nc, [arrays], core_ids=[0])
    return r.results[0]["out"].reshape(B, S, D)
```
